# Optimizing a Trainium2 kernel written in Bass

```python
import numpy as np
import jax
import jax.numpy as jnp

def _softmax(x, axis=-1):
    return jax.nn.softmax(x, axis=axis)

def _gelu(x):
    return jax.nn.gelu(x, approximate=True)

def _silu(x):
    return jax.nn.silu(x)

def _sigmoid(x):
    return jax.nn.sigmoid(x)

def _layernorm(x, axis=-1, eps=1e-05):
    m = jnp.mean(x, axis=axis, keepdims=True)
    v = jnp.var(x, axis=axis, keepdims=True)
    return (x - m) / jnp.sqrt(v + eps)

def _scatter_add(tgt, idx, src, axis=0):
    return tgt.at[idx].add(src)

def _segment_sum(src, seg, n):
    return jax.ops.segment_sum(src, seg, n)
kernel_name = 'mk_decoder_preln_d4_seqx_r4_e8c41b'

def setup_inputs(seed: int=0):
    np.random.seed(seed)
    _w = jnp.asarray

    def _rec_inputs():
        import jax
        import jax.numpy as jnp
        _rk = jax.random.key(seed)
        x = 0.002226 + 0.9996 * jax.random.normal(jax.random.fold_in(_rk, 1), (2, 1024, 256), jnp.float32)
        _lenS = 1024 - jax.random.randint(jax.random.fold_in(_rk, 7), (2,), 0, max(1, 1024 // 4) + 1, jnp.int32)
        _lenS2 = 77 - jax.random.randint(jax.random.fold_in(_rk, 8), (2,), 0, max(1, 77 // 4) + 1, jnp.int32)
        _ctx_1024P = jax.random.normal(jax.random.fold_in(_rk, 11), (2, 16, 256), jnp.float32)
        _ctx_1024c = jax.random.dirichlet(jax.random.fold_in(_rk, 511), 0.3 * jnp.ones((16,), jnp.float32), (2, 77))
        _ctx_1024t = jnp.einsum('bsk,bkd->bsd', _ctx_1024c, _ctx_1024P)
        _ctx_1024t = _ctx_1024t * jax.lax.rsqrt(jnp.mean(jnp.square(_ctx_1024t)) + 1e-12) * 0.953939
        ctx_1024 = -0.000125008 + 0.999885 * (_ctx_1024t + 0.3 * jax.random.normal(jax.random.fold_in(_rk, 611), (2, 77, 256), jnp.float32))
        _validS = jnp.arange(1024)[None, :] < _lenS[:, None]
        _validS2 = jnp.arange(77)[None, :] < _lenS2[:, None]
        _causal = jnp.tril(jnp.ones((1024, 1024), dtype=bool))
        mask_BxS2_bk0 = jnp.logical_not(jnp.broadcast_to(_validS2[:, :], (2, 77)))
        mask_Bx1xSxS2_if1 = jnp.where(jnp.ones((2, 1, 1024, 77), dtype=bool), 1, 0).astype(jnp.int32)
        return (x, ctx_1024, mask_BxS2_bk0, mask_Bx1xSxS2_if1)
    x, ctx_1024, mask_BxS2_bk0, mask_Bx1xSxS2_if1 = _rec_inputs()

    def _L0_attn_setup():
        import jax, jax.numpy as jnp
        import numpy as np
        EPS = 1e-08

        def _combine(c1, c2):
            a1, b1 = c1
            a2, b2 = c2
            return (a1 * a2, a2 * b1 + b2)
        key = jax.random.key(seed)
        ks = jax.random.split(key, 5)
        B, S, D = (4, 512, 256)
        H = 2 * D
        x = jax.random.normal(ks[0], (B, S, D), dtype=jnp.float32)
        rms_scale = jnp.ones((D,), dtype=jnp.float32)
        split_scale = jax.random.uniform(ks[1], (D,), dtype=jnp.float32)
        W_K = jax.random.normal(ks[2], (D, H), dtype=jnp.float32) * D ** (-0.5)
        W_ugg = jax.random.normal(ks[3], (D, 3 * H), dtype=jnp.float32) * D ** (-0.5)
        W_out = jax.random.normal(ks[4], (H, D), dtype=jnp.float32) * H ** (-0.5)
        return {'x': x, 'rms_scale': rms_scale, 'split_scale': split_scale, 'W_K': W_K, 'W_ugg': W_ugg, 'W_out': W_out}
    _L0_attn_all = _L0_attn_setup()
    _L0_attn_in = {k: v for k, v in _L0_attn_all.items() if k in ('rms_scale', 'split_scale', 'W_K', 'W_ugg', 'W_out')}
    del _L0_attn_all

    def _L0_xattn_setup():
        import jax, jax.numpy as jnp
        import numpy as np
        EPS = 1e-05

        def layer_norm(x, g, b):
            mu = jnp.mean(x, axis=-1, keepdims=True)
            var = jnp.mean((x - mu) ** 2, axis=-1, keepdims=True)
            return (x - mu) * jax.lax.rsqrt(var + EPS) * g + b
        key = jax.random.key(seed)
        ks = jax.random.split(key, 8)
        b, n, l, D = (8, 1024, 64, 256)
        heads, dim_head = (16, 64)
        inner = heads * dim_head
        x = jax.random.normal(ks[0], (b, n, D), dtype=jnp.float32)
        latents = jax.random.normal(ks[1], (b, l, D), dtype=jnp.float32)
        mask = jax.random.randint(ks[2], (b, n), 0, 2) > 0
        Wq = jax.random.normal(ks[3], (D, inner), dtype=jnp.float32) * D ** (-0.5)
        Wkv = jax.random.normal(ks[4], (D, 2 * inner), dtype=jnp.float32) * D ** (-0.5)
        Wout = jax.random.normal(ks[5], (inner, D), dtype=jnp.float32) * inner ** (-0.5)
        g1 = jnp.ones((D,), jnp.float32)
        b1 = jnp.zeros((D,), jnp.float32)
        g2 = jnp.ones((D,), jnp.float32)
        b2 = jnp.zeros((D,), jnp.float32)
        return {'x': x, 'latents': latents, 'mask': mask, 'g1': g1, 'b1': b1, 'g2': g2, 'b2': b2, 'Wq': Wq, 'Wkv': Wkv, 'Wout': Wout}
    _L0_xattn_all = _L0_xattn_setup()
    _L0_xattn_in = {k: v for k, v in _L0_xattn_all.items() if k in ('g1', 'b1', 'g2', 'b2', 'Wq', 'Wkv', 'Wout')}
    del _L0_xattn_all

    def _L0_ffn_setup():
        import jax, jax.numpy as jnp
        import numpy as np
        D_IN, D_HID = (256, 1024)

        def _ternary(key, shape):
            return jax.random.randint(key, shape, -1, 2).astype(jnp.float32)

        def _tlin(x, w, s):
            return jnp.einsum('bsi,oi->bso', x, w) * s
        key = jax.random.key(seed)
        ks = jax.random.split(key, 12)
        inv = lambda fan: 1.0 / np.sqrt(fan).astype(np.float32)
        return {'x': jax.random.normal(ks[0], (4, 512, D_IN), dtype=jnp.float32), 'w1_w': _ternary(ks[1], (D_HID, D_IN)), 'w1_s': jax.random.uniform(ks[2], (D_HID,), dtype=jnp.float32) * inv(D_IN), 'w2_w': _ternary(ks[3], (D_HID, D_IN)), 'w2_s': jax.random.uniform(ks[4], (D_HID,), dtype=jnp.float32) * inv(D_IN), 'h1_w': _ternary(ks[5], (D_HID, D_HID)), 'h1_s': jax.random.uniform(ks[6], (D_HID,), dtype=jnp.float32) * inv(D_HID), 'h2_w': _ternary(ks[7], (D_HID, D_HID)), 'h2_s': jax.random.uniform(ks[8], (D_HID,), dtype=jnp.float32) * inv(D_HID), 'w3_w': _ternary(ks[9], (D_IN, D_HID)), 'w3_s': jax.random.uniform(ks[10], (D_IN,), dtype=jnp.float32) * inv(D_HID)}
    _L0_ffn_all = _L0_ffn_setup()
    _L0_ffn_in = {k: v for k, v in _L0_ffn_all.items() if k in ('w1_w', 'w1_s', 'w2_w', 'w2_s', 'h1_w', 'h1_s', 'h2_w', 'h2_s', 'w3_w', 'w3_s')}
    del _L0_ffn_all

    def _L1_attn_setup():
        import jax, jax.numpy as jnp
        import numpy as np
        from functools import partial
        CHUNK = 32

        def _phi(x):
            return jax.nn.elu(x) + 1.0

        def _decay_scan(x, log_d, init):
            B, H, T, D = x.shape
            C = min(CHUNK, T)
            assert T % C == 0
            Nc = T // C
            c_idx = jnp.arange(C, dtype=x.dtype)
            lp = log_d[None, :, None, None] * c_idx[None, None, :, None]
            p = jnp.exp(lp)
            inv_p = jnp.exp(-lp)
            init_p = jnp.exp(log_d[None, :, None, None] * (c_idx + 1.0)[None, None, :, None])
            xc = x.reshape(B, H, Nc, C, D).transpose(2, 0, 1, 3, 4)

            def step(state, chunk):
                cs = jnp.cumsum(chunk * inv_p, axis=2)
                out = cs * p + state[:, :, None, :] * init_p
                return (out[:, :, -1, :], out)
            last, outs = jax.lax.scan(step, init, xc)
            out = outs.transpose(1, 2, 0, 3, 4).reshape(B, H, T, D)
            return (out, last)

        def _reference_tuple_inner(x, w_qkv, w_out, alpha, beta):
            B, T, HID = x.shape
            H = alpha.shape[0]
            D = HID // H
            qkv = x @ w_qkv
            q, k, v = jnp.split(qkv, 3, axis=-1)
            to_bhtd = lambda t: t.reshape(B, T, H, D).transpose(0, 2, 1, 3)
            q = _phi(to_bhtd(q))
            k = _phi(to_bhtd(k))
            v = to_bhtd(v)
            kv = k * v
            log_a = jnp.log(jnp.clip(jax.nn.sigmoid(alpha), 1e-08, None))
            log_b = jnp.log(jnp.clip(jax.nn.sigmoid(beta), 1e-08, None))
            z = jnp.zeros((B, H, D), dtype=x.dtype)
            run_kv_f, kv_f1 = _decay_scan(kv, log_a, z)
            run_ks_f, ks_f1 = _decay_scan(k, log_a, z)
            run_kv_s, kv_s1 = _decay_scan(kv, log_b, z)
            run_ks_s, ks_s1 = _decay_scan(k, log_b, z)
            eps = 1e-06
            den_f = jnp.clip(jnp.sum(q * run_ks_f, axis=-1, keepdims=True), eps, None)
            den_s = jnp.clip(jnp.sum(q * run_ks_s, axis=-1, keepdims=True), eps, None)
            out_f = (q * run_kv_f / den_f).transpose(0, 2, 1, 3).reshape(B, T, HID)
            out_s = (q * run_kv_s / den_s).transpose(0, 2, 1, 3).reshape(B, T, HID)
            out = jnp.concatenate([out_f, out_s], axis=-1) @ w_out
            return (out, (kv_f1, ks_f1, kv_s1, ks_s1))
        key = jax.random.key(seed)
        k1, k2, k3, k4, k5 = jax.random.split(key, 5)
        B, T, HID, H = (4, 1024, 256, 16)
        logit = lambda p: float(np.log(p / (1.0 - p)))
        return {'x': jax.random.normal(k1, (B, T, HID), dtype=jnp.float32), 'w_qkv': jax.random.normal(k2, (HID, 3 * HID), dtype=jnp.float32) * 0.02, 'w_out': jax.random.normal(k3, (2 * HID, HID), dtype=jnp.float32) * 0.02, 'alpha': jnp.full((H,), logit(0.7), dtype=jnp.float32) + 0.01 * jax.random.normal(k4, (H,), dtype=jnp.float32), 'beta': jnp.full((H,), logit(0.97), dtype=jnp.float32) + 0.01 * jax.random.normal(k5, (H,), dtype=jnp.float32)}
    _L1_attn_all = _L1_attn_setup()
    _L1_attn_in = {k: v for k, v in _L1_attn_all.items() if k in ('w_qkv', 'w_out', 'alpha', 'beta')}
    del _L1_attn_all

    def _L1_xattn_setup():
        import jax, jax.numpy as jnp
        import numpy as np
        EMBED = 256
        HEADS = 16
        HEAD_DIM = EMBED // HEADS
        EXP_DIM = 2 * HEAD_DIM

        def _feature_map(x, fm_w, fm_b):
            z = jnp.einsum('nshd,ed->nshe', x, fm_w) + fm_b
            return jnp.concatenate([jnp.exp(z), jnp.exp(-z)], axis=-1)
        key = jax.random.key(seed)
        ks = jax.random.split(key, 7)
        N, S = (4, 512)
        values = jax.random.normal(ks[0], (N, S, EMBED), dtype=jnp.float32)
        keys_ = jax.random.normal(ks[1], (N, S, EMBED), dtype=jnp.float32)
        query = jax.random.normal(ks[2], (N, S, EMBED), dtype=jnp.float32)
        fm_w = jnp.eye(HEAD_DIM, dtype=jnp.float32) + 0.02 * jax.random.normal(ks[3], (HEAD_DIM, HEAD_DIM), dtype=jnp.float32)
        fm_b = 0.02 * jax.random.normal(ks[4], (HEAD_DIM,), dtype=jnp.float32)
        fc_w = jax.random.normal(ks[5], (EMBED, HEADS * EXP_DIM), dtype=jnp.float32) * (1.0 / np.sqrt(HEADS * EXP_DIM))
        fc_b = jnp.zeros((EMBED,), dtype=jnp.float32)
        return {'values': values, 'keys': keys_, 'query': query, 'fm_w': fm_w, 'fm_b': fm_b, 'fc_w': fc_w, 'fc_b': fc_b}
    _L1_xattn_all = _L1_xattn_setup()
    _L1_xattn_in = {k: v for k, v in _L1_xattn_all.items() if k in ('fm_w', 'fm_b', 'fc_w', 'fc_b')}
    del _L1_xattn_all

    def _L1_ffn_setup():
        import jax, jax.numpy as jnp
        import numpy as np
        E = 8
        K = 2
        D = 256
        H = 4 * D
        EPS = 1e-05
        TEMP = 1.5
        key = jax.random.key(seed)
        ks = jax.random.split(key, 6)
        B, T = (2, 512)
        x = jax.random.normal(ks[0], (B, T, D), dtype=jnp.float32)
        gamma = jnp.ones((D,), dtype=jnp.float32)
        beta = jnp.zeros((D,), dtype=jnp.float32)
        router_w = jax.random.normal(ks[1], (E, D), dtype=jnp.float32) * 0.02
        W1 = jax.random.normal(ks[2], (E, D, H), dtype=jnp.float32) * 0.02
        W2 = jax.random.normal(ks[3], (E, H, D), dtype=jnp.float32) * 0.02
        return {'x': x, 'gamma': gamma, 'beta': beta, 'router_w': router_w, 'W1': W1, 'W2': W2}
    _L1_ffn_all = _L1_ffn_setup()
    _L1_ffn_in = {k: v for k, v in _L1_ffn_all.items() if k in ('gamma', 'beta', 'router_w', 'W1', 'W2')}
    del _L1_ffn_all

    def _L2_attn_setup():
        import jax, jax.numpy as jnp
        import numpy as np
        NUM_HEADS = 16
        LN_EPS = 1e-05
        FEAT_EPS = 0.0001
        key = jax.random.key(seed)
        ks = jax.random.split(key, 4)
        B, L, D = (2, 512, 256)
        scale = 0.02
        return {'x': jax.random.normal(ks[0], (B, L, D), dtype=jnp.float32), 'Wqkv': jax.random.normal(ks[1], (3 * D, D), dtype=jnp.float32) * scale, 'bqkv': jnp.zeros((3 * D,), dtype=jnp.float32), 'Wout': jax.random.normal(ks[2], (D, D), dtype=jnp.float32) * scale, 'bout': jnp.zeros((D,), dtype=jnp.float32), 'gamma': jnp.ones((D,), dtype=jnp.float32), 'beta': jnp.zeros((D,), dtype=jnp.float32)}
    _L2_attn_all = _L2_attn_setup()
    _L2_attn_in = {k: v for k, v in _L2_attn_all.items() if k in ('Wqkv', 'bqkv', 'Wout', 'bout', 'gamma', 'beta')}
    del _L2_attn_all

    def _L2_xattn_setup():
        import jax, jax.numpy as jnp
        import numpy as np
        HEADS = 16
        key = jax.random.key(seed)
        ks = jax.random.split(key, 8)
        N, S, E = (2, 512, 256)
        D = E // HEADS
        return {'values': jax.random.normal(ks[0], (N, S, E), jnp.float32), 'keys': jax.random.normal(ks[1], (N, S, E), jnp.float32), 'queries': jax.random.normal(ks[2], (N, S, E), jnp.float32), 'mask': jnp.ones((N, 1, S, S), jnp.int32), 'Wv': jax.random.normal(ks[3], (D, D), jnp.float32) * D ** (-0.5), 'Wk': jax.random.normal(ks[4], (D, D), jnp.float32) * D ** (-0.5), 'Wq': jax.random.normal(ks[5], (D, D), jnp.float32) * D ** (-0.5), 'Wo': jax.random.normal(ks[6], (E, E), jnp.float32) * E ** (-0.5), 'bo': jnp.zeros((E,), jnp.float32)}
    _L2_xattn_all = _L2_xattn_setup()
    _L2_xattn_in = {k: v for k, v in _L2_xattn_all.items() if k in ('Wv', 'Wk', 'Wq', 'Wo', 'bo')}
    del _L2_xattn_all

    def _L2_ffn_setup():
        import jax, jax.numpy as jnp
        import numpy as np
        key = jax.random.key(seed)
        ks = jax.random.split(key, 5)
        B, S, D_in, D_out, E, R = (4, 256, 256, 256, 8, 16)
        x = jax.random.normal(ks[0], (B, S, D_in), dtype=jnp.float32)
        weight = jax.random.normal(ks[1], (D_out, D_in), dtype=jnp.float32) / np.sqrt(D_in)
        gate_w = jax.random.normal(ks[2], (E, D_in), dtype=jnp.float32) / np.sqrt(D_in)
        lora_U = jax.random.normal(ks[3], (E, R, D_in), dtype=jnp.float32) / np.sqrt(D_in)
        lora_V = jax.random.normal(ks[4], (E, D_out, R), dtype=jnp.float32) / np.sqrt(R)
        return {'x': x, 'weight': weight, 'gate_w': gate_w, 'lora_U': lora_U, 'lora_V': lora_V}
    _L2_ffn_all = _L2_ffn_setup()
    _L2_ffn_in = {k: v for k, v in _L2_ffn_all.items() if k in ('weight', 'gate_w', 'lora_U', 'lora_V')}
    del _L2_ffn_all

    def _L3_attn_setup():
        import jax, jax.numpy as jnp
        import numpy as np
        B, T, D = (2, 512, 256)
        H = 16
        HD = D // H
        DL = 128
        NR = 64
        EPS = 1.1920929e-07

        def _rms_norm(x, w):
            ms = jnp.mean(jnp.square(x), axis=-1, keepdims=True)
            return x * jax.lax.rsqrt(ms + EPS) * w
        key = jax.random.key(seed)
        ks = jax.random.split(key, 10)
        s = 0.02
        return {'x': jax.random.normal(ks[0], (B, T, D), dtype=jnp.float32), 'W_DQ': jax.random.normal(ks[1], (DL, HD), dtype=jnp.float32) * s, 'W_UQ': jax.random.normal(ks[2], (HD, DL), dtype=jnp.float32) * s, 'W_DKV': jax.random.normal(ks[3], (2 * DL, HD), dtype=jnp.float32) * s, 'W_UKV': jax.random.normal(ks[4], (2 * HD, 2 * DL), dtype=jnp.float32) * s, 'W_QR': jax.random.normal(ks[5], (NR, HD), dtype=jnp.float32) * s, 'W_KR': jax.random.normal(ks[6], (NR, HD), dtype=jnp.float32) * s, 'W_O': jax.random.normal(ks[7], (HD, HD), dtype=jnp.float32) * s, 'q_norm_w': jnp.ones((HD,), dtype=jnp.float32), 'k_norm_w': jnp.ones((HD,), dtype=jnp.float32)}
    _L3_attn_all = _L3_attn_setup()
    _L3_attn_in = {k: v for k, v in _L3_attn_all.items() if k in ('W_DQ', 'W_UQ', 'W_DKV', 'W_UKV', 'W_QR', 'W_KR', 'W_O', 'q_norm_w', 'k_norm_w')}
    del _L3_attn_all

    def _L3_xattn_setup():
        import jax, jax.numpy as jnp
        import numpy as np
        D_MODEL = 256
        NUM_HEADS = 16
        D_K = D_MODEL // NUM_HEADS
        B, S = (4, 512)
        key = jax.random.key(seed)
        ks = jax.random.split(key, 11)
        scale = 1.0 / np.sqrt(D_MODEL)
        inp = {'query': jax.random.normal(ks[0], (B, S, D_MODEL), dtype=jnp.float32), 'key': jax.random.normal(ks[1], (B, S, D_MODEL), dtype=jnp.float32), 'value': jax.random.normal(ks[2], (B, S, D_MODEL), dtype=jnp.float32), 'Wq': jax.random.normal(ks[3], (D_MODEL, D_MODEL), dtype=jnp.float32) * scale, 'bq': jnp.zeros((D_MODEL,), dtype=jnp.float32), 'Wk': jax.random.normal(ks[4], (D_MODEL, D_MODEL), dtype=jnp.float32) * scale, 'bk': jnp.zeros((D_MODEL,), dtype=jnp.float32), 'Wv': jax.random.normal(ks[5], (D_MODEL, D_MODEL), dtype=jnp.float32) * scale, 'bv': jnp.zeros((D_MODEL,), dtype=jnp.float32), 'Wo': jax.random.normal(ks[6], (D_MODEL, D_MODEL), dtype=jnp.float32) * scale, 'bo': jnp.zeros((D_MODEL,), dtype=jnp.float32)}
        return inp
    _L3_xattn_all = _L3_xattn_setup()
    _L3_xattn_in = {k: v for k, v in _L3_xattn_all.items() if k in ('Wq', 'bq', 'Wk', 'bk', 'Wv', 'bv', 'Wo', 'bo')}
    del _L3_xattn_all

    def _L3_ffn_setup():
        import jax, jax.numpy as jnp
        import numpy as np
        key = jax.random.key(seed)
        kx, kw = jax.random.split(key)
        x = jax.random.normal(kx, (32, 1024, 256), dtype=jnp.float32)
        weight = jax.random.normal(kw, (256, 256), dtype=jnp.float32) * 0.01
        return {'x': x, 'weight': weight}
    _L3_ffn_all = _L3_ffn_setup()
    _L3_ffn_in = {k: v for k, v in _L3_ffn_all.items() if k in ('weight',)}
    del _L3_ffn_all
    return {'x': x, 'ctx_1024': ctx_1024, 'mask_BxS2_bk0': mask_BxS2_bk0, 'mask_Bx1xSxS2_if1': mask_Bx1xSxS2_if1, 'L0_attn_rms_scale': _L0_attn_in['rms_scale'], 'L0_attn_split_scale': _L0_attn_in['split_scale'], 'L0_attn_W_K': _L0_attn_in['W_K'], 'L0_attn_W_ugg': _L0_attn_in['W_ugg'], 'L0_attn_W_out': _L0_attn_in['W_out'], 'L0_xattn_g1': _L0_xattn_in['g1'], 'L0_xattn_b1': _L0_xattn_in['b1'], 'L0_xattn_g2': _L0_xattn_in['g2'], 'L0_xattn_b2': _L0_xattn_in['b2'], 'L0_xattn_Wq': _L0_xattn_in['Wq'], 'L0_xattn_Wkv': _L0_xattn_in['Wkv'], 'L0_xattn_Wout': _L0_xattn_in['Wout'], 'L0_ffn_w1_w': _L0_ffn_in['w1_w'], 'L0_ffn_w1_s': _L0_ffn_in['w1_s'], 'L0_ffn_w2_w': _L0_ffn_in['w2_w'], 'L0_ffn_w2_s': _L0_ffn_in['w2_s'], 'L0_ffn_h1_w': _L0_ffn_in['h1_w'], 'L0_ffn_h1_s': _L0_ffn_in['h1_s'], 'L0_ffn_h2_w': _L0_ffn_in['h2_w'], 'L0_ffn_h2_s': _L0_ffn_in['h2_s'], 'L0_ffn_w3_w': _L0_ffn_in['w3_w'], 'L0_ffn_w3_s': _L0_ffn_in['w3_s'], 'L1_attn_w_qkv': _L1_attn_in['w_qkv'], 'L1_attn_w_out': _L1_attn_in['w_out'], 'L1_attn_alpha': _L1_attn_in['alpha'], 'L1_attn_beta': _L1_attn_in['beta'], 'L1_xattn_fm_w': _L1_xattn_in['fm_w'], 'L1_xattn_fm_b': _L1_xattn_in['fm_b'], 'L1_xattn_fc_w': _L1_xattn_in['fc_w'], 'L1_xattn_fc_b': _L1_xattn_in['fc_b'], 'L1_ffn_gamma': _L1_ffn_in['gamma'], 'L1_ffn_beta': _L1_ffn_in['beta'], 'L1_ffn_router_w': _L1_ffn_in['router_w'], 'L1_ffn_W1': _L1_ffn_in['W1'], 'L1_ffn_W2': _L1_ffn_in['W2'], 'L2_attn_Wqkv': _L2_attn_in['Wqkv'], 'L2_attn_bqkv': _L2_attn_in['bqkv'], 'L2_attn_Wout': _L2_attn_in['Wout'], 'L2_attn_bout': _L2_attn_in['bout'], 'L2_attn_gamma': _L2_attn_in['gamma'], 'L2_attn_beta': _L2_attn_in['beta'], 'L2_xattn_Wv': _L2_xattn_in['Wv'], 'L2_xattn_Wk': _L2_xattn_in['Wk'], 'L2_xattn_Wq': _L2_xattn_in['Wq'], 'L2_xattn_Wo': _L2_xattn_in['Wo'], 'L2_xattn_bo': _L2_xattn_in['bo'], 'L2_ffn_weight': _L2_ffn_in['weight'], 'L2_ffn_gate_w': _L2_ffn_in['gate_w'], 'L2_ffn_lora_U': _L2_ffn_in['lora_U'], 'L2_ffn_lora_V': _L2_ffn_in['lora_V'], 'L3_attn_W_DQ': _L3_attn_in['W_DQ'], 'L3_attn_W_UQ': _L3_attn_in['W_UQ'], 'L3_attn_W_DKV': _L3_attn_in['W_DKV'], 'L3_attn_W_UKV': _L3_attn_in['W_UKV'], 'L3_attn_W_QR': _L3_attn_in['W_QR'], 'L3_attn_W_KR': _L3_attn_in['W_KR'], 'L3_attn_W_O': _L3_attn_in['W_O'], 'L3_attn_q_norm_w': _L3_attn_in['q_norm_w'], 'L3_attn_k_norm_w': _L3_attn_in['k_norm_w'], 'L3_xattn_Wq': _L3_xattn_in['Wq'], 'L3_xattn_bq': _L3_xattn_in['bq'], 'L3_xattn_Wk': _L3_xattn_in['Wk'], 'L3_xattn_bk': _L3_xattn_in['bk'], 'L3_xattn_Wv': _L3_xattn_in['Wv'], 'L3_xattn_bv': _L3_xattn_in['bv'], 'L3_xattn_Wo': _L3_xattn_in['Wo'], 'L3_xattn_bo': _L3_xattn_in['bo'], 'L3_ffn_weight': _L3_ffn_in['weight']}

def reference(x, ctx_1024, mask_BxS2_bk0, mask_Bx1xSxS2_if1, L0_attn_rms_scale, L0_attn_split_scale, L0_attn_W_K, L0_attn_W_ugg, L0_attn_W_out, L0_xattn_g1, L0_xattn_b1, L0_xattn_g2, L0_xattn_b2, L0_xattn_Wq, L0_xattn_Wkv, L0_xattn_Wout, L0_ffn_w1_w, L0_ffn_w1_s, L0_ffn_w2_w, L0_ffn_w2_s, L0_ffn_h1_w, L0_ffn_h1_s, L0_ffn_h2_w, L0_ffn_h2_s, L0_ffn_w3_w, L0_ffn_w3_s, L1_attn_w_qkv, L1_attn_w_out, L1_attn_alpha, L1_attn_beta, L1_xattn_fm_w, L1_xattn_fm_b, L1_xattn_fc_w, L1_xattn_fc_b, L1_ffn_gamma, L1_ffn_beta, L1_ffn_router_w, L1_ffn_W1, L1_ffn_W2, L2_attn_Wqkv, L2_attn_bqkv, L2_attn_Wout, L2_attn_bout, L2_attn_gamma, L2_attn_beta, L2_xattn_Wv, L2_xattn_Wk, L2_xattn_Wq, L2_xattn_Wo, L2_xattn_bo, L2_ffn_weight, L2_ffn_gate_w, L2_ffn_lora_U, L2_ffn_lora_V, L3_attn_W_DQ, L3_attn_W_UQ, L3_attn_W_DKV, L3_attn_W_UKV, L3_attn_W_QR, L3_attn_W_KR, L3_attn_W_O, L3_attn_q_norm_w, L3_attn_k_norm_w, L3_xattn_Wq, L3_xattn_bq, L3_xattn_Wk, L3_xattn_bk, L3_xattn_Wv, L3_xattn_bv, L3_xattn_Wo, L3_xattn_bo, L3_ffn_weight):
    import jax
    import jax.numpy as jnp

    def _L0_attn_ref(x, rms_scale, split_scale, W_K, W_ugg, W_out):
        import jax, jax.numpy as jnp
        import numpy as np
        EPS = 1e-08

        def _combine(c1, c2):
            a1, b1 = c1
            a2, b2 = c2
            return (a1 * a2, a2 * b1 + b2)
        B, S, D = x.shape
        residual = x
        norm = jnp.linalg.norm(x, axis=-1, keepdims=True) * D ** (-0.5)
        xn = rms_scale * x / (norm + EPS) * split_scale
        K = jax.nn.sigmoid(xn @ W_K)
        u, g_in, g_out = jnp.split(xn @ W_ugg, 3, axis=-1)
        u = u * jax.nn.sigmoid(g_in) * (1.0 - K)
        g_out = jax.nn.sigmoid(g_out)
        Kshift = jnp.concatenate([jnp.zeros_like(K[:, :1]), K[:, :-1]], axis=1)
        _, outputs = jax.lax.associative_scan(_combine, (Kshift, u), axis=1)
        y = outputs * g_out @ W_out
        return y + residual

    def _L0_xattn_ref(x, latents, mask, g1, b1, g2, b2, Wq, Wkv, Wout):
        import jax, jax.numpy as jnp
        import numpy as np
        EPS = 1e-05

        def layer_norm(x, g, b):
            mu = jnp.mean(x, axis=-1, keepdims=True)
            var = jnp.mean((x - mu) ** 2, axis=-1, keepdims=True)
            return (x - mu) * jax.lax.rsqrt(var + EPS) * g + b
        heads, dim_head = (16, 64)
        b, n, D = x.shape
        l = latents.shape[1]
        xn = layer_norm(x, g1, b1)
        ln_lat = layer_norm(latents, g2, b2)
        q = ln_lat @ Wq
        kv = jnp.concatenate([xn, ln_lat], axis=1) @ Wkv
        k, v = jnp.split(kv, 2, axis=-1)

        def to_heads(t):
            return t.reshape(t.shape[0], t.shape[1], heads, dim_head).transpose(0, 2, 1, 3)
        q, k, v = (to_heads(q), to_heads(k), to_heads(v))
        scale = 1.0 / np.sqrt(np.sqrt(dim_head)).astype(np.float32)
        weight = jnp.einsum('bhld,bhnd->bhln', q * scale, k * scale)
        full_mask = jnp.concatenate([mask, jnp.ones((b, l), dtype=bool)], axis=1)
        neg = -jnp.finfo(weight.dtype).max
        weight = jnp.where(full_mask[:, None, None, :], weight, neg)
        weight = jax.nn.softmax(weight.astype(jnp.float32), axis=-1).astype(q.dtype)
        out = jnp.einsum('bhln,bhnd->bhld', weight, v)
        out = out.transpose(0, 2, 1, 3).reshape(b, l, heads * dim_head)
        return out @ Wout

    def _L0_ffn_ref(x, w1_w, w1_s, w2_w, w2_s, h1_w, h1_s, h2_w, h2_s, w3_w, w3_s):
        import jax, jax.numpy as jnp
        import numpy as np
        D_IN, D_HID = (256, 1024)

        def _ternary(key, shape):
            return jax.random.randint(key, shape, -1, 2).astype(jnp.float32)

        def _tlin(x, w, s):
            return jnp.einsum('bsi,oi->bso', x, w) * s
        h = jax.nn.silu(_tlin(x, w1_w, w1_s)) * _tlin(x, w2_w, w2_s)
        h = jax.nn.gelu(_tlin(h, h1_w, h1_s), approximate=False)
        h = jax.nn.gelu(_tlin(h, h2_w, h2_s), approximate=False)
        return _tlin(h, w3_w, w3_s)

    def _L1_attn_ref(x, w_qkv, w_out, alpha, beta):
        import jax, jax.numpy as jnp
        import numpy as np
        from functools import partial
        CHUNK = 32

        def _phi(x):
            return jax.nn.elu(x) + 1.0

        def _decay_scan(x, log_d, init):
            B, H, T, D = x.shape
            C = min(CHUNK, T)
            assert T % C == 0
            Nc = T // C
            c_idx = jnp.arange(C, dtype=x.dtype)
            lp = log_d[None, :, None, None] * c_idx[None, None, :, None]
            p = jnp.exp(lp)
            inv_p = jnp.exp(-lp)
            init_p = jnp.exp(log_d[None, :, None, None] * (c_idx + 1.0)[None, None, :, None])
            xc = x.reshape(B, H, Nc, C, D).transpose(2, 0, 1, 3, 4)

            def step(state, chunk):
                cs = jnp.cumsum(chunk * inv_p, axis=2)
                out = cs * p + state[:, :, None, :] * init_p
                return (out[:, :, -1, :], out)
            last, outs = jax.lax.scan(step, init, xc)
            out = outs.transpose(1, 2, 0, 3, 4).reshape(B, H, T, D)
            return (out, last)

        def _reference_tuple_inner(x, w_qkv, w_out, alpha, beta):
            B, T, HID = x.shape
            H = alpha.shape[0]
            D = HID // H
            qkv = x @ w_qkv
            q, k, v = jnp.split(qkv, 3, axis=-1)
            to_bhtd = lambda t: t.reshape(B, T, H, D).transpose(0, 2, 1, 3)
            q = _phi(to_bhtd(q))
            k = _phi(to_bhtd(k))
            v = to_bhtd(v)
            kv = k * v
            log_a = jnp.log(jnp.clip(jax.nn.sigmoid(alpha), 1e-08, None))
            log_b = jnp.log(jnp.clip(jax.nn.sigmoid(beta), 1e-08, None))
            z = jnp.zeros((B, H, D), dtype=x.dtype)
            run_kv_f, kv_f1 = _decay_scan(kv, log_a, z)
            run_ks_f, ks_f1 = _decay_scan(k, log_a, z)
            run_kv_s, kv_s1 = _decay_scan(kv, log_b, z)
            run_ks_s, ks_s1 = _decay_scan(k, log_b, z)
            eps = 1e-06
            den_f = jnp.clip(jnp.sum(q * run_ks_f, axis=-1, keepdims=True), eps, None)
            den_s = jnp.clip(jnp.sum(q * run_ks_s, axis=-1, keepdims=True), eps, None)
            out_f = (q * run_kv_f / den_f).transpose(0, 2, 1, 3).reshape(B, T, HID)
            out_s = (q * run_kv_s / den_s).transpose(0, 2, 1, 3).reshape(B, T, HID)
            out = jnp.concatenate([out_f, out_s], axis=-1) @ w_out
            return (out, (kv_f1, ks_f1, kv_s1, ks_s1))
        return _reference_tuple_inner(x, w_qkv, w_out, alpha, beta)[0]

    def _L1_xattn_ref(values, keys, query, fm_w, fm_b, fc_w, fc_b):
        import jax, jax.numpy as jnp
        import numpy as np
        EMBED = 256
        HEADS = 16
        HEAD_DIM = EMBED // HEADS
        EXP_DIM = 2 * HEAD_DIM

        def _feature_map(x, fm_w, fm_b):
            z = jnp.einsum('nshd,ed->nshe', x, fm_w) + fm_b
            return jnp.concatenate([jnp.exp(z), jnp.exp(-z)], axis=-1)
        N, S, _ = query.shape
        v = values.reshape(N, -1, HEADS, HEAD_DIM)
        k = keys.reshape(N, -1, HEADS, HEAD_DIM)
        q = query.reshape(N, -1, HEADS, HEAD_DIM)
        v, k, q = (_feature_map(x, fm_w, fm_b) for x in (v, k, q))
        scores = jnp.einsum('nqhd,nkhd->nhqk', q, k) / jnp.sqrt(jnp.float32(EMBED))
        attn = jax.nn.softmax(scores, axis=-1)
        out = jnp.einsum('nhql,nlhd->nqhd', attn, v)
        out = out.reshape(N, S, HEADS * EXP_DIM)
        return out @ fc_w.T + fc_b

    def _L1_ffn_ref(x, gamma, beta, router_w, W1, W2):
        import jax, jax.numpy as jnp
        import numpy as np
        E = 8
        K = 2
        D = 256
        H = 4 * D
        EPS = 1e-05
        TEMP = 1.5
        res = x
        mu = jnp.mean(x, axis=-1, keepdims=True)
        var = jnp.mean(jnp.square(x - mu), axis=-1, keepdims=True)
        xn = (x - mu) * jax.lax.rsqrt(var + EPS) * gamma + beta
        logits = jnp.einsum('btd,ed->bte', xn, router_w)
        probs = jax.nn.softmax(logits / TEMP, axis=-1)
        w, idx = jax.lax.top_k(probs, K)
        wdense = jnp.sum(jax.nn.one_hot(idx, E, dtype=w.dtype) * w[..., None], axis=-2)
        h = jax.nn.silu(jnp.einsum('btd,edf->betf', xn, W1))
        y = jnp.einsum('betf,efd->betd', h, W2)
        out = jnp.einsum('bte,betd->btd', wdense, y)
        return out + res

    def _L2_attn_ref(x, Wqkv, bqkv, Wout, bout, gamma, beta):
        import jax, jax.numpy as jnp
        import numpy as np
        NUM_HEADS = 16
        LN_EPS = 1e-05
        FEAT_EPS = 0.0001
        B, L, D = x.shape
        H = NUM_HEADS
        E = D // H
        qkv = x @ Wqkv.T + bqkv
        q, k, v = jnp.split(qkv, 3, axis=-1)
        q = q.reshape(B, L, H, E)
        k = k.reshape(B, L, H, E)
        v = v.reshape(B, L, H, E)
        q = (jax.nn.elu(q) + 1.0 + FEAT_EPS) / jnp.sqrt(jnp.asarray(E, q.dtype))
        k = jax.nn.elu(k) + 1.0 + FEAT_EPS
        kv = jnp.einsum('blhe,blhf->blhef', k, v)
        kv_cumsum = jnp.cumsum(kv, axis=1)
        k_cumsum = jnp.cumsum(k, axis=1)
        num = jnp.einsum('blhe,blhef->blhf', q, kv_cumsum)
        den = jnp.einsum('blhe,blhe->blh', q, k_cumsum)[..., None] + FEAT_EPS
        out = (num / den).reshape(B, L, D)
        out = out @ Wout.T + bout
        mu = jnp.mean(out, axis=-1, keepdims=True)
        var = jnp.var(out, axis=-1, keepdims=True)
        return (out - mu) / jnp.sqrt(var + LN_EPS) * gamma + beta

    def _L2_xattn_ref(values, keys, queries, mask, Wv, Wk, Wq, Wo, bo):
        import jax, jax.numpy as jnp
        import numpy as np
        HEADS = 16
        N, Sq, E = queries.shape
        H = HEADS
        D = E // H
        v = values.reshape(N, -1, H, D)
        k = keys.reshape(N, -1, H, D)
        q = queries.reshape(N, Sq, H, D)
        v = jnp.einsum('nlhd,od->nlho', v, Wv)
        k = jnp.einsum('nlhd,od->nlho', k, Wk)
        q = jnp.einsum('nqhd,od->nqho', q, Wq)
        energy = jnp.einsum('nqhd,nkhd->nhqk', q, k)
        energy = jnp.where(mask == 0, jnp.float32(-1e+20), energy)
        attn = jax.nn.softmax(energy * (1.0 / E ** 0.5), axis=3)
        out = jnp.einsum('nhqk,nkhd->nqhd', attn, v).reshape(N, Sq, E)
        return out @ Wo.T + bo

    def _L2_ffn_ref(x, weight, gate_w, lora_U, lora_V):
        import jax, jax.numpy as jnp
        import numpy as np
        scaling = 1.0 / lora_U.shape[1]
        B, S, D_in = x.shape
        xt = x.reshape(-1, D_in)
        gate = jax.nn.softmax(xt @ gate_w.T, axis=-1)
        base = xt @ weight.T
        t = jnp.einsum('nh,erh->ner', xt, lora_U)
        lora = jnp.einsum('ne,eor,ner->no', gate, lora_V, t)
        out = base + scaling * lora
        return out.reshape(B, S, -1)

    def _L3_attn_ref(x, W_DQ, W_UQ, W_DKV, W_UKV, W_QR, W_KR, W_O, q_norm_w, k_norm_w):
        import jax, jax.numpy as jnp
        import numpy as np
        B, T, D = (2, 512, 256)
        H = 16
        HD = D // H
        DL = 128
        NR = 64
        EPS = 1.1920929e-07

        def _rms_norm(x, w):
            ms = jnp.mean(jnp.square(x), axis=-1, keepdims=True)
            return x * jax.lax.rsqrt(ms + EPS) * w
        b, t, d = x.shape
        scale = HD ** (-0.5)
        xh = x.reshape(b, t, H, HD).transpose(0, 2, 1, 3)
        c_q = jnp.einsum('bhtd,ld->bhtl', xh, W_DQ)
        q_c = jnp.einsum('bhtl,dl->bhtd', c_q, W_UQ)
        q_c_norm = _rms_norm(q_c, q_norm_w)
        q_r = jnp.einsum('bhtd,rd->bhtr', q_c_norm, W_QR)
        q = jnp.concatenate([q_c_norm, q_r], axis=-1)
        c_kv = jnp.einsum('bhtd,ld->bhtl', xh, W_DKV)
        kv = jnp.einsum('bhtl,dl->bhtd', c_kv, W_UKV)
        k_c, v_c = (kv[..., :HD], kv[..., HD:])
        k_c_norm = _rms_norm(k_c, k_norm_w)
        k_r = jnp.einsum('bhtd,rd->bhtr', xh, W_KR)
        k = jnp.concatenate([k_c_norm, k_r], axis=-1)
        scores = jnp.einsum('bhqd,bhkd->bhqk', q, k) * scale
        causal = jnp.triu(jnp.full((t, t), -jnp.inf, dtype=scores.dtype), k=1)
        attn = jax.nn.softmax(scores + causal, axis=-1)
        ctx = jnp.einsum('bhqk,bhkd->bhqd', attn, v_c)
        out = jnp.einsum('bhtd,od->bhto', ctx, W_O)
        return out.transpose(0, 2, 1, 3).reshape(b, t, d)

    def _L3_xattn_ref(query, key, value, Wq, bq, Wk, bk, Wv, bv, Wo, bo):
        import jax, jax.numpy as jnp
        import numpy as np
        D_MODEL = 256
        NUM_HEADS = 16
        D_K = D_MODEL // NUM_HEADS
        B, S = (4, 512)
        b, sq, _ = query.shape
        sk = key.shape[1]
        Q = query @ Wq + bq
        K = key @ Wk + bk
        V = value @ Wv + bv
        Q = Q.reshape(b, sq, NUM_HEADS, D_K).transpose(0, 2, 1, 3)
        K = K.reshape(b, sk, NUM_HEADS, D_K).transpose(0, 2, 1, 3)
        V = V.reshape(b, sk, NUM_HEADS, D_K).transpose(0, 2, 1, 3)
        scores = jnp.einsum('bhqd,bhkd->bhqk', Q, K) / jnp.sqrt(jnp.float32(D_K))
        attn = jax.nn.softmax(scores, axis=-1)
        out = jnp.einsum('bhqk,bhkd->bhqd', attn, V)
        out = out.transpose(0, 2, 1, 3).reshape(b, sq, D_MODEL)
        return out @ Wo + bo

    def _L3_ffn_ref(x, weight):
        import jax, jax.numpy as jnp
        import numpy as np
        b_weight = jnp.sign(weight)
        return jnp.einsum('bsi,oi->bso', x, b_weight)
    x = x + _L0_attn_ref(_layernorm(x, axis=-1), L0_attn_rms_scale, L0_attn_split_scale, L0_attn_W_K, L0_attn_W_ugg, L0_attn_W_out)
    x = x + _L0_xattn_ref(ctx_1024, _layernorm(x, axis=-1), mask_BxS2_bk0, L0_xattn_g1, L0_xattn_b1, L0_xattn_g2, L0_xattn_b2, L0_xattn_Wq, L0_xattn_Wkv, L0_xattn_Wout)
    x = x + _L0_ffn_ref(_layernorm(x, axis=-1), L0_ffn_w1_w, L0_ffn_w1_s, L0_ffn_w2_w, L0_ffn_w2_s, L0_ffn_h1_w, L0_ffn_h1_s, L0_ffn_h2_w, L0_ffn_h2_s, L0_ffn_w3_w, L0_ffn_w3_s)
    x = x + _L1_attn_ref(_layernorm(x, axis=-1), L1_attn_w_qkv, L1_attn_w_out, L1_attn_alpha, L1_attn_beta)
    x = x + _L1_xattn_ref(ctx_1024, ctx_1024, _layernorm(x, axis=-1), L1_xattn_fm_w, L1_xattn_fm_b, L1_xattn_fc_w, L1_xattn_fc_b)
    x = x + _L1_ffn_ref(_layernorm(x, axis=-1), L1_ffn_gamma, L1_ffn_beta, L1_ffn_router_w, L1_ffn_W1, L1_ffn_W2)
    x = x + _L2_attn_ref(_layernorm(x, axis=-1), L2_attn_Wqkv, L2_attn_bqkv, L2_attn_Wout, L2_attn_bout, L2_attn_gamma, L2_attn_beta)
    x = x + _L2_xattn_ref(ctx_1024, ctx_1024, _layernorm(x, axis=-1), mask_Bx1xSxS2_if1, L2_xattn_Wv, L2_xattn_Wk, L2_xattn_Wq, L2_xattn_Wo, L2_xattn_bo)
    x = x + _L2_ffn_ref(_layernorm(x, axis=-1), L2_ffn_weight, L2_ffn_gate_w, L2_ffn_lora_U, L2_ffn_lora_V)
    x = x + _L3_attn_ref(_layernorm(x, axis=-1), L3_attn_W_DQ, L3_attn_W_UQ, L3_attn_W_DKV, L3_attn_W_UKV, L3_attn_W_QR, L3_attn_W_KR, L3_attn_W_O, L3_attn_q_norm_w, L3_attn_k_norm_w)
    x = x + _L3_xattn_ref(_layernorm(x, axis=-1), ctx_1024, ctx_1024, L3_xattn_Wq, L3_xattn_bq, L3_xattn_Wk, L3_xattn_bk, L3_xattn_Wv, L3_xattn_bv, L3_xattn_Wo, L3_xattn_bo)
    x = x + _L3_ffn_ref(_layernorm(x, axis=-1), L3_ffn_weight)
    return x

_drawn_inputs = setup_inputs


def setup_inputs(seed=0):
    import zlib

    import numpy as np

    out = dict(_drawn_inputs(seed))
    spreads = {'L0_attn_rms_scale': (1.0, 0.2),
     'L0_xattn_g1': (1.0, 0.2),
     'L0_xattn_b1': (0.0, 0.1),
     'L0_xattn_g2': (1.0, 0.2),
     'L0_xattn_b2': (0.0, 0.1),
     'L1_xattn_fc_b': (0.0, 0.1),
     'L1_ffn_gamma': (1.0, 0.2),
     'L1_ffn_beta': (0.0, 0.1),
     'L2_attn_bqkv': (0.0, 0.1),
     'L2_attn_bout': (0.0, 0.1),
     'L2_attn_gamma': (1.0, 0.2),
     'L2_attn_beta': (0.0, 0.1),
     'L2_xattn_bo': (0.0, 0.1),
     'L3_attn_q_norm_w': (1.0, 0.2),
     'L3_attn_k_norm_w': (1.0, 0.2),
     'L3_xattn_bq': (0.0, 0.1),
     'L3_xattn_bk': (0.0, 0.1),
     'L3_xattn_bv': (0.0, 0.1),
     'L3_xattn_bo': (0.0, 0.1)}
    factors = {}
    for name, (base, spread) in spreads.items():
        noise = np.random.default_rng([zlib.crc32(name.encode()), seed]).standard_normal(out[name].shape)
        drawn = base * np.exp(spread * noise) if base else spread * noise
        out[name] = jnp.asarray(drawn.astype(out[name].dtype))
    for name, factor in factors.items():
        out[name] = (out[name] * factor).astype(out[name].dtype)
    return out
```

```python
import numpy as np
from contextlib import ExitStack
import concourse.bass as bass
from concourse import mybir

F32 = mybir.dt.float32
ALU = mybir.AluOpType
ACT = mybir.ActivationFunctionType
AXX = mybir.AxisListType.X
ds = bass.ds

P = 128
B, S, D = 2, 1024, 256
NT = B * S // P
CH = 512
TC = CH // P
NC = B * S // CH
KD = D // P
L2 = 77
LN_EPS = 1e-5


CREDITED = ("z_added", "x_added", "zT_copied", "state_made", "pv_done", "o_read")


class Event:

    def __init__(self, nc, name):
        self.sem = nc.alloc_semaphore(name)
        self.base = int(name in CREDITED)
        self.per = 0

    def begin(self, per):
        self.per = per

    def at(self, it, k):
        return self.sem, self.base + it * self.per + k

    def end(self, iters=1):
        self.base += self.per * iters


class Banks:

    def __init__(self, g, fills):
        self.g = g
        self.bank, self.nth, self.per = {}, {}, [0] * 8
        for name, b in fills:
            assert name not in self.bank
            self.bank[name], self.nth[name] = b, self.per[b]
            self.per[b] += 1

    def free(self, name, it):
        b = self.bank[name]
        return self.g.bank_free[b], self.g.fills[b] + it * self.per[b] + self.nth[name]

    def full(self, name, it):
        b = self.bank[name]
        return self.g.bank_full[b], self.g.fills[b] + it * self.per[b] + self.nth[name] + 1

    def read(self, name, it):
        sem, n = self.free(name, it)
        return sem, n + 1

    def fill(self, name):
        return self.g.bank_full[self.bank[name]]

    def release(self, name):
        return self.g.bank_free[self.bank[name]]

    def end(self, iters=1):
        for b in range(8):
            self.g.fills[b] += self.per[b] * iters


class Chain:

    def __init__(self, eng, event, it):
        self.eng, self.event, self.it, self.n = eng, event, it, 0

    def __call__(self, ins):
        self.n += 1
        ins.then_inc(self.event.sem, 1)
        self.eng.wait_ge(*self.event.at(self.it, self.n))

    def close(self):
        assert self.n == self.event.per, (self.n, self.event.per)


class Kernel:

    def __init__(self, nc, ctx):
        self.nc = nc
        self.ctx = ctx
        self.events = {}
        self.names = {}
        self.fills = [1] * 8
        self.bank_full = [nc.alloc_semaphore(f"bank_full{b}") for b in range(8)]
        self.bank_free = [nc.alloc_semaphore(f"bank_free{b}") for b in range(8)]
        self.x = self.sb(ctx, "x", [P, NT, D])
        self.ident = self.sb(ctx, "ident", [P, P])
        self.ps = ctx.enter_context(nc.psum_tensor("ps", [P, 8, 512], F32))
        self.eps = self.sb(ctx, "eps", [P, 4])
        self.bn = self.sb(ctx, "bn", [P, NT, 6])
        self.mean = self.sb(ctx, "mean", [P, NT])
        self.rstd = self.sb(ctx, "rstd", [P, NT])
        self.std = self.sb(ctx, "std", [P, NT])
        self.bt = self.sb(ctx, "bt", [P, 3, NT])
        self.stage = 0

    def sb(self, ctx, name, shape, dt=F32):
        self.names[name] = n = self.names.get(name, 0) + 1
        return ctx.enter_context(self.nc.sbuf_tensor(name if n == 1 else f"{name}_{n}", shape, dt))

    def ev(self, name, per=1):
        e = self.events.get(name)
        if e is None:
            e = self.events[name] = Event(self.nc, name)
        e.begin(per)
        return e

    def bk(self, b):
        return self.ps[:, b, :]


def rows(w):
    return w.rearrange("(k p) n -> p k n", p=P)


def col(v):
    return v.rearrange("(k p) -> p k", p=P)


def load(eng, dst, src, event):
    eng.dma_start(dst, src).then_inc(event.sem, 16)


def opening(g, x):
    nc = g.nc
    loaded = g.ev("x_loaded", 16)
    zeroed = g.ev("consts_zeroed", 1)
    made = g.ev("consts_made", 1)
    credited = [g.ev(name).sem for name in CREDITED]
    with nc.Block() as block:
        @block.sync
        def _(sp):
            sp.dma_start(g.x[:], x.rearrange("b (t p) d -> p (b t) d", p=P)).then_inc(loaded.sem, 16)
            sp.wait_ge(*loaded.at(0, 16))

        @block.scalar
        def _(act):
            for sem in g.bank_full + g.bank_free + credited:
                act.sem_inc(sem, 1)

        @block.vector
        def _(dve):
            dve.memset(g.eps[:, 0:1], LN_EPS)
            dve.memset(g.eps[:, 1:2], 0.0)
            dve.memset(g.eps[:, 2:3], 1.0)
            dve.memset(g.eps[:, 3:4], 1.1920929e-07)

        @block.gpsimd
        def _(pool):
            pool.memset(g.ident[:], 0.0).then_inc(zeroed.sem, 1)
            pool.wait_ge(*zeroed.at(0, 1))
            pool.affine_select(out=g.ident[:], in_=g.ident[:], compare_op=ALU.not_equal, fill=1.0,
                               base=0, pattern=[[-1, P]], channel_multiplier=1).then_inc(made.sem, 1)
            pool.wait_ge(*made.at(0, 1))
    for e in (loaded, zeroed, made):
        e.end()


def ln_stats_vector(g, dve, src, n, spread, rooted, link):
    with dve.Fori(0, n) as t:
        ins = dve.bn_stats(g.bn[:, ds(t, 1), :].rearrange("p a b -> p (a b)"),
                           src[:, ds(t, 1), :].rearrange("p a b -> p (a b)"))
        ins.then_inc(g.ev_bn.sem, 1)
    dve.wait_ge(g.ev_bn.sem, g.ev_bn.base + n)
    bt = g.bt[:, :, 0:n]
    dve.tensor_tensor(bt[:, 0, :], g.bn[:, 0:n, 1], g.bn[:, 0:n, 4], ALU.subtract)
    dve.tensor_tensor(bt[:, 1, :], g.bn[:, 0:n, 2], g.bn[:, 0:n, 5], ALU.add)
    link(dve.tensor_tensor(bt[:, 2, :], g.bn[:, 0:n, 1], g.bn[:, 0:n, 4], ALU.add))
    dve.tensor_scalar(g.mean[:, 0:n], bt[:, 2, :], 0.5, None, ALU.mult)
    link(dve.tensor_tensor(bt[:, 0, :], bt[:, 0, :], bt[:, 0, :], ALU.mult))
    dve.scalar_tensor_tensor(bt[:, 1, :], bt[:, 0, :], D / 4.0, bt[:, 1, :], ALU.mult, ALU.add)\
        .then_inc(spread.sem, 1)
    dve.wait_ge(*rooted.at(0, 1))
    link(dve.reciprocal(g.rstd[:, 0:n], g.std[:, 0:n]))


LN_LINKS = 3


def ln_stats_scalar(g, act, n, spread, rooted):
    act.wait_ge(*spread.at(0, 1))
    act.activation(g.std[:, 0:n], g.bt[:, 1, 0:n], ACT.Sqrt, scale=1.0 / D, bias=g.eps[:, 0:1])\
        .then_inc(rooted.sem, 1)


def ln_block(g):
    nc = g.nc
    g.ev_bn = g.ev("bn_stats_done", NT)
    spread, rooted, step = g.ev("ln_variance", 1), g.ev("ln_root", 1), g.ev("dve_step", LN_LINKS)
    with nc.Block() as block:
        @block.vector
        def _(dve):
            link = Chain(dve, step, 0)
            ln_stats_vector(g, dve, g.x, NT, spread, rooted, link)
            link.close()

        @block.scalar
        def _(act):
            ln_stats_scalar(g, act, NT, spread, rooted)
    for e in (g.ev_bn, spread, rooted, step):
        e.end()


def normalise(g, dve, c, z4):
    for j in range(TC):
        t = ds(c * TC + j, 1)
        ins = dve.tensor_scalar(z4[:, j, :], g.x[:, t, :].rearrange("p a b -> p (a b)"), g.mean[:, t], g.rstd[:, t],
                                ALU.subtract, ALU.mult)
    return ins


def turn(g, pe, bk, it, names, src4):
    for k, name in enumerate(names):
        pe.wait_ge(*bk.free(name, it))
        for j in range(TC):
            ins = pe.transpose(g.ps[:, bk.bank[name], j * P:(j + 1) * P], src4[:, j, k * P:(k + 1) * P], g.ident[:])
        ins.then_inc(bk.fill(name), 1)


def twice_normalised(g, add):
    nc = g.nc
    ln_block(g)
    with nc.Block() as block:
        @block.vector
        def _(dve):
            with dve.Fori(0, NT) as t:
                tt = ds(t, 1)
                dve.tensor_scalar(g.z[:, tt, :].rearrange("p a b -> p (a b)"), g.x[:, tt, :].rearrange("p a b -> p (a b)"),
                                  g.mean[:, tt], g.rstd[:, tt], ALU.subtract, ALU.mult)
    g.ev_bn = g.ev("bn_stats_done", NT)
    spread, rooted, step = g.ev("ln_variance", 1), g.ev("ln_root", 1), g.ev("dve_step", LN_LINKS)
    with nc.Block() as block:
        @block.vector
        def _(dve):
            link = Chain(dve, step, 0)
            ln_stats_vector(g, dve, g.z, NT, spread, rooted, link)
            link.close()

        @block.gpsimd
        def _(pool):
            if add:
                with pool.Fori(0, NC) as c:
                    t = ds(c * TC, TC)
                    pool.tensor_tensor(g.x[:, t, :], g.x[:, t, :], g.z[:, t, :], ALU.add)

        @block.scalar
        def _(act):
            ln_stats_scalar(g, act, NT, spread, rooted)
    for e in (g.ev_bn, spread, rooted, step):
        e.end()


def stage_l0_attn(g, rms, split, W_K, W_ugg, W_out):
    nc = g.nc
    H = 512
    HB = H // P
    ln_block(g)
    with ExitStack() as ctx:
        sb = lambda n, s: g.sb(ctx, n, s)
        wk, wu, wo = sb("wk", [P, KD, H]), sb("wu", [P, KD, 3 * H]), sb("wo", [P, HB, D])
        rs, sps, gain = sb("rs", [P, KD]), sb("sps", [P, KD]), sb("gain", [P, KD])
        z4, xn4 = sb("z4", [P, TC, D]), sb("xn4", [P, TC, D])
        sq, ss, rn = sb("sq", [P, TC, D]), sb("ss", [P, TC]), sb("rn", [P, TC])
        zT = sb("zT", [P, KD, CH])
        keep = sb("keep", [P, HB, CH + 1])
        gi, go = sb("gi", [P, HB, CH]), sb("go", [P, HB, CH])
        u, sc, yT = sb("u", [P, HB, CH]), sb("sc", [P, HB, CH]), sb("yT", [P, HB, CH])
        carry = sb("carry", [P, HB])
        bk = Banks(g, [("t0", 0), ("t1", 1)] + [(f"{n}{f}", (f % 2) * 4 + i) for f in range(HB)
                                                for i, n in enumerate("kiuo")]
                   + [(f"y{j}", j) for j in range(TC)])
        w_in, gain_made = g.ev("w_loaded", 16 * 5), g.ev("gain_made", 1)
        z_made, norm_made, xn_made = g.ev("z_made", 1), g.ev("norm_made", 2), g.ev("xn_made", 1)
        z_added, step, gated = g.ev("z_added", 1), g.ev("dve_step", 3 + 2 * HB), g.ev("gated_made", HB)
        with nc.Block() as block:
            @block.sync
            def _(sp):
                load(sp, rs[:], rms, w_in)
                load(sp, sps[:], split, w_in)
                load(sp, wk[:], rows(W_K), w_in)
                load(sp, wu[:], rows(W_ugg), w_in)
                load(sp, wo[:], rows(W_out), w_in)

            @block.gpsimd
            def _(pool):
                with pool.Fori(0, NC) as c:
                    pool.wait_ge(*z_made.at(c, 1))
                    pool.tensor_tensor(g.x[:, ds(c * TC, TC), :], g.x[:, ds(c * TC, TC), :], z4[:], ALU.add)\
                        .then_inc(z_added.sem, 1)

            @block.tensor
            def _(pe):
                pe.wait_ge(*w_in.at(0, 80))
                with pe.Fori(0, NC) as c:
                    pe.wait_ge(*xn_made.at(c, 1))
                    turn(g, pe, bk, c, ("t0", "t1"), xn4)
                    pe.wait_ge(*bk.read("t0", c))
                    pe.wait_ge(*bk.read("t1", c))
                    for f in range(HB):
                        for n in "kiuo":
                            name = f"{n}{f}"
                            w = wk if n == "k" else wu[:, :, {"u": 0, "i": H, "o": 2 * H}[n]:{"u": 0, "i": H, "o": 2 * H}[n] + H]
                            pe.wait_ge(*bk.free(name, c))
                            for k in range(KD):
                                ins = pe.matmul(g.bk(bk.bank[name]), w[:, k, f * P:(f + 1) * P], zT[:, k, :],
                                                start=k == 0, stop=k == KD - 1)
                            ins.then_inc(bk.fill(name), 1)
                    pe.wait_ge(*gated.at(c, HB))
                    for j in range(TC):
                        pe.wait_ge(*bk.free(f"y{j}", c))
                        for f in range(HB):
                            ins = pe.matmul(g.bk(j)[:, 0:D], yT[:, f, j * P:(j + 1) * P], wo[:, f, :],
                                            start=f == 0, stop=f == HB - 1)
                        ins.then_inc(bk.fill(f"y{j}"), 1)

            @block.scalar
            def _(act):
                act.wait_ge(*gain_made.at(0, 1))
                with act.Fori(0, NC) as c:
                    act.wait_ge(*z_made.at(c, 1))
                    for j in range(TC):
                        ins = act.activation(sq[:, j, :], z4[:, j, :], ACT.Square, accum_out=ss[:, j:j + 1])
                    ins.then_inc(norm_made.sem, 1)
                    act.wait_ge(*norm_made.at(c, 1))
                    act.activation(rn[:], ss[:], ACT.Sqrt, scale=1.0 / D).then_inc(norm_made.sem, 1)
                    act.wait_ge(*bk.full("t0", c))
                    act.activation(zT[:, 0, :], g.bk(0), ACT.Copy, scale=gain[:, 0:1]).then_inc(bk.release("t0"), 1)
                    for f in range(HB):
                        for n, dst in (("k", keep[:, f, 1:CH + 1]), ("i", gi[:, f, :]), ("o", go[:, f, :])):
                            name = f"{n}{f}"
                            act.wait_ge(*bk.full(name, c))
                            act.activation(dst, g.bk(bk.bank[name]), ACT.Sigmoid).then_inc(bk.release(name), 1)

            @block.vector
            def _(dve):
                dve.wait_ge(*w_in.at(0, 80))
                dve.tensor_tensor(gain[:], rs[:], sps[:], ALU.mult).then_inc(gain_made.sem, 1)
                dve.wait_ge(*gain_made.at(0, 1))
                with dve.Fori(0, B) as b:
                    dve.memset(keep[:, :, 0:1], 0.0)
                    dve.memset(carry[:], 0.0)
                    with dve.Fori(0, NC // B) as h:
                        c = b * (NC // B) + h
                        link = Chain(dve, step, c)
                        dve.wait_ge(*z_added.at(c, 0))
                        normalise(g, dve, c, z4).then_inc(z_made.sem, 1)
                        dve.wait_ge(*norm_made.at(c, 2))
                        link(dve.tensor_scalar(rn[:], rn[:], 1e-8, None, ALU.add))
                        link(dve.reciprocal(rn[:], rn[:]))
                        for j in range(TC):
                            ins = dve.tensor_scalar(xn4[:, j, :], z4[:, j, :], rn[:, j:j + 1], None, ALU.mult)
                        ins.then_inc(xn_made.sem, 1)
                        dve.wait_ge(*bk.full("t1", c))
                        dve.tensor_scalar(zT[:, 1, :], g.bk(1), gain[:, 1:2], None, ALU.mult)\
                            .then_inc(bk.release("t1"), 1)
                        for f in range(HB):
                            dve.wait_ge(*bk.full(f"u{f}", c))
                            dve.wait_ge(*bk.read(f"i{f}", c))
                            dve.tensor_tensor(u[:, f, :], g.bk(bk.bank[f"u{f}"]), gi[:, f, :], ALU.mult)\
                                .then_inc(bk.release(f"u{f}"), 1)
                            dve.wait_ge(*bk.read(f"u{f}", c))
                            link(dve.scalar_tensor_tensor(u[:, f, :], keep[:, f, 1:CH + 1], 1.0, u[:, f, :],
                                                          ALU.subtract, ALU.mult))
                            link(dve.tensor_tensor_scan(sc[:, f, :], keep[:, f, 0:CH], u[:, f, :],
                                                        carry[:, f:f + 1], ALU.mult, ALU.subtract))
                            dve.wait_ge(*bk.read(f"o{f}", c))
                            dve.tensor_tensor(yT[:, f, :], sc[:, f, :], go[:, f, :], ALU.mult)\
                                .then_inc(gated.sem, 1)
                        dve.tensor_scalar(keep[:, :, 0:1], keep[:, :, CH:CH + 1], 1.0, None, ALU.mult)
                        link(dve.tensor_scalar(carry[:], sc[:, :, CH - 1], 1.0, None, ALU.mult))
                        dve.wait_ge(*z_added.at(c, 1))
                        for j in range(TC):
                            dve.wait_ge(*bk.full(f"y{j}", c))
                            xt = g.x[:, ds(c * TC + j, 1), :]
                            dve.tensor_tensor(xt, xt, g.bk(j)[:, 0:D].rearrange("p (a n) -> p a n", a=1), ALU.add)\
                                .then_inc(bk.release(f"y{j}"), 1)
                        link.close()
        bk.end(NC)
        for e in (w_in, gain_made):
            e.end()
        for e in (z_made, norm_made, xn_made, z_added, step, gated):
            e.end(NC)


def stage_l0_xattn(g, ctx_rows, mask_row, mask_col, g1, b1, g2, b2, Wq, Wk, Wv, Wo):
    nc = g.nc
    HN, HD = 8, 64
    PR = HN // 2
    HW = HN * HD
    NK = S // P
    NB = NC // B
    SC = float(np.float32(1.0) / np.sqrt(np.sqrt(HD)).astype(np.float32))
    with ExitStack() as ctx:
        sb = lambda n, s, dt=F32: g.sb(ctx, n, s, dt)
        zT_all, cxT = sb("zT_all", [P, KD, B * S]), sb("cxT", [P, KD, B * L2])
        mrow, mcol = sb("mrow", [P, B * L2]), sb("mcol", [L2, B])
        with ExitStack() as inner:
            sb = lambda n, s, dt=F32: g.sb(inner, n, s, dt)
            g.z = sb("z_all", [P, NT, D])
            twice_normalised(g, add=False)
            cx, cz, z4 = sb("cx", [P, B, D]), sb("cz", [P, B, D]), sb("z4", [P, TC, D])
            cols = sb("cols", [P, 4, KD])
            mrow_int, mcol_int = sb("mrow_int", [P, B * L2], mybir.dt.int32), sb("mcol_int", [L2, B], mybir.dt.int32)
            bk = Banks(g, [("t0", 0), ("t1", 1)])
            z_made = g.ev("z_made", 1)
            w_in = g.ev("w_loaded", 96)
            zeroed = g.ev("ctx_zeroed", 1)
            with nc.Block() as block:
                @block.sync
                def _(sp):
                    for i, v in enumerate((g1, b1, g2, b2)):
                        load(sp, cols[:, i, :], v, w_in)
                    load(sp, mrow_int[:], mask_row, w_in)
                    load(sp, mcol_int[:], mask_col, w_in)

                @block.vector
                def _(dve):
                    dve.memset(cx[:], 0.0).then_inc(zeroed.sem, 1)
                    with dve.Fori(0, NC) as c:
                        for k in range(KD):
                            dve.wait_ge(*bk.free(f"t{k}", c))
                        for j in range(TC):
                            t = ds(c * TC + j, 1)
                            ins = dve.tensor_scalar(z4[:, j, :], g.z[:, t, :].rearrange("p a b -> p (a b)"),
                                                    g.mean[:, t], g.rstd[:, t], ALU.subtract, ALU.mult)
                        ins.then_inc(z_made.sem, 1)

                @block.tensor
                def _(pe):
                    with pe.Fori(0, NC) as c:
                        pe.wait_ge(*z_made.at(c, 1))
                        turn(g, pe, bk, c, ("t0", "t1"), z4)

                @block.scalar
                def _(act):
                    act.wait_ge(*w_in.at(0, 96))
                    with act.Fori(0, NC) as c:
                        for k in range(KD):
                            act.wait_ge(*bk.full(f"t{k}", c))
                            act.activation(zT_all[:, k, ds(c * CH, CH)], g.bk(k), ACT.Identity, scale=cols[:, 2, k:k + 1],
                                           bias=cols[:, 3, k:k + 1]).then_inc(bk.release(f"t{k}"), 1)
            bk.end(NC)
            z_made.end(NC)
            w_in.end()
            zeroed.end()

            g.ev_bn = g.ev("bn_stats_done", B)
            spread, rooted, step = g.ev("ln_variance", 1), g.ev("ln_root", 1), g.ev("dve_step", LN_LINKS)
            w_in, cz_made = g.ev("w_loaded", 16), g.ev("z_made", 1)
            bk = Banks(g, [("t0", 0), ("t1", 1)])
            with nc.Block() as block:
                @block.sync
                def _(sp):
                    load(sp, cx[0:L2, :, :], ctx_rows.rearrange("b l d -> l b d"), w_in)

                @block.vector
                def _(dve):
                    dve.wait_ge(*w_in.at(0, 16))
                    dve.tensor_scalar(mrow[:], mrow_int[:], 1.0, 1e30, ALU.subtract, ALU.mult)
                    dve.tensor_scalar(mcol[:], mcol_int[:], 1.0, 1e30, ALU.subtract, ALU.mult)
                    link = Chain(dve, step, 0)
                    ln_stats_vector(g, dve, cx, B, spread, rooted, link)
                    link.close()
                    for b in range(B):
                        ins = dve.tensor_scalar(cz[:, b, :], cx[:, b, :], g.mean[:, b:b + 1], g.rstd[:, b:b + 1], ALU.subtract, ALU.mult)
                    ins.then_inc(cz_made.sem, 1)

                @block.scalar
                def _(act):
                    ln_stats_scalar(g, act, B, spread, rooted)
                    for k in range(KD):
                        act.wait_ge(*bk.full(f"t{k}", 0))
                        act.activation(cxT[:, k, :], g.bk(k)[:, 0:B * L2], ACT.Identity, scale=cols[:, 0, k:k + 1],
                                       bias=cols[:, 1, k:k + 1]).then_inc(bk.release(f"t{k}"), 1)

                @block.tensor
                def _(pe):
                    pe.wait_ge(*cz_made.at(0, 1))
                    for k in range(KD):
                        pe.wait_ge(*bk.free(f"t{k}", 0))
                        for b in range(B):
                            ins = pe.transpose(g.bk(k)[:, b * L2:(b + 1) * L2], cz[0:L2, b, k * P:(k + 1) * P], g.ident[0:L2, 0:L2])
                        ins.then_inc(bk.fill(f"t{k}"), 1)
            bk.end()
            for e in (g.ev_bn, spread, rooted, step, w_in, cz_made):
                e.end()

        sb = lambda n, s, dt=F32: g.sb(ctx, n, s, dt)
        wq, wk, wv, wo = sb("wq", [P, KD, HW]), sb("wk", [P, KD, HW]), sb("wv", [P, KD, HW]), sb("wo", [P, PR, D])
        zb, cb = sb("zb", [P, KD, S]), sb("cb", [P, KD, L2])
        kT, qT = sb("kT", [HD + 1, HN, S + L2]), sb("qT", [HD + 1, HN, S])
        v = sb("v", [P, NK + 1, PR, 3, HD])
        mx, mxa = sb("mx", [P, 2, TC, HN]), sb("mxa", [P, 2, TC, 2, HN])
        mc, nm = sb("mc", [P, 2, TC, HN]), sb("nm", [P, 2, TC, HN])
        nT = sb("nT", [HN, 2, CH])
        pT = sb("pT", [P, 4, CH])
        rec, oT = sb("rec", [P, 2, CH]), sb("oT", [P, PR, CH])

        kcols = [(0, CH), (CH, CH), (S, L2)]
        fills, n, bank = [], 0, {}

        def fill(name, ring):
            nonlocal n
            bank[name] = ring[n % len(ring)]
            n += 1
            fills.append((name, bank[name]))

        for p in range(PR):
            for i in range(3):
                fill(f"k{p}_{i}", range(8))
        for t in range(NK + 1):
            fill(f"v{t}", range(8))
        for cc in range(2):
            for p in range(PR):
                fill(f"q{cc}_{p}", range(8))
        for cc in range(2):
            for j in range(TC):
                for h in range(HN):
                    m = (cc * TC + j) * HN + h
                    fills += [(f"m{cc}_{j}_{h}_{a}", 2 * (m % 2) + a) for a in range(2)]
                fills += [(f"c{cc}_{j}_{a}", 4 + a) for a in range(2)]
            fills.append((f"n{cc}", 7))
        for cc in range(2):
            n = 0
            for h in range(HN):
                for t in range(NK + 1):
                    fill(f"s{cc}_{h}_{t}", range(4))
                fills.append((f"o{cc}_{h}", 4 + h % 2))
            fills += [(f"y{cc}_{j}", 6 + j % 2) for j in range(TC)]
        bk = Banks(g, fills)
        NP = 2 * HN * (NK + 1)
        w_in, wo_in, ones = g.ev("w_loaded", 48), g.ev("wo_loaded", 16), g.ev("ones_made", 2)
        batch = g.ev("batch_copied", 3)
        mb = sb("mb", [L2, 1])
        nm_made, row_in, pv, mstep = g.ev("negmax_made", 2), [g.ev(f"negmax_row{cc}_in", 16) for cc in range(2)], g.ev("pv_done", NP), g.ev("ctx_masked", 2 * 2 * TC)
        step = g.ev("dve_step", 4 + 2 * HN)
        half_out = g.ev("even_heads_out", 3 * PR + 2 * PR)
        with nc.Block() as block:
            @block.sync
            def _(sp):
                with sp.Fori(0, B) as b, sp.Fori(0, 2) as half:
                    it = b * 2 + half
                    hs = ds(half, 1)
                    sp.wait_ge(*bk.free("k0_0", it))
                    for dst, src in ((wq, Wq), (wk, Wk), (wv, Wv)):
                        sp.dma_start(dst[:], src[hs].rearrange("a (k p) n -> p (a k) n", p=P)).then_inc(w_in.sem, 16)
                    sp.wait_ge(*bk.free(f"y0_0", it))
                    sp.wait_ge(*bk.free(f"y0_1", it))
                    sp.dma_start(wo[:], Wo[hs].rearrange("a (k p) n -> p (a k) n", p=P)).then_inc(wo_in.sem, 16)
                    for cc in range(2):
                        sp.wait_ge(*bk.read(f"n{cc}", it))
                        sp.dma_start(qT[HD:HD + 1, :, cc * CH:(cc + 1) * CH], nT[:, cc, :]).then_inc(row_in[cc].sem, 16)

            @block.gpsimd
            def _(pool):
                pool.memset(kT[HD:HD + 1, :, :], 1.0).then_inc(ones.sem, 1)
                pool.wait_ge(*ones.at(0, 1))
                pool.memset(v[:, :, :, 1, :], 1.0).then_inc(ones.sem, 1)
                pool.wait_ge(*ones.at(0, 2))
                with pool.Fori(0, B) as b, pool.Fori(0, 2) as half:
                    it = b * 2 + half
                    pool.wait_ge(*pv.at(it, 0))
                    pool.tensor_copy(zb[:], zT_all[:, :, ds(b * S, S)]).then_inc(batch.sem, 1)
                    pool.tensor_copy(cb[:], cxT[:, :, ds(b * L2, L2)]).then_inc(batch.sem, 1)
                    pool.tensor_copy(mb[:], mcol[:, ds(b, 1)]).then_inc(batch.sem, 1)

            @block.tensor
            def _(pe):
                pe.wait_ge(*ones.at(0, 2))
                with pe.Fori(0, B) as b, pe.Fori(0, 2) as half:
                    it = b * 2 + half
                    pe.wait_ge(*w_in.at(it, 48))
                    pe.wait_ge(*batch.at(it, 3))
                    for p in range(PR):
                        for i, (c0, w) in enumerate(kcols):
                            name = f"k{p}_{i}"
                            pe.wait_ge(*bk.free(name, it))
                            for k in range(KD):
                                src = cb[:, k, :] if i == 2 else zb[:, k, c0:c0 + w]
                                ins = pe.matmul(g.bk(bank[name])[:, 0:w], wk[:, k, p * P:(p + 1) * P], src, start=k == 0, stop=k == KD - 1)
                            ins.then_inc(bk.fill(name), 1)
                    for t in range(NK + 1):
                        name, rows_ = f"v{t}", P if t < NK else L2
                        pe.wait_ge(*bk.free(name, it))
                        for k in range(KD):
                            src = zb[:, k, t * P:(t + 1) * P] if t < NK else cb[:, k, :]
                            ins = pe.matmul(g.bk(bank[name])[0:rows_, :], src, wv[:, k, :], start=k == 0, stop=k == KD - 1)
                        ins.then_inc(bk.fill(name), 1)
                    for cc in range(2):
                        for p in range(PR):
                            name = f"q{cc}_{p}"
                            pe.wait_ge(*bk.free(name, it))
                            for k in range(KD):
                                ins = pe.matmul(g.bk(bank[name]), wq[:, k, p * P:(p + 1) * P], zb[:, k, cc * CH:(cc + 1) * CH],
                                                start=k == 0, stop=k == KD - 1)
                            ins.then_inc(bk.fill(name), 1)

                    for p in range(PR):
                        for i in range(3):
                            if bank[f"k{p}_{i}"] not in [bank[f"k{q}_{m}"] for q in range(PR) for m in range(3) if (q, m) > (p, i)]:
                                pe.wait_ge(*bk.read(f"k{p}_{i}", it))
                    for cc in range(2):
                        for p in range(PR):
                            pe.wait_ge(*bk.read(f"q{cc}_{p}", it))
                        for j in range(TC):
                            q0 = cc * CH + j * P
                            for h in range(HN):
                                for a in range(2):
                                    name = f"m{cc}_{j}_{h}_{a}"
                                    pe.wait_ge(*bk.free(name, it))
                                    pe.matmul(g.bk(bk.bank[name]), qT[0:HD, h, q0:q0 + P], kT[0:HD, h, a * CH:(a + 1) * CH],
                                              start=True, stop=True).then_inc(bk.fill(name), 1)
                            for a in range(2):
                                pe.wait_ge(*bk.free(f"c{cc}_{j}_{a}", it))
                                for h4 in range(4):
                                    ins = pe.matmul(g.bk(4 + a)[:, h4 * L2:(h4 + 1) * L2], qT[0:HD, 4 * a + h4, q0:q0 + P],
                                                    kT[0:HD, 4 * a + h4, S:], start=True, stop=True)
                                ins.then_inc(bk.fill(f"c{cc}_{j}_{a}"), 1)
                        pe.wait_ge(*nm_made.at(it, cc + 1))
                        pe.wait_ge(*bk.free(f"n{cc}", it))
                        for j in range(TC):
                            ins = pe.transpose(g.bk(7)[0:HN, j * P:(j + 1) * P], nm[:, cc, j, :], g.ident[:])
                        ins.then_inc(bk.fill(f"n{cc}"), 1)

                    for cc in range(2):
                        pieces = [(h, t) for h in range(HN) for t in range(NK + 1)]

                        def scores(h, t):
                            name, rows_ = f"s{cc}_{h}_{t}", P if t < NK else L2
                            pe.wait_ge(*bk.free(name, it))
                            pe.matmul(g.bk(bank[name])[0:rows_, :], kT[:, h, t * P:t * P + rows_], qT[:, h, cc * CH:(cc + 1) * CH],
                                      start=True, stop=True).then_inc(bk.fill(name), 1)

                        def values(h, t):
                            rows_ = P if t < NK else L2
                            pe.wait_ge(*bk.read(f"s{cc}_{h}_{t}", it))
                            if t == 0:
                                pe.wait_ge(*bk.free(f"o{cc}_{h}", it))
                            a, m = h % 2, h * (NK + 1) + t
                            pe.matmul(g.bk(4 + a), v[0:rows_, t, h // 2, a:a + 2, :].rearrange("p a d -> p (a d)"),
                                      pT[0:rows_, m % 4, :], start=t == 0, stop=t == NK).then_inc(pv.sem, 1)
                            if t == NK:
                                pe.wait_ge(*pv.at(it, cc * HN * (NK + 1) + m + 1))
                                pe.sem_inc(bk.fill(f"o{cc}_{h}"), 1)

                        pe.wait_ge(*row_in[cc].at(it, 16))
                        scores(*pieces[0])
                        scores(*pieces[1])
                        for m, (h, t) in enumerate(pieces):
                            if m + 2 < len(pieces):
                                scores(*pieces[m + 2])
                            values(h, t)
                        if cc == 0:
                            pe.wait_ge(*wo_in.at(it, 16))
                        for j in range(TC):
                            name = f"y{cc}_{j}"
                            pe.wait_ge(*bk.free(name, it))
                            for a in range(2):
                                pe.wait_ge(*bk.read(f"o{cc}_{HN - 2 + a}", it))
                            for p in range(PR):
                                ins = pe.matmul(g.bk(bk.bank[name])[:, 0:D], oT[:, p, j * P:(j + 1) * P], wo[:, p, :],
                                                start=p == 0, stop=p == PR - 1)
                            ins.then_inc(bk.fill(name), 1)

            @block.scalar
            def _(act):
                with act.Fori(0, B) as b, act.Fori(0, 2) as half:
                    it = b * 2 + half
                    for p in range(PR):
                        for i, (c0, w) in enumerate(kcols):
                            name = f"k{p}_{i}"
                            act.wait_ge(*bk.full(name, it))
                            act.activation(kT[0:HD, 2 * p, c0:c0 + w], g.bk(bank[name])[0:HD, 0:w], ACT.Copy, scale=SC).then_inc(half_out.sem, 1)
                    for t in range(NK + 1):
                        name, rows_ = f"v{t}", P if t < NK else L2
                        act.wait_ge(*bk.full(name, it))
                        act.activation(v[0:rows_, t, :, 0:3:2, :], g.bk(bank[name])[0:rows_, :].rearrange("p (r a d) -> p r a d", a=2, d=HD),
                                       ACT.Copy).then_inc(bk.release(name), 1)
                    for cc in range(2):
                        for p in range(PR):
                            name = f"q{cc}_{p}"
                            act.wait_ge(*bk.full(name, it))
                            act.activation(qT[0:HD, 2 * p, cc * CH:(cc + 1) * CH], g.bk(bank[name])[0:HD, :], ACT.Copy, scale=SC)\
                                .then_inc(half_out.sem, 1)
                    for cc in range(2):
                        act.wait_ge(*bk.full(f"n{cc}", it))
                        act.activation(nT[:, cc, :], g.bk(7)[0:HN, :], ACT.Copy).then_inc(bk.release(f"n{cc}"), 1)
                    for cc in range(2):
                        for h in range(HN):
                            for t in range(NK + 1):
                                name, rows_ = f"s{cc}_{h}_{t}", P if t < NK else L2
                                m = h * (NK + 1) + t
                                act.wait_ge(*bk.full(name, it))
                                act.wait_ge(*pv.at(it, max(0, cc * HN * (NK + 1) + m - 3)))
                                act.activation(pT[0:rows_, m % 4, :], g.bk(bank[name])[0:rows_, :], ACT.Exp,
                                               bias=mb[:, 0:1] if t == NK else 0.0).then_inc(bk.release(name), 1)

            @block.vector
            def _(dve):
                with dve.Fori(0, B) as b, dve.Fori(0, 2) as half:
                    it = b * 2 + half
                    link = Chain(dve, step, it)
                    nh = 0
                    for p in range(PR):
                        for i, (c0, w) in enumerate(kcols):
                            name = f"k{p}_{i}"
                            nh += 1
                            dve.wait_ge(*bk.full(name, it))
                            dve.wait_ge(*half_out.at(it, nh))
                            dve.tensor_scalar(kT[0:HD, 2 * p + 1, c0:c0 + w], g.bk(bank[name])[HD:P, 0:w], SC, None, ALU.mult)\
                                .then_inc(bk.release(name), 1)
                    for cc in range(2):
                        for p in range(PR):
                            name = f"q{cc}_{p}"
                            nh += 1
                            dve.wait_ge(*bk.full(name, it))
                            dve.wait_ge(*half_out.at(it, nh))
                            dve.tensor_scalar(qT[0:HD, 2 * p + 1, cc * CH:(cc + 1) * CH], g.bk(bank[name])[HD:P, :], SC, None, ALU.mult)\
                                .then_inc(bk.release(name), 1)
                    ml = 0
                    for cc in range(2):
                        for j in range(TC):
                            for h in range(HN):
                                for a in range(2):
                                    name = f"m{cc}_{j}_{h}_{a}"
                                    dve.wait_ge(*bk.full(name, it))
                                    dve.tensor_reduce(mxa[:, cc, j, a, h:h + 1], g.bk(bk.bank[name]), AXX, ALU.max).then_inc(bk.release(name), 1)
                            for a in range(2):
                                name = f"c{cc}_{j}_{a}"
                                cv = g.bk(4 + a)[:, 0:4 * L2].rearrange("p (h l) -> p h l", l=L2)
                                dve.wait_ge(*bk.full(name, it))
                                ml += 1
                                dve.tensor_tensor(cv, cv, mrow[:, ds(b * L2, L2)].unsqueeze(1).broadcast_to([P, 4, L2]), ALU.add)\
                                    .then_inc(mstep.sem, 1)
                                dve.wait_ge(*mstep.at(it, ml))
                                dve.tensor_reduce(mc[:, cc, j, 4 * a:4 * a + 4], cv, AXX, ALU.max).then_inc(bk.release(name), 1)
                        for a in range(2):
                            dve.wait_ge(*bk.read(f"m{cc}_{TC - 1}_{HN - 2}_{a}", it))
                            dve.wait_ge(*bk.read(f"m{cc}_{TC - 1}_{HN - 1}_{a}", it))
                            dve.wait_ge(*bk.read(f"c{cc}_{TC - 1}_{a}", it))
                        link(dve.tensor_tensor(mx[:, cc], mxa[:, cc, :, 0, :], mxa[:, cc, :, 1, :], ALU.max))
                        link(dve.tensor_tensor(mx[:, cc], mx[:, cc], mc[:, cc], ALU.max))
                        dve.tensor_scalar(nm[:, cc], mx[:, cc], -1.0, None, ALU.mult).then_inc(nm_made.sem, 1)
                    for cc in range(2):
                        for h in range(HN):
                            a = h % 2
                            me, other = (slice(0, HD), slice(HD, P)) if a == 0 else (slice(HD, P), slice(0, HD))
                            dve.wait_ge(*bk.full(f"o{cc}_{h}", it))
                            link(dve.reciprocal(rec[me, a, :], g.bk(4 + a)[other, :]))
                            dve.tensor_tensor(oT[me, h // 2, :], g.bk(4 + a)[me, :], rec[me, a, :], ALU.mult).then_inc(bk.release(f"o{cc}_{h}"), 1)
                        for j in range(TC):
                            name = f"y{cc}_{j}"
                            dve.wait_ge(*bk.full(name, it))
                            xt = g.x[:, ds(b * NK + cc * TC + j, 1), :].rearrange("p a b -> p (a b)")
                            dve.tensor_tensor(xt, xt, g.bk(bk.bank[name])[:, 0:D], ALU.add).then_inc(bk.release(name), 1)
                    link.close()
        bk.end(B * 2)
        ones.end()
        for e in (w_in, wo_in, batch, nm_made, *row_in, pv, mstep, step, half_out):
            e.end(B * 2)


def stage_l0_ffn(g, w1, s1, w2, s2, h1, hs1, h2, hs2, w3, s3):
    nc = g.nc
    H = 1024
    HB = H // P
    ln_block(g)
    with ExitStack() as ctx:
        sb = lambda n, s: g.sb(ctx, n, s)
        w1s, w2s = sb("w1s", [P, KD, H]), sb("w2s", [P, KD, H])
        h1s, h2s, w3s = sb("h1s", [P, HB, H]), sb("h2s", [P, HB, H]), sb("w3s", [P, HB, D])
        c1, c2, c3, c4, r3 = sb("c1", [P, HB]), sb("c2", [P, HB]), sb("c3", [P, HB]), sb("c4", [P, HB]), sb("r3", [P, D])
        z4, zT = sb("z4", [P, TC, D]), sb("zT", [P, KD, CH])
        ga, gb = sb("ga", [P, HB, CH]), sb("gb", [P, HB, CH])
        ys = sb("ys", [P, TC, D])
        bk = Banks(g, [("t0", 0), ("t1", 1)]
                   + [(f"{n}{f}", 2 + (f % 3) * 2 + i) for f in range(HB) for i, n in enumerate("ab")]
                   + [(f"c{f}", f) for f in range(HB)] + [(f"d{f}", f) for f in range(HB)]
                   + [(f"y{j}", j) for j in range(TC)])
        loads = [(c1, s1), (c2, s2), (c3, hs1), (c4, hs2), (r3, s3), (w1s, rows(w1)), (w2s, rows(w2)),
                 (h1s, rows(h1)), (h2s, rows(h2)), (w3s, rows(w3))]
        w_in = g.ev("w_loaded", 16 * 7)
        h1_in, h2_in = g.ev("h1_loaded", 16), g.ev("h2_loaded", 32)
        z_made, x_added = g.ev("z_made", 1), g.ev("x_added", TC)
        with nc.Block() as block:
            @block.sync
            def _(sp):
                for dst, src in loads[:7]:
                    load(sp, dst[:], src, w_in)
                load(sp, h1s[:], rows(h1), h1_in)
                load(sp, h2s[:], rows(h2), h2_in)
                load(sp, w3s[:], rows(w3), h2_in)

            @block.gpsimd
            def _(pool):
                with pool.Fori(0, NC) as c:
                    for j in range(TC):
                        xt = g.x[:, ds(c * TC + j, 1), :]
                        pool.wait_ge(*bk.read(f"y{j}", c))
                        pool.tensor_tensor(xt, xt, ys[:, j:j + 1, :], ALU.add).then_inc(x_added.sem, 1)

            @block.tensor
            def _(pe):
                pe.wait_ge(*w_in.at(0, 112))
                pe.wait_ge(*h1_in.at(0, 16))
                pe.wait_ge(*h2_in.at(0, 32))
                with pe.Fori(0, NC) as c:
                    pe.wait_ge(*z_made.at(c, 1))
                    turn(g, pe, bk, c, ("t0", "t1"), z4)
                    pe.wait_ge(*bk.read("t0", c))
                    pe.wait_ge(*bk.read("t1", c))
                    for f in range(HB):
                        for n, w in (("a", w1s), ("b", w2s)):
                            name = f"{n}{f}"
                            pe.wait_ge(*bk.free(name, c))
                            for k in range(KD):
                                ins = pe.matmul(g.bk(bk.bank[name]), w[:, k, f * P:(f + 1) * P], zT[:, k, :],
                                                start=k == 0, stop=k == KD - 1)
                            ins.then_inc(bk.fill(name), 1)
                    for n, w, src, made in (("c", h1s, ga, "b"), ("d", h2s, gb, "c")):
                        for f in range(HB):
                            name = f"{n}{f}"
                            pe.wait_ge(*bk.free(name, c))
                            for k in range(HB):
                                if f == 0:
                                    pe.wait_ge(*bk.read(f"{made}{k}", c))
                                ins = pe.matmul(g.bk(f), w[:, k, f * P:(f + 1) * P], src[:, k, :],
                                                start=k == 0, stop=k == HB - 1)
                            ins.then_inc(bk.fill(name), 1)
                    for j in range(TC):
                        pe.wait_ge(*bk.free(f"y{j}", c))
                        for k in range(HB):
                            if j == 0:
                                pe.wait_ge(*bk.read(f"d{k}", c))
                            ins = pe.matmul(g.bk(j)[:, 0:D], ga[:, k, j * P:(j + 1) * P], w3s[:, k, :],
                                            start=k == 0, stop=k == HB - 1)
                        ins.then_inc(bk.fill(f"y{j}"), 1)

            @block.scalar
            def _(act):
                act.wait_ge(*w_in.at(0, 112))
                with act.Fori(0, NC) as c:
                    act.wait_ge(*bk.full("t0", c))
                    act.activation(zT[:, 0, :], g.bk(0), ACT.Copy).then_inc(bk.release("t0"), 1)
                    for f in range(HB):
                        act.wait_ge(*bk.full(f"a{f}", c))
                        act.activation(ga[:, f, :], g.bk(bk.bank[f"a{f}"]), ACT.Silu, scale=c1[:, f:f + 1])\
                            .then_inc(bk.release(f"a{f}"), 1)
                    for n, dst, sc in (("c", gb, c3), ("d", ga, c4)):
                        for f in range(HB):
                            act.wait_ge(*bk.full(f"{n}{f}", c))
                            if n == "d" and f == 0:
                                act.wait_ge(*bk.full("c7", c))
                            act.activation(dst[:, f, :], g.bk(f), ACT.Gelu, scale=sc[:, f:f + 1])\
                                .then_inc(bk.release(f"{n}{f}"), 1)

            @block.vector
            def _(dve):
                dve.wait_ge(*w_in.at(0, 112))
                with dve.Fori(0, NC) as c:
                    normalise(g, dve, c, z4).then_inc(z_made.sem, 1)
                    dve.wait_ge(*bk.full("t1", c))
                    dve.tensor_scalar(zT[:, 1, :], g.bk(1), 1.0, None, ALU.mult).then_inc(bk.release("t1"), 1)
                    for f in range(HB):
                        dve.wait_ge(*bk.full(f"b{f}", c))
                        dve.wait_ge(*bk.read(f"a{f}", c))
                        dve.scalar_tensor_tensor(ga[:, f, :], g.bk(bk.bank[f"b{f}"]), c2[:, f:f + 1], ga[:, f, :],
                                                 ALU.mult, ALU.mult).then_inc(bk.release(f"b{f}"), 1)
                    dve.wait_ge(*x_added.at(c, 0))
                    for j in range(TC):
                        dve.wait_ge(*bk.full(f"y{j}", c))
                        dve.tensor_tensor(ys[:, j, :], g.bk(j)[:, 0:D], r3[:], ALU.mult)\
                            .then_inc(bk.release(f"y{j}"), 1)
        bk.end(NC)
        for e in (w_in, h1_in, h2_in):
            e.end()
        for e in (z_made, x_added):
            e.end(NC)


def chunk_to_features(g, bk, z_made, zT, z4=None):
    pass


def stage_l1_attn(g, w_qkv, w_out, alpha, beta, headsum):
    nc = g.nc
    ln_block(g)
    with ExitStack() as ctx:
        sb = lambda n, s: g.sb(ctx, n, s)
        wq, wo, hs = sb("wq", [P, KD, 3 * D]), sb("wo", [P, 2 * KD, D]), sb("hs", [P, P])
        decay = sb("decay", [P, 2, KD])
        z4, zT = sb("z4", [P, TC, D]), sb("zT", [P, KD, CH])
        q, k_, kv = sb("q", [P, KD, CH]), sb("k_", [P, KD, CH]), sb("kv", [P, KD, CH])
        run_k, run_kv = sb("run_k", [P, 2 * KD, CH]), sb("run_kv", [P, 2 * KD, CH])
        carry_k, carry_kv = sb("carry_k", [P, 2 * KD]), sb("carry_kv", [P, 2 * KD])
        qk, rec, yT = sb("qk", [P, 2 * KD, CH]), sb("rec", [P, 2 * KD, CH]), sb("yT", [P, 2 * KD, CH])
        bk = Banks(g, [("t0", 0), ("t1", 1), ("k0", 2), ("v0", 3), ("k1", 4), ("v1", 5), ("q0", 6), ("q1", 7)]
                   + [(f"d{i}", i) for i in range(4)] + [(f"y{j}", 4 + j) for j in range(TC)])
        w_in, decay_made = g.ev("w_loaded", 16 * 5), g.ev("decay_made", 1)
        ready = g.ev("decay_sigmoid", 1)
        z_made, exp_made = g.ev("z_made", 1), g.ev("exp_made", 4)
        qk_made, num_made, y_made, qready = g.ev("qk_made", 4), g.ev("num_made", 4), g.ev("y_made", 4), g.ev("scan_made", 4)
        step = g.ev("dve_step", 4 + 4 + 2 + 4)
        with nc.Block() as block:
            @block.sync
            def _(sp):
                load(sp, decay[:, 0, :], alpha, w_in)
                load(sp, decay[:, 1, :], beta, w_in)
                load(sp, hs[:], headsum, w_in)
                load(sp, wq[:], rows(w_qkv), w_in)
                load(sp, wo[:], rows(w_out), w_in)

            @block.tensor
            def _(pe):
                pe.wait_ge(*w_in.at(0, 80))
                with pe.Fori(0, NC) as c:
                    pe.wait_ge(*z_made.at(c, 1))
                    turn(g, pe, bk, c, ("t0", "t1"), z4)
                    pe.wait_ge(*bk.read("t0", c))
                    pe.wait_ge(*bk.read("t1", c))
                    for name in ("k0", "v0", "k1", "v1", "q0", "q1"):
                        o = {"q": 0, "k": D, "v": 2 * D}[name[0]] + int(name[1]) * P
                        pe.wait_ge(*bk.free(name, c))
                        for k in range(KD):
                            ins = pe.matmul(g.bk(bk.bank[name]), wq[:, k, o:o + P], zT[:, k, :], start=k == 0, stop=k == KD - 1)
                        ins.then_inc(bk.fill(name), 1)
                    for i in range(4):
                        pe.wait_ge(*qk_made.at(c, i + 1))
                        pe.wait_ge(*bk.free(f"d{i}", c))
                        pe.matmul(g.bk(i), hs[:], qk[:, i, :], start=True, stop=True).then_inc(bk.fill(f"d{i}"), 1)
                    pe.wait_ge(*y_made.at(c, 4))
                    for j in range(TC):
                        pe.wait_ge(*bk.free(f"y{j}", c))
                        for f in range(2 * KD):
                            ins = pe.matmul(g.bk(4 + j)[:, 0:D], yT[:, f, j * P:(j + 1) * P], wo[:, f, :],
                                            start=f == 0, stop=f == 2 * KD - 1)
                        ins.then_inc(bk.fill(f"y{j}"), 1)

            @block.scalar
            def _(act):
                act.wait_ge(*w_in.at(0, 80))
                act.activation(decay[:], decay[:], ACT.Sigmoid).then_inc(ready.sem, 1)
                with act.Fori(0, NC) as c:
                    act.wait_ge(*bk.full("t0", c))
                    act.activation(zT[:, 0, :], g.bk(0), ACT.Copy).then_inc(bk.release("t0"), 1)
                    for i, (name, dst) in enumerate((("k0", k_[:, 0, :]), ("k1", k_[:, 1, :]), ("q0", q[:, 0, :]), ("q1", q[:, 1, :]))):
                        act.wait_ge(*bk.full(name, c))
                        act.activation(dst, g.bk(bk.bank[name]), ACT.Exp).then_inc(exp_made.sem, 1)

            @block.gpsimd
            def _(pool):
                with pool.Fori(0, NC) as c:
                    for i in range(4):
                        pool.wait_ge(*qready.at(c, i + 1))
                        pool.tensor_tensor(yT[:, i, :], q[:, i % KD, :], run_kv[:, i, :], ALU.mult).then_inc(num_made.sem, 1)

            @block.vector
            def _(dve):
                dve.wait_ge(*ready.at(0, 1))
                dve.tensor_scalar(decay[:], decay[:], 1e-8, None, ALU.max).then_inc(decay_made.sem, 1)
                dve.wait_ge(*decay_made.at(0, 1))
                with dve.Fori(0, B) as b:
                    dve.memset(carry_k[:], 0.0)
                    dve.memset(carry_kv[:], 0.0)
                    with dve.Fori(0, NC // B) as hh:
                        c = b * (NC // B) + hh
                        link = Chain(dve, step, c)
                        normalise(g, dve, c, z4).then_inc(z_made.sem, 1)
                        dve.wait_ge(*bk.full("t1", c))
                        dve.tensor_scalar(zT[:, 1, :], g.bk(1), 1.0, None, ALU.mult).then_inc(bk.release("t1"), 1)
                        for i, (name, dst) in enumerate((("k0", k_[:, 0, :]), ("k1", k_[:, 1, :]), ("q0", q[:, 0, :]), ("q1", q[:, 1, :]))):
                            dve.wait_ge(*exp_made.at(c, i + 1))
                            link(dve.tensor_scalar(dst, dst, 1.0, None, ALU.min))
                            dve.scalar_tensor_tensor(dst, g.bk(bk.bank[name]), 0.0, dst, ALU.max, ALU.add)\
                                .then_inc(bk.release(name), 1)
                            dve.wait_ge(*bk.read(name, c))
                            if name[0] == "k":
                                f = int(name[1])
                                dve.wait_ge(*bk.full(f"v{f}", c))
                                dve.tensor_tensor(kv[:, f, :], dst, g.bk(bk.bank[f"v{f}"]), ALU.mult)\
                                    .then_inc(bk.release(f"v{f}"), 1)
                                dve.wait_ge(*bk.read(f"v{f}", c))
                        for i in range(4):
                            f, d = i % KD, decay[:, i // KD, i % KD:i % KD + 1].broadcast_to([P, CH])
                            dve.tensor_tensor_scan(run_kv[:, i, :], d, kv[:, f, :], carry_kv[:, i:i + 1], ALU.mult, ALU.add)\
                                .then_inc(qready.sem, 1)
                            link(dve.tensor_tensor_scan(run_k[:, i, :], d, k_[:, f, :], carry_k[:, i:i + 1], ALU.mult, ALU.add))
                            dve.tensor_tensor(qk[:, i, :], q[:, f, :], run_k[:, i, :], ALU.mult).then_inc(qk_made.sem, 1)
                        dve.wait_ge(*qready.at(c, 4))
                        link(dve.tensor_scalar(carry_k[:], run_k[:, :, CH - 1], 1.0, None, ALU.mult))
                        link(dve.tensor_scalar(carry_kv[:], run_kv[:, :, CH - 1], 1.0, None, ALU.mult))
                        for i in range(4):
                            dve.wait_ge(*bk.full(f"d{i}", c))
                            dve.tensor_scalar(rec[:, i, :], g.bk(i), 1e-6, None, ALU.max).then_inc(bk.release(f"d{i}"), 1)
                            dve.wait_ge(*bk.read(f"d{i}", c))
                            link(dve.reciprocal(rec[:, i, :], rec[:, i, :]))
                            dve.wait_ge(*num_made.at(c, i + 1))
                            dve.tensor_tensor(yT[:, i, :], yT[:, i, :], rec[:, i, :], ALU.mult).then_inc(y_made.sem, 1)
                        for j in range(TC):
                            dve.wait_ge(*bk.full(f"y{j}", c))
                            xt = g.x[:, ds(c * TC + j, 1), :].rearrange("p a b -> p (a b)")
                            dve.tensor_tensor(xt, xt, g.bk(4 + j)[:, 0:D], ALU.add).then_inc(bk.release(f"y{j}"), 1)
                        link.close()
        bk.end(NC)
        for e in (w_in, decay_made, ready):
            e.end()
        for e in (z_made, exp_made, qk_made, num_made, y_made, qready, step):
            e.end(NC)


def stage_ctx_attn(g, kind, ctxT, Wq, Wk, Wv, bq, bk_, bv, Wo, bo, sgn=None, sgn_row=None, mask=None):
    nc = g.nc
    G, W, NL = 4, 512, B * L2
    scale = {"exp": 1.0 / 16, "mask": 1.0 / 16, "plain": 1.0 / 4}[kind]
    ln_block(g)
    with ExitStack() as ctx:
        sb = lambda n, s, dt=F32: g.sb(ctx, n, s, dt)
        wq, wk, wv, wo = sb("wq", [P, KD, W]), sb("wk", [P, KD, W]), sb("wv", [P, KD, W]), sb("wo", [P, G, D])
        cq, ck, rv, ro = sb("cq", [P, G]), sb("ck", [P, G]), sb("rv", [P, W]), sb("ro", [P, D])
        cT = sb("cT", [P, KD, NL])
        kT, v = sb("kT", [P, G, NL]), sb("v", [L2, B, W])
        kb, vb = sb("kb", [P, G, L2]), sb("vb", [L2, W])
        z4, zT, qT = sb("z4", [P, TC, D]), sb("zT", [P, KD, CH]), sb("qT", [P, G, CH])
        e = sb("e", [P, 2, G, G, L2])
        mx2, sm2 = sb("mx2", [P, 2, G, G]), sb("sm2", [P, 2, G, G])
        pT, oT = sb("pT", [L2, G, G, CH]), sb("oT", [P, G, CH])
        loads = [(cq, bq), (ck, bk_), (rv, bv), (ro, bo), (cT, rows(ctxT)), (wk, rows(Wk)), (wv, rows(Wv)), (wq, rows(Wq)), (wo, rows(Wo))]
        if kind == "exp":
            sg, sr = sb("sg", [P, 1]), sb("sr", [P, W])
            loads += [(sg, sgn), (sr, sgn_row)]
        if kind == "mask":
            mi, mf, ma = sb("mi", [P, NT, L2], mybir.dt.int32), sb("mf", [P, NT, L2]), sb("ma", [P, NT, L2])
            loads += [(mi, mask.rearrange("b o (t p) l -> p (b o t) l", p=P))]
        nload = 16 * len(loads)
        NB = NC // B

        bk = Banks(g, [(f"k{f}", f) for f in range(G)] + [(f"v{b}", 4 + b) for b in range(B)])
        w_in, v_step, prepared = g.ev("w_loaded", nload), g.ev("dve_step", 2 * B if kind == "exp" else 0), g.ev("mask_made", 1)
        with nc.Block() as block:
            @block.sync
            def _(sp):
                for dst, src in loads:
                    load(sp, dst[:], src, w_in)

            @block.tensor
            def _(pe):
                pe.wait_ge(*w_in.at(0, nload))
                for f in range(G):
                    pe.wait_ge(*bk.free(f"k{f}", 0))
                    for k in range(KD):
                        ins = pe.matmul(g.bk(f)[:, 0:NL], wk[:, k, f * P:(f + 1) * P], cT[:, k, :], start=k == 0, stop=k == KD - 1)
                    ins.then_inc(bk.fill(f"k{f}"), 1)
                for b in range(B):
                    pe.wait_ge(*bk.free(f"v{b}", 0))
                    for k in range(KD):
                        ins = pe.matmul(g.bk(4 + b)[0:L2, :], cT[:, k, b * L2:(b + 1) * L2], wv[:, k, :], start=k == 0, stop=k == KD - 1)
                    ins.then_inc(bk.fill(f"v{b}"), 1)

            @block.scalar
            def _(act):
                act.wait_ge(*w_in.at(0, nload))
                if kind == "exp":
                    act.wait_ge(*prepared.at(0, 1))
                for f in range(G):
                    act.wait_ge(*bk.full(f"k{f}", 0))
                    act.activation(kT[:, f, :], g.bk(f)[:, 0:NL], ACT.Exp if kind == "exp" else ACT.Identity,
                                   scale=sg[:, 0:1] if kind == "exp" else 1.0, bias=ck[:, f:f + 1]).then_inc(bk.release(f"k{f}"), 1)
                if kind == "exp":
                    for b in range(B):
                        act.wait_ge(*v_step.at(0, b + 1))
                        act.activation(v[:, b, :], v[:, b, :], ACT.Exp)

            @block.vector
            def _(dve):
                dve.wait_ge(*w_in.at(0, nload))
                if kind == "exp":
                    dve.tensor_scalar(cq[:], cq[:], sg[:, 0:1], None, ALU.mult)
                    dve.tensor_scalar(ck[:], ck[:], sg[:, 0:1], None, ALU.mult).then_inc(prepared.sem, 1)
                for b in range(B):
                    dve.wait_ge(*bk.full(f"v{b}", 0))
                    dve.tensor_tensor(v[:, b, :], g.bk(4 + b)[0:L2, :], rv[0:L2, :], ALU.add).then_inc(bk.release(f"v{b}"), 1)
                    dve.wait_ge(*bk.read(f"v{b}", 0))
                    if kind == "exp":
                        dve.tensor_tensor(v[:, b, :], v[:, b, :], sr[0:L2, :], ALU.mult).then_inc(v_step.sem, 1)
                if kind == "mask":
                    dve.tensor_scalar(mf[:], mi[:], 0.0, None, ALU.not_equal).then_inc(prepared.sem, 1)
                    dve.wait_ge(*prepared.at(0, 1))
                    dve.tensor_scalar(ma[:], mf[:], 1.0, 1e20, ALU.subtract, ALU.mult)
        if kind == "plain":
            prepared.begin(0)
        v_step.begin(B if kind == "exp" else 0)
        bk.end()
        for ev in (w_in, v_step, prepared):
            ev.end()

        fills = [("t0", 4), ("t1", 5)] + [(f"q{f}", [6, 7, 4, 5][f]) for f in range(G)]
        order = [("s", 0)]
        for j in range(TC):
            if j + 1 < TC:
                order.append(("s", j + 1))
            order.append(("p", j))
        for n, j in order:
            fills += [(f"{n}{j}_{h}", h + (4 if n == "p" else 0)) for h in range(G)]
        fills += [(f"o{f}", f) for f in range(G)] + [(f"y{j}", 4 + j) for j in range(TC)]
        bk = Banks(g, fills)
        z_made, kv_ready, y_added = g.ev("z_made", 1), g.ev("kv_ready", 2), g.ev("x_added", 1)
        e_made, exp_made, p_made = g.ev("e_made", TC), g.ev("exp_made", TC), g.ev("p_made", TC)
        step = g.ev("dve_step", TC * (4 if kind == "mask" else 3))
        with nc.Block() as block:
            @block.gpsimd
            def _(pool):
                with pool.Fori(0, B) as b:
                    bl = ds(b * L2, L2)
                    pool.wait_ge(g.bank_full[7], g.fills[7] + b * (NB * bk.per[7]))
                    pool.tensor_copy(kb[:], kT[:, :, bl]).then_inc(kv_ready.sem, 1)
                    pool.tensor_copy(vb[:], v[:, ds(b, 1), :].rearrange("p a b -> p (a b)")).then_inc(kv_ready.sem, 1)
                    with pool.Fori(0, NB) as hh:
                        c = b * NB + hh
                        pool.wait_ge(*z_made.at(c, 1))
                        x4 = g.x[:, ds(c * TC, TC), :]
                        pool.tensor_tensor(x4, x4, ro[:].unsqueeze(1).broadcast_to([P, TC, D]), ALU.add).then_inc(y_added.sem, 1)

            @block.tensor
            def _(pe):
                def scores(c, j):
                    for h in range(G):
                        pe.wait_ge(*bk.free(f"s{j}_{h}", c))
                    for f in range(G):
                        for h in range(G):
                            r = slice(32 * h, 32 * h + 32)
                            ins = pe.matmul(g.bk(h)[:, f * L2:(f + 1) * L2], qT[r, f, j * P:(j + 1) * P], kb[r, f, :],
                                            start=True, stop=True)
                            if f == G - 1:
                                ins.then_inc(bk.fill(f"s{j}_{h}"), 1)

                with pe.Fori(0, B) as b, pe.Fori(0, NB) as hh:
                    c = b * NB + hh
                    pe.wait_ge(*z_made.at(c, 1))
                    turn(g, pe, bk, c, ("t0", "t1"), z4)
                    pe.wait_ge(*bk.read("t0", c))
                    pe.wait_ge(*bk.read("t1", c))
                    for f in range(G):
                        b_ = bk.bank[f"q{f}"]
                        pe.wait_ge(*bk.free(f"q{f}", c))
                        for k in range(KD):
                            ins = pe.matmul(g.bk(b_), wq[:, k, f * P:(f + 1) * P], zT[:, k, :], start=k == 0, stop=k == KD - 1)
                        ins.then_inc(bk.fill(f"q{f}"), 1)
                    for f in range(G):
                        pe.wait_ge(*bk.read(f"q{f}", c))
                    pe.wait_ge(*kv_ready.at(b, 2))
                    scores(c, 0)
                    for j in range(TC):
                        if j + 1 < TC:
                            scores(c, j + 1)
                        pe.wait_ge(*p_made.at(c, j + 1))
                        for h in range(G):
                            pe.wait_ge(*bk.free(f"p{j}_{h}", c))
                            for f in range(G):
                                ins = pe.transpose(g.bk(4 + h)[0:L2, f * P:(f + 1) * P], e[:, j % 2, h, f, :], g.ident[:])
                            ins.then_inc(bk.fill(f"p{j}_{h}"), 1)
                    for f in range(G):
                        if f == 0:
                            for h in range(G):
                                pe.wait_ge(*bk.read(f"p{TC - 1}_{h}", c))
                        pe.wait_ge(*bk.free(f"o{f}", c))
                        for h in range(G):
                            ins = pe.matmul(g.bk(f)[32 * h:32 * h + 32, :], vb[:, (f * G + h) * 32:(f * G + h + 1) * 32], pT[:, h, f, :],
                                            start=True, stop=True)
                        ins.then_inc(bk.fill(f"o{f}"), 1)
                    for j in range(TC):
                        pe.wait_ge(*bk.free(f"y{j}", c))
                        for f in range(G):
                            if j == 0:
                                pe.wait_ge(*bk.read(f"o{f}", c))
                            ins = pe.matmul(g.bk(4 + j)[:, 0:D], oT[:, f, j * P:(j + 1) * P], wo[:, f, :], start=f == 0, stop=f == G - 1)
                        ins.then_inc(bk.fill(f"y{j}"), 1)

            @block.scalar
            def _(act):
                def probs_out(act, c, j):
                    for h in range(G):
                        act.wait_ge(*bk.full(f"p{j}_{h}", c))
                        act.activation(pT[:, h, :, j * P:(j + 1) * P], g.bk(4 + h)[0:L2, :].rearrange("p (f q) -> p f q", q=P),
                                       ACT.Copy).then_inc(bk.release(f"p{j}_{h}"), 1)

                with act.Fori(0, NC) as c:
                    act.wait_ge(*bk.full("t0", c))
                    act.activation(zT[:, 0, :], g.bk(4), ACT.Copy).then_inc(bk.release("t0"), 1)
                    for f in range(G):
                        act.wait_ge(*bk.full(f"q{f}", c))
                        act.activation(qT[:, f, :], g.bk(bk.bank[f"q{f}"]), ACT.Exp if kind == "exp" else ACT.Identity,
                                       scale=sg[:, 0:1] if kind == "exp" else 1.0, bias=cq[:, f:f + 1]).then_inc(bk.release(f"q{f}"), 1)
                    for j in range(TC):
                        act.wait_ge(*e_made.at(c, j + 1))
                        act.activation(e[:, j % 2], e[:, j % 2], ACT.Exp, scale=scale).then_inc(exp_made.sem, 1)
                        if j:
                            probs_out(act, c, j - 1)
                    probs_out(act, c, TC - 1)
                    for f in (0, 2):
                        act.wait_ge(*bk.full(f"o{f}", c))
                        act.activation(oT[:, f, :], g.bk(f), ACT.Copy).then_inc(bk.release(f"o{f}"), 1)

            @block.vector
            def _(dve):
                def shifted(c, j, link):
                    for h in range(G):
                        dve.wait_ge(*bk.full(f"s{j}_{h}", c))
                    mx = mx2[:, j % 2]
                    s = g.ps[:, 0:G, 0:G * L2].rearrange("p h (f l) -> p h f l", l=L2)
                    ej = e[:, j % 2]
                    if kind == "mask":
                        t = ds(c * TC + j, 1)
                        m = lambda a: a[:, t, :].unsqueeze(1).broadcast_to([P, G, G, L2])
                        for h in range(G):
                            dve.tensor_tensor(ej[:, h], s[:, h], mf[:, t, :].broadcast_to([P, G, L2]), ALU.mult)\
                                .then_inc(bk.release(f"s{j}_{h}"), 1)
                        for h in range(G):
                            dve.wait_ge(*bk.read(f"s{j}_{h}", c))
                            ins = dve.tensor_tensor(ej[:, h], ej[:, h], ma[:, t, :].broadcast_to([P, G, L2]), ALU.add)
                        link(ins)
                        link(dve.tensor_reduce(mx, ej, AXX, ALU.max))
                        for h in range(G):
                            ins = dve.tensor_tensor(ej[:, h], ej[:, h], mx[:, h].unsqueeze(2).broadcast_to([P, G, L2]), ALU.subtract)
                        ins.then_inc(e_made.sem, 1)
                    else:
                        link(dve.tensor_reduce(mx, s, AXX, ALU.max))
                        for h in range(G):
                            dve.tensor_tensor(ej[:, h], s[:, h], mx[:, h].unsqueeze(2).broadcast_to([P, G, L2]), ALU.subtract)\
                                .then_inc(bk.release(f"s{j}_{h}"), 1)
                        for h in range(G):
                            dve.wait_ge(*bk.read(f"s{j}_{h}", c))
                        dve.sem_inc(e_made.sem, 1)

                def softened(c, j, link):
                    dve.wait_ge(*exp_made.at(c, j + 1))
                    sm = sm2[:, j % 2]
                    ej = e[:, j % 2]
                    link(dve.tensor_reduce(sm, ej, AXX, ALU.add))
                    link(dve.reciprocal(sm, sm))
                    for h in range(G):
                        ins = dve.tensor_tensor(ej[:, h], ej[:, h], sm[:, h].unsqueeze(2).broadcast_to([P, G, L2]), ALU.mult)
                    ins.then_inc(p_made.sem, 1)

                with dve.Fori(0, NC) as c:
                    link = Chain(dve, step, c)
                    normalise(g, dve, c, z4).then_inc(z_made.sem, 1)
                    dve.wait_ge(*bk.full("t1", c))
                    dve.tensor_scalar(zT[:, 1, :], g.bk(5), 1.0, None, ALU.mult).then_inc(bk.release("t1"), 1)
                    for j in range(TC):
                        if j >= 2:
                            for h in range(G):
                                dve.wait_ge(*bk.full(f"p{j - 2}_{h}", c))
                        shifted(c, j, link)
                        if j:
                            softened(c, j - 1, link)
                    softened(c, TC - 1, link)
                    for f in (1, 3):
                        dve.wait_ge(*bk.full(f"o{f}", c))
                        dve.tensor_scalar(oT[:, f, :], g.bk(f), 1.0, None, ALU.mult).then_inc(bk.release(f"o{f}"), 1)
                    dve.wait_ge(*y_added.at(c, 1))
                    for j in range(TC):
                        dve.wait_ge(*bk.full(f"y{j}", c))
                        xt = g.x[:, ds(c * TC + j, 1), :].rearrange("p a b -> p (a b)")
                        dve.tensor_tensor(xt, xt, g.bk(4 + j)[:, 0:D], ALU.add).then_inc(bk.release(f"y{j}"), 1)
                    link.close()
        bk.end(NC)
        kv_ready.end(B)
        for ev in (z_made, y_added, e_made, exp_made, p_made, step):
            ev.end(NC)


E8 = 8


def moe_prologue(g, zT_all, wd, gamma, beta, rw):
    nc = g.nc
    twice_normalised(g, add=True)
    with ExitStack() as ctx:
        sb = lambda n, s: g.sb(ctx, n, s)
        gm, bt, rws = sb("gm", [P, KD]), sb("bt_", [P, KD]), sb("rws", [P, KD, E8])
        z4, zT = sb("z4", [P, TC, D]), sb("zT", [P, KD, CH])
        lg, pr, mx, sm = sb("lg", [P, NT, E8]), sb("pr", [P, NT, E8]), sb("mx", [P, NT]), sb("sm", [P, NT])
        rank, cmp_ = sb("rank", [P, NT, E8]), sb("cmp_", [P, NT, E8])
        bk = Banks(g, [("t0", 0), ("t1", 1), ("lg", 2)])
        w_in, z_made, copied = g.ev("w_loaded", 16 * 3), g.ev("z_made", 1), g.ev("zT_copied", 1)
        with nc.Block() as block:
            @block.sync
            def _(sp):
                load(sp, gm[:], gamma, w_in)
                load(sp, bt[:], beta, w_in)
                load(sp, rws[:], rows(rw), w_in)

            @block.vector
            def _(dve):
                with dve.Fori(0, NC) as c:
                    for j in range(TC):
                        t = ds(c * TC + j, 1)
                        ins = dve.tensor_scalar(z4[:, j, :], g.z[:, t, :].rearrange("p a b -> p (a b)"),
                                                g.mean[:, t], g.rstd[:, t], ALU.subtract, ALU.mult)
                    ins.then_inc(z_made.sem, 1)
                    dve.wait_ge(*bk.full("lg", c))
                    dve.tensor_scalar(lg[:, ds(c * TC, TC), :], g.bk(2)[:, 0:TC * E8].rearrange("p (t e) -> p t e", e=E8),
                                      1.0 / 1.5, None, ALU.mult).then_inc(bk.release("lg"), 1)

            @block.scalar
            def _(act):
                act.wait_ge(*w_in.at(0, 48))
                with act.Fori(0, NC) as c:
                    act.wait_ge(*copied.at(c, 0))
                    for k in range(KD):
                        act.wait_ge(*bk.full(f"t{k}", c))
                        act.activation(zT[:, k, :], g.bk(k), ACT.Identity, scale=gm[:, k:k + 1], bias=bt[:, k:k + 1])\
                            .then_inc(bk.release(f"t{k}"), 1)

            @block.gpsimd
            def _(pool):
                with pool.Fori(0, NC) as c:
                    pool.wait_ge(*bk.read("t0", c))
                    pool.wait_ge(*bk.read("t1", c))
                    pool.tensor_copy(zT_all[:, :, ds(c * CH, CH)], zT[:]).then_inc(copied.sem, 1)

            @block.tensor
            def _(pe):
                pe.wait_ge(*w_in.at(0, 48))
                with pe.Fori(0, NC) as c:
                    pe.wait_ge(*z_made.at(c, 1))
                    turn(g, pe, bk, c, ("t0", "t1"), z4)
                    pe.wait_ge(*bk.read("t0", c))
                    pe.wait_ge(*bk.read("t1", c))
                    pe.wait_ge(*bk.free("lg", c))
                    for j in range(TC):
                        for k in range(KD):
                            ins = pe.matmul(g.bk(2)[:, j * E8:(j + 1) * E8], zT[:, k, j * P:(j + 1) * P], rws[:, k, :],
                                            start=k == 0, stop=k == KD - 1)
                    ins.then_inc(bk.fill("lg"), 1)
        bk.end(NC)
        w_in.end()
        for e in (z_made, copied):
            e.end(NC)

        expd = g.ev("router_exp", 1)
        step = g.ev("dve_step", 7 + 2 * E8)
        wide = lambda a: a.unsqueeze(2).broadcast_to([P, NT, E8])
        with nc.Block() as block:
            @block.scalar
            def _(act):
                act.wait_ge(*step.at(0, 2))
                act.activation(pr[:], lg[:], ACT.Exp).then_inc(expd.sem, 1)

            @block.vector
            def _(dve):
                link = Chain(dve, step, 0)
                link(dve.tensor_reduce(mx[:], lg[:], AXX, ALU.max))
                link(dve.tensor_tensor(lg[:], lg[:], wide(mx[:]), ALU.subtract))
                dve.wait_ge(*expd.at(0, 1))
                link(dve.tensor_reduce(sm[:], pr[:], AXX, ALU.add))
                link(dve.reciprocal(sm[:], sm[:]))
                link(dve.tensor_tensor(pr[:], pr[:], wide(sm[:]), ALU.mult))
                link(dve.memset(rank[:], 0.0))
                for j in range(E8):
                    pj = pr[:, :, j:j + 1]
                    if j < E8 - 1:
                        dve.tensor_tensor(cmp_[:, :, j + 1:], pj.broadcast_to([P, NT, E8 - 1 - j]), pr[:, :, j + 1:], ALU.is_ge)
                    link(dve.tensor_tensor(cmp_[:, :, 0:j + 1], pj.broadcast_to([P, NT, j + 1]), pr[:, :, 0:j + 1], ALU.is_gt))
                    link(dve.tensor_tensor(rank[:], rank[:], cmp_[:], ALU.add))
                link(dve.tensor_scalar(cmp_[:], rank[:], 1.5, None, ALU.is_lt))
                dve.tensor_tensor(wd[:], pr[:], cmp_[:], ALU.mult)
                link.close()
        for e in (expd, step):
            e.end()


def stage_l1_ffn(g, gamma, beta, rw, W1, W2):
    nc = g.nc
    H = 1024
    HB = H // P
    with ExitStack() as ctx:
        sb = lambda n, s: g.sb(ctx, n, s)
        w1s = [sb(f"w1s{i}", [P, KD, H]) for i in range(2)]
        w2s = [sb(f"w2s{i}", [P, HB, D]) for i in range(2)]
        zT_all, wd = sb("zT_all", [P, KD, B * S]), sb("wd", [P, NT, E8])
        h = sb("h", [P, HB, CH])
        g.z = sb("z_all", [P, NT, D])
        moe_prologue(g, zT_all, wd, gamma, beta, rw)
        bk = Banks(g, [(f"a{f}", f) for f in range(HB)] + [(f"y{j}", j) for j in range(TC)])
        w_in = [g.ev("expert_even_loaded", 32), g.ev("expert_odd_loaded", 32)]
        with nc.Block() as block:
            @block.sync
            def _(sp):
                def load_expert(e, s):
                    sp.dma_start(w1s[s][:], W1[e].rearrange("(k p) n -> p k n", p=P)).then_inc(w_in[s].sem, 16)
                    sp.dma_start(w2s[s][:], W2[e].rearrange("(k p) n -> p k n", p=P)).then_inc(w_in[s].sem, 16)
                load_expert(0, 0)
                load_expert(1, 1)
                with sp.Fori(1, E8 // 2) as i:
                    for s in range(2):
                        sp.wait_ge(*bk.read("y3", (i * 2 + (s - 2)) * NC + NC - 1))
                        e = ds(i * 2 + s, 1)
                        sp.dma_start(w1s[s][:], W1[e].rearrange("a (k p) n -> p (a k) n", p=P)).then_inc(w_in[s].sem, 16)
                        sp.dma_start(w2s[s][:], W2[e].rearrange("a (k p) n -> p (a k) n", p=P)).then_inc(w_in[s].sem, 16)

            @block.tensor
            def _(pe):
                with pe.Fori(0, E8 // 2) as i:
                    for s in range(2):
                        with pe.Fori(0, NC) as c:
                            pe.wait_ge(*w_in[s].at(i, 32))
                            it = (i * 2 + s) * NC + c
                            for f in range(HB):
                                pe.wait_ge(*bk.free(f"a{f}", it))
                                for k in range(KD):
                                    ins = pe.matmul(g.bk(f), w1s[s][:, k, f * P:(f + 1) * P],
                                                    zT_all[:, k, ds(c * CH, CH)], start=k == 0, stop=k == KD - 1)
                                ins.then_inc(bk.fill(f"a{f}"), 1)
                            for j in range(TC):
                                pe.wait_ge(*bk.free(f"y{j}", it))
                                for f in range(HB):
                                    if j == 0:
                                        pe.wait_ge(*bk.read(f"a{f}", it))
                                    ins = pe.matmul(g.bk(j)[:, 0:D], h[:, f, j * P:(j + 1) * P], w2s[s][:, f, :],
                                                    start=f == 0, stop=f == HB - 1)
                                ins.then_inc(bk.fill(f"y{j}"), 1)

            @block.scalar
            def _(act):
                with act.Fori(0, E8) as e:
                    with act.Fori(0, NC) as c:
                        it = e * NC + c
                        for f in range(HB):
                            act.wait_ge(*bk.full(f"a{f}", it))
                            act.activation(h[:, f, :], g.bk(f), ACT.Silu).then_inc(bk.release(f"a{f}"), 1)

            @block.vector
            def _(dve):
                with dve.Fori(0, E8) as e:
                    with dve.Fori(0, NC) as c:
                        it = e * NC + c
                        for j in range(TC):
                            t = ds(c * TC + j, 1)
                            xt = g.x[:, t, :].rearrange("p a b -> p (a b)")
                            dve.wait_ge(*bk.full(f"y{j}", it))
                            dve.scalar_tensor_tensor(xt, g.bk(j)[:, 0:D], wd[:, t, ds(e, 1)].rearrange("p a b -> p (a b)"),
                                                     xt, ALU.mult, ALU.add).then_inc(bk.release(f"y{j}"), 1)
        bk.end(E8 * NC)
        for e in w_in:
            e.end(E8 // 2)


def stage_l2_attn(g, Wq, Wk, Wv, bq, bk_, bv, Wo, bo, gamma, beta, causal, own):
    nc = g.nc
    NH, HD, VW, G = 16, 16, 17, 4
    GW = G * VW
    FE = 1e-4
    ln_block(g)
    with ExitStack() as ctx:
        sb = lambda n, s: g.sb(ctx, n, s)
        out = sb("attn_out", [P, NT, D])
        with ExitStack() as inner:
            sb = lambda n, s: g.sb(inner, n, s)
            wq, wk, wv, wo = sb("wq", [P, KD, 512]), sb("wk", [P, KD, 512]), sb("wv", [P, KD, D]), sb("wo", [P, KD, D])
            cq, ck, rv, ro = sb("cq", [P, G]), sb("ck", [P, G]), sb("rv", [P, D]), sb("ro", [P, D])
            ceq = sb("ceq", [P, 2, G])
            cau, ownm = sb("cau", [P, P]), sb("ownm", [P, G * GW])
            z4, zT = sb("z4", [P, TC, D]), sb("zT", [P, KD, CH])
            q, k_, pos = sb("q", [P, G, CH]), sb("k_", [P, G, CH]), sb("pos", [P, 2, CH])
            v1 = [sb(f"v1_{i}", [P, NH, VW]) for i in range(2)]
            ktok = sb("ktok", [P, 512])
            am = sb("am", [P, NH, P])
            st, dst_ = sb("state", [P, G * GW]), sb("state_new", [P, G * GW])
            den, o, oT = sb("den", [P, NH]), sb("o", [P, NH, HD]), sb("oT", [P, D])
            fills = [("t0", 4), ("t1", 5)] + [(f"{n}{f}", f) for n in "kq" for f in range(G)]
            for j in range(TC):
                fills += [(f"v_{j}", 4), (f"kt_{j}", 5)] + [(f"a{f}_{j}", f) for f in range(G)]
                fills += [(f"s_{j}", 7), (f"o_{j}", 6), (f"ot_{j}", 5), (f"w_{j}", 7)]
            bk = Banks(g, fills)
            w_in, ones_made = g.ev("w_loaded", 16 * 10), g.ev("ones_made", 1)
            z_made, exp_made = g.ev("z_made", 1), g.ev("exp_made", 2 * G)
            state_zero, state_made, o_made = g.ev("state_zero", 1), g.ev("state_made", TC), g.ev("o_made", TC)
            step = g.ev("dve_step", 2 * TC)
            qk_step = g.ev("qk_pos_made", 2 * G)
            NB = NC // B
            with nc.Block() as block:
                @block.sync
                def _(sp):
                    for dst, src in ((cq, bq), (ck, bk_), (rv, bv), (ro, bo), (cau, causal), (ownm, own)):
                        load(sp, dst[:], src, w_in)
                    for dst, src in ((wq, Wq), (wk, Wk), (wv, Wv), (wo, Wo)):
                        load(sp, dst[:], rows(src), w_in)

                @block.tensor
                def _(pe):
                    pe.wait_ge(*w_in.at(0, 160))
                    pe.wait_ge(*ones_made.at(0, 1))
                    with pe.Fori(0, B) as b, pe.Fori(0, NB) as hh:
                        c = b * NB + hh
                        pe.wait_ge(*z_made.at(c, 1))
                        turn(g, pe, bk, c, ("t0", "t1"), z4)
                        pe.wait_ge(*bk.read("t0", c))
                        pe.wait_ge(*bk.read("t1", c))
                        for n, w in (("k", wk), ("q", wq)):
                            for f in range(G):
                                pe.wait_ge(*bk.free(f"{n}{f}", c))
                                for k in range(KD):
                                    ins = pe.matmul(g.bk(f), w[:, k, f * P:(f + 1) * P], zT[:, k, :], start=k == 0, stop=k == KD - 1)
                                ins.then_inc(bk.fill(f"{n}{f}"), 1)
                        for j in range(TC):
                            tile = slice(j * P, (j + 1) * P)
                            pe.wait_ge(*bk.free(f"v_{j}", c))
                            for k in range(KD):
                                ins = pe.matmul(g.bk(4)[:, 0:D], zT[:, k, tile], wv[:, k, :], start=k == 0, stop=k == KD - 1)
                            ins.then_inc(bk.fill(f"v_{j}"), 1)
                            pe.wait_ge(*bk.read("k3", c))
                            pe.wait_ge(*bk.free(f"kt_{j}", c))
                            for f in range(G):
                                ins = pe.transpose(g.bk(5)[:, f * P:(f + 1) * P], k_[:, f, tile], g.ident[:])
                            ins.then_inc(bk.fill(f"kt_{j}"), 1)
                            pe.wait_ge(*bk.read("q3", c))
                            for h in range(G):
                                pe.wait_ge(*bk.free(f"a{h}_{j}", c))
                            for f in range(G):
                                for h in range(G):
                                    r = slice(32 * h, 32 * h + HD)
                                    ins = pe.matmul(g.bk(h)[:, f * P:(f + 1) * P], k_[r, f, tile], q[r, f, tile], start=True, stop=True)
                                    if f == G - 1:
                                        ins.then_inc(bk.fill(f"a{h}_{j}"), 1)
                            pe.wait_ge(*bk.read(f"v_{j}", c))
                            pe.wait_ge(*bk.read(f"kt_{j}", c))
                            pe.wait_ge(*bk.free(f"s_{j}", c))
                            for f in range(G):
                                ins = pe.matmul(g.bk(7)[:, f * GW:(f + 1) * GW], ktok[:, f * P:(f + 1) * P],
                                                v1[j % 2][:, f * G:(f + 1) * G, :].rearrange("p a b -> p (a b)"), start=True, stop=True)
                            ins.then_inc(bk.fill(f"s_{j}"), 1)
                            pe.wait_ge(*state_made.at(c, j))
                            pe.wait_ge(*state_zero.at(b, 1))
                            pe.wait_ge(*bk.free(f"o_{j}", c))
                            for f in range(G):
                                pe.matmul(g.bk(6)[:, f * GW:(f + 1) * GW], q[:, f, tile], st[:, f * GW:(f + 1) * GW],
                                          start=True, stop=False, skip_group_check=True)
                                if f == 0:
                                    for h in range(G):
                                        pe.wait_ge(*bk.read(f"a{h}_{j}", c))
                                for h in range(G):
                                    o0 = (f * G + h) * VW
                                    ins = pe.matmul(g.bk(6)[:, o0:o0 + VW], am[:, f * G + h, :], v1[j % 2][:, f * G + h, :],
                                                    start=False, stop=True, skip_group_check=True)
                            ins.then_inc(bk.fill(f"o_{j}"), 1)
                            pe.wait_ge(*o_made.at(c, j + 1))
                            pe.wait_ge(*bk.free(f"ot_{j}", c))
                            for k in range(KD):
                                ins = pe.transpose(g.bk(5)[:, k * P:(k + 1) * P],
                                                   o[:, k * 8:(k + 1) * 8, :].rearrange("p a b -> p (a b)"), g.ident[:])
                            ins.then_inc(bk.fill(f"ot_{j}"), 1)
                            pe.wait_ge(*bk.read(f"ot_{j}", c))
                            pe.wait_ge(*bk.free(f"w_{j}", c))
                            for k in range(KD):
                                ins = pe.matmul(g.bk(7)[:, 0:D], oT[:, k * P:(k + 1) * P], wo[:, k, :], start=k == 0, stop=k == KD - 1)
                            ins.then_inc(bk.fill(f"w_{j}"), 1)

                @block.scalar
                def _(act):
                    act.wait_ge(*w_in.at(0, 160))
                    with act.Fori(0, NC) as c:
                        act.wait_ge(*bk.full("t0", c))
                        act.activation(zT[:, 0, :], g.bk(4), ACT.Copy).then_inc(bk.release("t0"), 1)
                        for n, dst, bias in (("k", k_, ck), ("q", q, cq)):
                            for f in range(G):
                                act.wait_ge(*bk.full(f"{n}{f}", c))
                                act.activation(dst[:, f, :], g.bk(f), ACT.Exp, bias=bias[:, f:f + 1]).then_inc(exp_made.sem, 1)
                        for j in range(TC):
                            act.wait_ge(*bk.full(f"kt_{j}", c))
                            act.activation(ktok[:], g.bk(5), ACT.Copy).then_inc(bk.release(f"kt_{j}"), 1)
                            act.wait_ge(*bk.full(f"ot_{j}", c))
                            act.activation(oT[:], g.bk(5)[:, 0:D], ACT.Copy).then_inc(bk.release(f"ot_{j}"), 1)

                @block.gpsimd
                def _(pool):
                    with pool.Fori(0, B) as b:
                        pool.memset(st[:], 0.0).then_inc(state_zero.sem, 1)
                        with pool.Fori(0, NB) as hh:
                            c = b * NB + hh
                            for j in range(TC):
                                pool.wait_ge(*state_zero.at(b, 1))
                                pool.wait_ge(*bk.read(f"s_{j}", c))
                                pool.wait_ge(*bk.full(f"o_{j}", c))
                                pool.tensor_tensor(st[:], st[:], dst_[:], ALU.add).then_inc(state_made.sem, 1)
                                pool.wait_ge(*state_made.at(c, j + 1))

                @block.vector
                def _(dve):
                    dve.memset(v1[0][:, :, HD:VW], 1.0)
                    dve.memset(v1[1][:, :, HD:VW], 1.0)
                    dve.wait_ge(*w_in.at(0, 160))
                    dve.tensor_scalar(ceq[:, 0, :], ck[:], FE, None, ALU.add)
                    dve.tensor_scalar(ceq[:, 1, :], cq[:], FE, None, ALU.add).then_inc(ones_made.sem, 1)
                    dve.wait_ge(*ones_made.at(0, 1))
                    with dve.Fori(0, NC) as c:
                        link = Chain(dve, step, c)
                        normalise(g, dve, c, z4).then_inc(z_made.sem, 1)
                        dve.wait_ge(*bk.full("t1", c))
                        dve.tensor_scalar(zT[:, 1, :], g.bk(5), 1.0, None, ALU.mult).then_inc(bk.release("t1"), 1)
                        for i, (n, dst) in enumerate((("k", k_), ("q", q))):
                            for f in range(G):
                                dve.wait_ge(*exp_made.at(c, i * G + f + 1))
                                dve.tensor_scalar(pos[:, f % 2, :], g.bk(f), ceq[:, i, f:f + 1], FE, ALU.add, ALU.max)\
                                    .then_inc(qk_step.sem, 1)
                                dve.wait_ge(*qk_step.at(c, i * G + f + 1))
                                dve.scalar_tensor_tensor(dst[:, f, :], dst[:, f, :], 1.0, pos[:, f % 2, :], ALU.min, ALU.add)\
                                    .then_inc(bk.release(f"{n}{f}"), 1)
                                dve.wait_ge(*bk.read(f"{n}{f}", c))
                        for j in range(TC):
                            dve.wait_ge(*bk.full(f"v_{j}", c))
                            dve.tensor_tensor(v1[j % 2][:, :, 0:HD], g.bk(4)[:, 0:D].rearrange("p (h d) -> p h d", d=HD),
                                              rv[:].rearrange("p (h d) -> p h d", d=HD), ALU.add).then_inc(bk.release(f"v_{j}"), 1)
                            for f in range(G):
                                dve.wait_ge(*bk.full(f"a{f}_{j}", c))
                                dve.tensor_tensor(am[:, f::G, :], g.bk(f).rearrange("p (h q) -> p h q", q=P),
                                                  cau[:].unsqueeze(1).broadcast_to([P, G, P]), ALU.mult)\
                                    .then_inc(bk.release(f"a{f}_{j}"), 1)
                            dve.wait_ge(*bk.full(f"s_{j}", c))
                            dve.wait_ge(*state_made.at(c, j))
                            dve.tensor_tensor(dst_[:], g.bk(7)[:, 0:G * GW], ownm[:], ALU.mult).then_inc(bk.release(f"s_{j}"), 1)
                            dve.wait_ge(*bk.full(f"o_{j}", c))
                            ov = g.bk(6)[:, 0:NH * VW].rearrange("p (h e) -> p h e", e=VW)
                            link(dve.tensor_scalar(den[:], ov[:, :, HD], 4.0 * FE, None, ALU.add))
                            link(dve.reciprocal(den[:], den[:]))
                            dve.tensor_tensor(o[:], ov[:, :, 0:HD], den[:].unsqueeze(2).broadcast_to([P, NH, HD]), ALU.mult)\
                                .then_inc(bk.release(f"o_{j}"), 1)
                            dve.wait_ge(*bk.read(f"o_{j}", c))
                            dve.sem_inc(o_made.sem, 1)
                            dve.wait_ge(*bk.full(f"w_{j}", c))
                            dve.tensor_tensor(out[:, ds(c * TC + j, 1), :].rearrange("p a b -> p (a b)"), g.bk(7)[:, 0:D], ro[:], ALU.add)\
                                .then_inc(bk.release(f"w_{j}"), 1)
                        link.close()
            bk.end(NC)
            for e in (w_in, ones_made):
                e.end()
            state_zero.end(B)
            for e in (z_made, exp_made, state_made, o_made, step, qk_step):
                e.end(NC)

        sb = lambda n, s: g.sb(ctx, n, s)
        rg, rb, y = sb("rg", [P, D]), sb("rb", [P, D]), sb("y", [P, 2, D])
        g.ev_bn = g.ev("bn_stats_done", NT)
        spread, rooted, step = g.ev("ln_variance", 1), g.ev("ln_root", 1), g.ev("dve_step", LN_LINKS)
        w_in = g.ev("w_loaded", 32)
        with nc.Block() as block:
            @block.sync
            def _(sp):
                load(sp, rg[:], gamma, w_in)
                load(sp, rb[:], beta, w_in)
                sp.wait_ge(*w_in.at(0, 32))

            @block.vector
            def _(dve):
                link = Chain(dve, step, 0)
                ln_stats_vector(g, dve, out, NT, spread, rooted, link)
                link.close()

            @block.scalar
            def _(act):
                ln_stats_scalar(g, act, NT, spread, rooted)
        for e in (g.ev_bn, spread, rooted, step, w_in):
            e.end()
        normed, scaled, added = g.ev("out_normed", 1), g.ev("out_scaled", 1), g.ev("out_added", 1)
        with nc.Block() as block:
            @block.vector
            def _(dve):
                with dve.Fori(0, NT) as t:
                    tt = ds(t, 1)
                    ot = out[:, tt, :].rearrange("p a b -> p (a b)")
                    dve.tensor_scalar(ot, ot, g.mean[:, tt], g.rstd[:, tt], ALU.subtract, ALU.mult).then_inc(normed.sem, 1)
                    dve.wait_ge(*normed.at(t, 1))
                    dve.tensor_tensor(ot, ot, rg[:], ALU.mult).then_inc(scaled.sem, 1)

            @block.gpsimd
            def _(pool):
                with pool.Fori(0, NT) as t:
                    xt = g.x[:, ds(t, 1), :].rearrange("p a b -> p (a b)")
                    pool.tensor_tensor(xt, xt, rb[:], ALU.add).then_inc(added.sem, 1)
                    pool.wait_ge(*added.at(t, 1))
                    pool.wait_ge(*scaled.at(t, 1))
                    pool.tensor_tensor(xt, xt, out[:, ds(t, 1), :].rearrange("p a b -> p (a b)"), ALU.add)
        for e in (normed, scaled, added):
            e.end(NT)


def stage_l2_ffn(g, W, gu, V):
    nc = g.nc
    E, R = 8, 16
    ln_block(g)
    with ExitStack() as ctx:
        sb = lambda n, s: g.sb(ctx, n, s)
        w, gus, v = sb("w", [P, KD, D]), sb("gus", [P, KD, E + E * R]), sb("v", [P, D])
        z4, zT = sb("z4", [P, TC, D]), sb("zT", [P, KD, CH])
        t, gate, mx = sb("t", [P, TC, E * R]), sb("gate", [P, TC, E]), sb("mx", [P, TC])
        tT = sb("tT", [P, CH])
        bk = Banks(g, [("t0", 0), ("t1", 1), ("p0", 2), ("p1", 3), ("p2", 4), ("p3", 5), ("tT", 6)]
                   + [(f"y{j}", [7, 0, 1, 2][j]) for j in range(TC)])
        w_in, z_made, step = g.ev("w_loaded", 48), g.ev("z_made", 1), g.ev("dve_step", 5)
        logit, expd, t_made = g.ev("logit_made", 1), g.ev("exp_made", 1), g.ev("t_made", 1)
        with nc.Block() as block:
            @block.sync
            def _(sp):
                load(sp, gus[:], rows(gu), w_in)
                load(sp, w[:], rows(W), w_in)
                load(sp, v[:], V, w_in)

            @block.tensor
            def _(pe):
                pe.wait_ge(*w_in.at(0, 48))
                with pe.Fori(0, NC) as c:
                    pe.wait_ge(*z_made.at(c, 1))
                    turn(g, pe, bk, c, ("t0", "t1"), z4)
                    pe.wait_ge(*bk.read("t0", c))
                    pe.wait_ge(*bk.read("t1", c))
                    for j in range(TC):
                        pe.wait_ge(*bk.free(f"p{j}", c))
                        for k in range(KD):
                            ins = pe.matmul(g.bk(2 + j)[:, 0:E + E * R], zT[:, k, j * P:(j + 1) * P], gus[:, k, :],
                                            start=k == 0, stop=k == KD - 1)
                        ins.then_inc(bk.fill(f"p{j}"), 1)
                    pe.wait_ge(*t_made.at(c, 1))
                    pe.wait_ge(*bk.free("tT", c))
                    for j in range(TC):
                        ins = pe.transpose(g.bk(6)[:, j * P:(j + 1) * P], t[:, j, :], g.ident[:])
                    ins.then_inc(bk.fill("tT"), 1)
                    for j in range(TC):
                        b = bk.bank[f"y{j}"]
                        pe.wait_ge(*bk.free(f"y{j}", c))
                        for k in range(KD):
                            pe.matmul(g.bk(b)[:, 0:D], zT[:, k, j * P:(j + 1) * P], w[:, k, :], start=k == 0, stop=False)
                        pe.wait_ge(*bk.read("tT", c))
                        pe.matmul(g.bk(b)[:, 0:D], tT[:, j * P:(j + 1) * P], v[:], start=False, stop=True)\
                            .then_inc(bk.fill(f"y{j}"), 1)

            @block.scalar
            def _(act):
                with act.Fori(0, NC) as c:
                    act.wait_ge(*bk.full("t0", c))
                    act.activation(zT[:, 0, :], g.bk(0), ACT.Copy).then_inc(bk.release("t0"), 1)
                    act.wait_ge(*logit.at(c, 1))
                    act.activation(gate[:], gate[:], ACT.Exp).then_inc(expd.sem, 1)
                    act.wait_ge(*bk.full("tT", c))
                    act.activation(tT[:], g.bk(6), ACT.Copy).then_inc(bk.release("tT"), 1)

            @block.vector
            def _(dve):
                with dve.Fori(0, NC) as c:
                    link = Chain(dve, step, c)
                    normalise(g, dve, c, z4).then_inc(z_made.sem, 1)
                    dve.wait_ge(*bk.full("t1", c))
                    dve.tensor_scalar(zT[:, 1, :], g.bk(1), 1.0, None, ALU.mult).then_inc(bk.release("t1"), 1)
                    for j in range(TC):
                        dve.wait_ge(*bk.full(f"p{j}", c))
                    lg = g.ps[:, 2:6, 0:E]
                    link(dve.tensor_reduce(mx[:], lg, AXX, ALU.max))
                    dve.tensor_tensor(gate[:], lg, mx[:].unsqueeze(2).broadcast_to([P, TC, E]), ALU.subtract)\
                        .then_inc(logit.sem, 1)
                    dve.wait_ge(*expd.at(c, 1))
                    link(dve.tensor_reduce(mx[:], gate[:], AXX, ALU.add))
                    link(dve.reciprocal(mx[:], mx[:]))
                    link(dve.tensor_scalar(mx[:], mx[:], 1.0 / R, None, ALU.mult))
                    link(dve.tensor_tensor(gate[:], gate[:], mx[:].unsqueeze(2).broadcast_to([P, TC, E]), ALU.mult))
                    for j in range(TC):
                        dve.tensor_tensor(t[:, j, :].rearrange("p (e r) -> p e r", r=R),
                                          g.bk(2 + j)[:, E:E + E * R].rearrange("p (e r) -> p e r", r=R),
                                          gate[:, j, :].unsqueeze(2).broadcast_to([P, E, R]), ALU.mult)\
                            .then_inc(bk.release(f"p{j}"), 1)
                    for j in range(TC):
                        dve.wait_ge(*bk.read(f"p{j}", c))
                    dve.sem_inc(t_made.sem, 1)
                    for j in range(TC):
                        dve.wait_ge(*bk.full(f"y{j}", c))
                        xt = g.x[:, ds(c * TC + j, 1), :].rearrange("p a b -> p (a b)")
                        dve.tensor_tensor(xt, xt, g.bk(bk.bank[f"y{j}"])[:, 0:D], ALU.add).then_inc(bk.release(f"y{j}"), 1)
                    link.close()
        bk.end(NC)
        w_in.end()
        for e in (z_made, step, logit, expd, t_made):
            e.end(NC)


def stage_l3_ffn(g, W, out):
    nc = g.nc
    ln_block(g)
    with ExitStack() as ctx:
        sb = lambda n, s: g.sb(ctx, n, s)
        w, z4, zT = sb("w", [P, KD, D]), sb("z4", [P, TC, D]), sb("zT", [P, KD, CH])
        bk = Banks(g, [("t0", 0), ("t1", 1)] + [(f"y{j}", 2 + j) for j in range(TC)])
        w_in, signed, z_made, stored = g.ev("w_loaded", 16), g.ev("sign_made", 1), g.ev("z_made", 1), g.ev("out_stored", 16)
        out_t = out.rearrange("b (t p) d -> p (b t) d", p=P)
        with nc.Block() as block:
            @block.sync
            def _(sp):
                load(sp, w[:], rows(W), w_in)
                with sp.Fori(0, NC) as c:
                    sp.wait_ge(*bk.read(f"y{TC - 1}", c))
                    t = ds(c * TC, TC)
                    sp.dma_start(out_t[:, t, :], g.x[:, t, :]).then_inc(stored.sem, 16)
                sp.wait_ge(*stored.at(NC - 1, 16))

            @block.tensor
            def _(pe):
                pe.wait_ge(*signed.at(0, 1))
                with pe.Fori(0, NC) as c:
                    pe.wait_ge(*z_made.at(c, 1))
                    turn(g, pe, bk, c, ("t0", "t1"), z4)
                    pe.wait_ge(*bk.read("t0", c))
                    pe.wait_ge(*bk.read("t1", c))
                    for j in range(TC):
                        pe.wait_ge(*bk.free(f"y{j}", c))
                        for k in range(KD):
                            ins = pe.matmul(g.bk(2 + j)[:, 0:D], zT[:, k, j * P:(j + 1) * P], w[:, k, :], start=k == 0, stop=k == KD - 1)
                        ins.then_inc(bk.fill(f"y{j}"), 1)

            @block.scalar
            def _(act):
                act.wait_ge(*w_in.at(0, 16))
                act.activation(w[:], w[:], ACT.Sign).then_inc(signed.sem, 1)
                with act.Fori(0, NC) as c:
                    act.wait_ge(*bk.full("t0", c))
                    act.activation(zT[:, 0, :], g.bk(0), ACT.Copy).then_inc(bk.release("t0"), 1)

            @block.vector
            def _(dve):
                with dve.Fori(0, NC) as c:
                    normalise(g, dve, c, z4).then_inc(z_made.sem, 1)
                    dve.wait_ge(*bk.full("t1", c))
                    dve.tensor_scalar(zT[:, 1, :], g.bk(1), 1.0, None, ALU.mult).then_inc(bk.release("t1"), 1)
                    for j in range(TC):
                        dve.wait_ge(*bk.full(f"y{j}", c))
                        xt = g.x[:, ds(c * TC + j, 1), :].rearrange("p a b -> p (a b)")
                        dve.tensor_tensor(xt, xt, g.bk(2 + j)[:, 0:D], ALU.add).then_inc(bk.release(f"y{j}"), 1)
        bk.end(NC)
        for e in (w_in, signed):
            e.end()
        for e in (z_made, stored):
            e.end(NC)


def stage_l3_attn(g, DQ, UQ, DKV, UKV, QR, KR, same_head, norm_w, WO, neg):
    nc = g.nc
    NH, HD, G = 16, 16, 4
    ST = S // P
    NB = NC // B
    EPS = 1.1920929e-07
    ln_block(g)
    with ExitStack() as ctx:
        sb = lambda n, s: g.sb(ctx, n, s)
        qT_all, kT_all = sb("qT_all", [P, B * G, S]), sb("kT_all", [P, B * G, S])
        v_all = sb("v_all", [P, NT, NH, 32])

        with ExitStack() as inner:
            sb = lambda n, s: g.sb(inner, n, s)
            dq, uq = sb("dq", [P, P]), sb("uq", [P, P])
            dkv, ukv = sb("dkv", [P, 2, P]), sb("ukv", [P, 2, 2 * P])
            kr, qr = sb("kr", [64, P]), sb("qr", [64, P])
            same, nw = sb("same", [P, P]), sb("nw", [P, 2 * P])
            w = sb("w", [P, 4 * P])
            z4, zT = sb("z4", [P, TC, D]), sb("zT", [P, KD, CH])
            sq, ss = sb("sq", [P, 2, 2 * P]), sb("ss", [P, 2, 16])
            qk = sb("qk", [P, 2, 2 * P])
            qp, kp = sb("qp", [P, NH, 32]), sb("kp", [P, NH, 32])
            bk = Banks(g, [("wq", 0), ("wkv", 1), ("wr", 2)])
            w_in, w_made = g.ev("w_loaded", 16 * 8), g.ev("maps_made", 1)
            with nc.Block() as block:
                @block.sync
                def _(sp):
                    for dst, src in ((dq, DQ), (uq, UQ), (kr, KR), (qr, QR), (same, same_head), (nw, norm_w)):
                        load(sp, dst[:], src, w_in)
                    for dst, src in ((dkv, DKV), (ukv, UKV)):
                        load(sp, dst[:], rows(src), w_in)

                @block.tensor
                def _(pe):
                    pe.wait_ge(*w_in.at(0, 128))
                    pe.wait_ge(*bk.free("wq", 0))
                    pe.matmul(g.bk(0)[:, 0:P], dq[:], uq[:], start=True, stop=True).then_inc(bk.fill("wq"), 1)
                    pe.wait_ge(*bk.free("wkv", 0))
                    for k in range(2):
                        ins = pe.matmul(g.bk(1)[:, 0:2 * P], dkv[:, k, :], ukv[:, k, :], start=k == 0, stop=k == 1)
                    ins.then_inc(bk.fill("wkv"), 1)
                    pe.wait_ge(*bk.free("wr", 0))
                    pe.matmul(g.bk(2)[:, 0:P], kr[:], qr[:], start=True, stop=True).then_inc(bk.fill("wr"), 1)

                @block.gpsimd
                def _(pool):
                    pool.memset(qp[:], 0.0)
                    pool.memset(kp[:], 0.0)
                    pool.memset(v_all[:], 0.0).then_inc(w_made.sem, 1)
                    pool.wait_ge(*w_made.at(0, 1))
                    pool.memset(kp[:, :, HD:HD + 1], 1.0)
                    pool.memset(v_all[:, :, :, HD:HD + 1], 1.0)

                @block.vector
                def _(dve):
                    dve.wait_ge(*w_in.at(0, 128))
                    same2 = same[:].unsqueeze(1).broadcast_to([P, 2, P])
                    dve.wait_ge(*bk.full("wq", 0))
                    dve.tensor_tensor(w[:, 0:P], g.bk(0)[:, 0:P], same[:], ALU.mult).then_inc(bk.release("wq"), 1)
                    dve.wait_ge(*bk.full("wkv", 0))
                    dve.tensor_tensor(w[:, P:3 * P].rearrange("p (a n) -> p a n", a=2), g.bk(1)[:, 0:2 * P].rearrange("p (a n) -> p a n", a=2),
                                      same2, ALU.mult).then_inc(bk.release("wkv"), 1)
                    dve.wait_ge(*bk.full("wr", 0))
                    dve.tensor_tensor(w[:, 3 * P:], g.bk(2)[:, 0:P], same[:], ALU.mult).then_inc(bk.release("wr"), 1)
            bk.end()
            w_in.end()
            w_made.end()

            fills = [("t0", 0), ("t1", 1)]
            for j in range(TC):
                fills += [(f"p{j}_0", 2 + 2 * (j % 2)), (f"p{j}_1", 3 + 2 * (j % 2)), (f"q{j}", 6), (f"k{j}", 7)]
            bk = Banks(g, fills)
            z_made, sq_made, root_made = g.ev("z_made", 1), g.ev("sq_made", TC), g.ev("root_made", TC)
            padded, step, ss_made = g.ev("padded_made", TC), g.ev("dve_step", 2 * TC), g.ev("ss_made", TC)
            qk_made = g.ev("qk_made", TC)
            with nc.Block() as block:
                @block.tensor
                def _(pe):
                    def turn_qk(c, j):
                        pe.wait_ge(*padded.at(c, j + 1))
                        for name, src in ((f"q{j}", qp), (f"k{j}", kp)):
                            pe.wait_ge(*bk.free(name, c))
                            for f in range(G):
                                ins = pe.transpose(g.bk(bk.bank[name])[:, f * P:(f + 1) * P],
                                                   src[:, f * G:(f + 1) * G, :].rearrange("p a b -> p (a b)"), g.ident[:])
                            ins.then_inc(bk.fill(name), 1)

                    with pe.Fori(0, NC) as c:
                        pe.wait_ge(*z_made.at(c, 1))
                        turn(g, pe, bk, c, ("t0", "t1"), z4)
                        pe.wait_ge(*bk.read("t0", c))
                        pe.wait_ge(*bk.read("t1", c))
                        for j in range(TC):
                            for k in range(KD):
                                pe.wait_ge(*bk.free(f"p{j}_{k}", c))
                                pe.matmul(g.bk(bk.bank[f"p{j}_{k}"]), zT[:, k, j * P:(j + 1) * P], w[:], start=True, stop=True)\
                                    .then_inc(bk.fill(f"p{j}_{k}"), 1)
                            if j:
                                turn_qk(c, j - 1)
                        turn_qk(c, TC - 1)

                @block.scalar
                def _(act):
                    def keep_qk(b, hh, c, j):
                        t = ds(hh * CH + j * P, P)
                        for name, dst in ((f"q{j}", qT_all), (f"k{j}", kT_all)):
                            act.wait_ge(*bk.full(name, c))
                            act.activation(dst[:, ds(b * G, G), t], g.bk(bk.bank[name]).rearrange("p (f n) -> p f n", n=P),
                                           ACT.Copy).then_inc(bk.release(name), 1)

                    with act.Fori(0, B) as b, act.Fori(0, NB) as hh:
                        c = b * NB + hh
                        act.wait_ge(*bk.full("t0", c))
                        act.activation(zT[:, 0, :], g.bk(0), ACT.Copy).then_inc(bk.release("t0"), 1)
                        for j in range(TC):
                            for k in range(KD):
                                act.wait_ge(*bk.full(f"p{j}_{k}", c))
                            if j:
                                act.wait_ge(*ss_made.at(c, j))
                            p0 = bk.bank[f"p{j}_0"]
                            act.activation(sq[:], g.ps[:, p0:p0 + 2, 0:2 * P], ACT.Square).then_inc(sq_made.sem, 1)
                            act.wait_ge(*ss_made.at(c, j + 1))
                            act.activation(ss[:], ss[:], ACT.Sqrt, scale=1.0 / HD, bias=g.eps[:, 3:4]).then_inc(root_made.sem, 1)
                            if j:
                                keep_qk(b, hh, c, j - 1)
                        keep_qk(b, hh, c, TC - 1)

                @block.vector
                def _(dve):
                    with dve.Fori(0, NC) as c:
                        link = Chain(dve, step, c)
                        normalise(g, dve, c, z4).then_inc(z_made.sem, 1)
                        dve.wait_ge(*bk.full("t1", c))
                        dve.tensor_scalar(zT[:, 1, :], g.bk(1), 1.0, None, ALU.mult).then_inc(bk.release("t1"), 1)
                        for j in range(TC):
                            p0 = bk.bank[f"p{j}_0"]
                            pj = g.ps[:, p0:p0 + 2, :]
                            heads = lambda a, n: a.rearrange("p k (h d) -> p k h d", d=HD)
                            dve.wait_ge(*sq_made.at(c, j + 1))
                            dve.tensor_reduce(ss[:], heads(sq[:], 16), AXX, ALU.add).then_inc(ss_made.sem, 1)
                            t = ds(c * TC + j, 1)
                            dve.tensor_scalar(v_all[:, t, :, 0:HD].rearrange("p a (k h) d -> p (a k) h d", k=KD),
                                              heads(pj[:, :, 2 * P:3 * P], 8), 1.0, None, ALU.mult)
                            dve.wait_ge(*root_made.at(c, j + 1))
                            link(dve.reciprocal(ss[:], ss[:]))
                            for k in range(KD):
                                ins = dve.tensor_tensor(heads(qk[:], 16)[:, k], heads(pj[:, :, 0:2 * P], 16)[:, k],
                                                        ss[:, k].unsqueeze(2).broadcast_to([P, 2 * 8, HD]), ALU.mult)
                            ins.then_inc(qk_made.sem, 1)
                            dve.wait_ge(*qk_made.at(c, j + 1))
                            if j:
                                dve.wait_ge(*bk.full(f"q{j - 1}", c))
                                dve.wait_ge(*bk.full(f"k{j - 1}", c))
                            nwh = nw[:].rearrange("p (s h d) -> p s h d", s=2, d=HD)
                            qkh = qk[:].rearrange("p k (s h d) -> p k s h d", s=2, d=HD)
                            for k in range(KD):
                                hk = slice(k * 8, k * 8 + 8)
                                dve.tensor_tensor(qp[:, hk, 0:HD], qkh[:, k, 0], nwh[:, 0], ALU.mult)
                                ins = dve.tensor_tensor(kp[:, hk, 0:HD], qkh[:, k, 1], nwh[:, 1], ALU.mult)
                            link(ins)
                            for k in range(KD):
                                hk = slice(k * 8, k * 8 + 8)
                                dve.tensor_tensor(kp[:, hk, 0:HD], kp[:, hk, 0:HD],
                                                  pj[:, k, 3 * P:].rearrange("p (h d) -> p h d", d=HD), ALU.add)\
                                    .then_inc(bk.release(f"p{j}_{k}"), 1)
                            for k in range(KD):
                                dve.wait_ge(*bk.read(f"p{j}_{k}", c))
                            dve.sem_inc(padded.sem, 1)
                        link.close()
            bk.end(NC)
            for ev in (z_made, sq_made, root_made, padded, step, ss_made, qk_made):
                ev.end(NC)

        sb = lambda n, s: g.sb(ctx, n, s)
        qs, ks, qa = sb("qs", [P, S]), sb("ks", [P, S]), sb("qa", [P, S])
        vs = sb("vs", [P, ST, G, 32])
        ngq, ngk = sb("ngq", [P, P]), sb("ngk", [P, P])
        wo = sb("wo", [P, HD * G + G])
        mx, m4, nm = sb("mx", [P, ST, 2, G]), sb("m4", [P, TC, G]), sb("nm", [P, ST, G, 32])
        pT = sb("pT", [P, 4, 2, CH])
        oT, rec, y = sb("oT", [P, 2, CH]), sb("rec", [P, 2, TC, G]), sb("y", [P, 2, TC, HD * G])
        ps1 = [(i, half, pr) for i in range(ST) for half in range(i // TC + 1) for pr in range(2)]
        ps2 = [[(kt, pr) for kt in range((cc + 1) * TC) for pr in range(2)] for cc in range(2)]
        fills, n = [], 0
        sets = {}
        for key in [("m",) + p for p in ps1 if p[0] < TC] + [("m",) + p for p in ps1 if p[0] >= TC]:
            sets[key] = 2 * (n % 3)
            fills += [(f"{key}{a}", sets[key] + a) for a in range(2)]
            n += 1
        for cc in range(2):
            fills.append((f"n{cc}", 6))
            for p in ps2[cc]:
                sets[(cc,) + p] = 2 * (n % 3)
                fills += [(f"{(cc,) + p}{a}", sets[(cc,) + p] + a) for a in range(2)]
                n += 1
            fills.append((f"y{cc}", 6))
        bk = Banks(g, fills)
        NP2 = [len(p) for p in ps2]
        first = [0, NP2[0]]
        w_in, nm_zero = g.ev("w_loaded", 48), g.ev("nm_zero", 1)
        copied = g.ev("head_copied", 3)
        step = g.ev("dve_step", 2 * ST + 3)
        nm_made, masked = g.ev("negmax_made", 2), g.ev("diag_masked", 2 * ST)
        pv, o_read, added = g.ev("pv_done", sum(NP2)), g.ev("o_read", 2), g.ev("x_added", 2)
        with nc.Block() as block:
            @block.sync
            def _(sp):
                load(sp, ngq[:], neg[0], w_in)
                load(sp, ngk[:], neg[1], w_in)
                load(sp, wo[:], WO, w_in)

            def static_head(eng, b, f, what):
                pass

            @block.gpsimd
            def _(pool):
                pool.memset(nm[:], 0.0).then_inc(nm_zero.sem, 1)
                with pool.Fori(0, B) as b, pool.Fori(0, G) as f:
                    it = b * G + f
                    pool.wait_ge(*pv.at(it, 0))
                    pool.tensor_copy(vs[:], v_all[:, ds(b * ST, ST), ds(f * G, G), :]).then_inc(copied.sem, 1)
                    for cc in range(2):
                        pool.wait_ge(*bk.read(f"y{cc}", it))
                        xt = g.x[:, ds(b * ST + cc * TC, TC), ds(f * (G * HD), G * HD)]
                        pool.tensor_tensor(xt, xt, y[:, cc], ALU.add).then_inc(added.sem, 1)

            @block.tensor
            def _(pe):
                def max_piece(it, i, half, pr):
                    key = ("m", i, half, pr)
                    wd = min(CH, (i + 1) * P - half * CH)
                    for a in range(2):
                        pe.wait_ge(*bk.free(f"{key}{a}", it))
                        r = slice(32 * (2 * pr + a), 32 * (2 * pr + a) + HD)
                        pe.matmul(g.bk(sets[key] + a)[:, 0:wd], qs[r, i * P:(i + 1) * P], ks[r, half * CH:half * CH + wd],
                                  start=True, stop=True).then_inc(bk.fill(f"{key}{a}"), 1)

                def score_piece(it, cc, kt, pr):
                    key = (cc, kt, pr)
                    lo = max(0, kt * P - cc * CH)
                    for a in range(2):
                        pe.wait_ge(*bk.free(f"{key}{a}", it))
                        r = slice(32 * (2 * pr + a), 32 * (2 * pr + a) + 32)
                        pe.matmul(g.bk(sets[key] + a)[:, lo:CH], ks[r, kt * P:(kt + 1) * P], qa[r, cc * CH + lo:(cc + 1) * CH],
                                  start=True, stop=True).then_inc(bk.fill(f"{key}{a}"), 1)

                def value_piece(it, cc, n):
                    kt, pr = ps2[cc][n]
                    lo = max(0, kt * P - cc * CH)
                    pe.wait_ge(*bk.read(f"{(cc, kt, pr)}0", it))
                    pe.wait_ge(*bk.read(f"{(cc, kt, pr)}1", it))
                    if n == 0:
                        pe.wait_ge(*o_read.at(it, cc))
                    for a in range(2):
                        h = 2 * pr + a
                        ins = pe.matmul(g.bk(7)[32 * h:32 * h + 32, lo:CH], vs[:, kt, h, :], pT[:, (first[cc] + n) % 4, a, lo:CH],
                                        start=kt == 0, stop=kt == (cc + 1) * TC - 1, skip_group_check=True)
                    ins.then_inc(pv.sem, 1)

                pe.wait_ge(*w_in.at(0, 48))
                with pe.Fori(0, B) as b, pe.Fori(0, G) as f:
                    it = b * G + f
                    pe.wait_ge(*copied.at(it, 3))
                    for i, half, pr in ps1:
                        max_piece(it, i, half, pr)
                    for cc in range(2):
                        pe.wait_ge(*nm_made.at(it, cc + 1))
                        pe.wait_ge(*bk.free(f"n{cc}", it))
                        for j in range(TC):
                            ins = pe.transpose(g.bk(6)[:, j * P:(j + 1) * P], nm[:, cc * TC + j].rearrange("p h d -> p (h d)"), g.ident[:])
                        ins.then_inc(bk.fill(f"n{cc}"), 1)
                        pe.wait_ge(*bk.read(f"n{cc}", it))
                        N = NP2[cc]
                        score_piece(it, cc, *ps2[cc][0])
                        score_piece(it, cc, *ps2[cc][1])
                        for n in range(N):
                            if n + 2 < N:
                                score_piece(it, cc, *ps2[cc][n + 2])
                            value_piece(it, cc, n)
                        pe.wait_ge(*o_read.at(it, cc + 1))
                        pe.wait_ge(*bk.free(f"y{cc}", it))
                        for j in range(TC):
                            ins = pe.matmul(g.bk(6)[:, j * 68:(j + 1) * 68], oT[:, cc, j * P:(j + 1) * P], wo[:], start=True, stop=True)
                        ins.then_inc(bk.fill(f"y{cc}"), 1)

            @block.scalar
            def _(act):
                with act.Fori(0, B) as b, act.Fori(0, G) as f:
                    it = b * G + f
                    act.wait_ge(*pv.at(it, 0))
                    act.activation(ks[:], kT_all[:, ds(it, 1), :].rearrange("p a b -> p (a b)"), ACT.Copy).then_inc(copied.sem, 1)
                    nd = 0
                    for cc in range(2):
                        for n, (kt, pr) in enumerate(ps2[cc]):
                            key = (cc, kt, pr)
                            lo = max(0, kt * P - cc * CH)
                            m = first[cc] + n
                            if kt >= cc * TC:
                                nd += 1
                                act.wait_ge(*masked.at(it, nd))
                            for a in range(2):
                                act.wait_ge(*bk.full(f"{key}{a}", it))
                            act.wait_ge(*pv.at(it, max(0, m - 3)))
                            for a in range(2):
                                act.activation(pT[:, m % 4, a, lo:CH], g.bk(sets[key] + a)[:, lo:CH], ACT.Exp, scale=HD ** -0.5)\
                                    .then_inc(bk.release(f"{key}{a}"), 1)
                        act.wait_ge(*pv.at(it, first[cc] + NP2[cc]))
                        act.activation(oT[:, cc, :], g.bk(7), ACT.Copy).then_inc(o_read.sem, 1)

            @block.vector
            def _(dve):
                dve.wait_ge(*w_in.at(0, 48))
                dve.wait_ge(*nm_zero.at(0, 1))
                with dve.Fori(0, B) as b, dve.Fori(0, G) as f:
                    it = b * G + f
                    link = Chain(dve, step, it)
                    dve.wait_ge(*pv.at(it, 0))
                    dve.tensor_scalar(qs[:], qT_all[:, ds(it, 1), :].rearrange("p a b -> p (a b)"), 1.0, None, ALU.mult)\
                        .then_inc(copied.sem, 1)
                    nd = 0

                    def two(base):
                        return g.ps[:, base:base + 2, :]

                    def maxima(cc):
                        nonlocal nd
                        for i, half, pr in ps1:
                            if i // TC != cc:
                                continue
                            key = ("m", i, half, pr)
                            wd = min(CH, (i + 1) * P - half * CH)
                            for a in range(2):
                                dve.wait_ge(*bk.full(f"{key}{a}", it))
                            if half == i // TC:
                                link(dve.tensor_tensor(two(sets[key])[:, :, wd - P:wd], two(sets[key])[:, :, wd - P:wd],
                                                       ngq[:].unsqueeze(1).broadcast_to([P, 2, P]), ALU.add))
                            for a in range(2):
                                dve.tensor_reduce(mx[:, i, half, 2 * pr + a:2 * pr + a + 1], g.bk(sets[key] + a)[:, 0:wd], AXX, ALU.max)\
                                    .then_inc(bk.release(f"{key}{a}"), 1)
                        last = {bk.bank[f"{('m',) + p}{a}"]: f"{('m',) + p}{a}" for p in ps1 if p[0] // TC == cc for a in range(2)}
                        for name in last.values():
                            dve.wait_ge(*bk.read(name, it))
                        if cc:
                            link(dve.tensor_tensor(m4[:], mx[:, TC:, 0, :], mx[:, TC:, 1, :], ALU.max))
                            src = m4[:]
                        else:
                            src = mx[:, 0:TC, 0, :]
                        dve.tensor_scalar(nm[:, cc * TC:(cc + 1) * TC, :, HD], src, -1.0, None, ALU.mult).then_inc(nm_made.sem, 1)

                    def queries(cc):
                        dve.wait_ge(*bk.full(f"n{cc}", it))
                        h = slice(cc * CH, (cc + 1) * CH)
                        dve.tensor_tensor(qa[:, h], qs[:, h], g.bk(6), ALU.add).then_inc(bk.release(f"n{cc}"), 1)

                    def mask_diagonal(cc):
                        for kt, pr in ps2[cc]:
                            if kt >= cc * TC:
                                key = (cc, kt, pr)
                                lo = kt * P - cc * CH
                                for a in range(2):
                                    dve.wait_ge(*bk.full(f"{key}{a}", it))
                                v = two(sets[key])[:, :, lo:lo + P]
                                dve.tensor_tensor(v, v, ngk[:].unsqueeze(1).broadcast_to([P, 2, P]), ALU.add).then_inc(masked.sem, 1)

                    def rows_out(cc):
                        dve.wait_ge(*bk.full(f"y{cc}", it))
                        yv = g.bk(6)[:, 0:TC * 68].rearrange("p (t e) -> p t e", e=68)
                        link(dve.reciprocal(rec[:, cc], yv[:, :, 64:68]))
                        dve.wait_ge(*added.at(it, 0))
                        for j in range(TC):
                            ins = dve.tensor_tensor(y[:, cc, j].rearrange("p (h d) -> p h d", d=HD),
                                                    yv[:, j, 0:64].rearrange("p (h d) -> p h d", d=HD),
                                                    rec[:, cc, j].unsqueeze(2).broadcast_to([P, G, HD]), ALU.mult)
                        ins.then_inc(bk.release(f"y{cc}"), 1)

                    maxima(0)
                    maxima(1)
                    queries(0)
                    mask_diagonal(0)
                    rows_out(0)
                    queries(1)
                    mask_diagonal(1)
                    rows_out(1)
                    link.close()
        bk.end(B * G)
        w_in.end()
        nm_zero.end()
        for ev in (copied, step, nm_made, masked, pv, o_read, added):
            ev.end(B * G)



def program(nc, t, out):
    with ExitStack() as ctx:
        g = Kernel(nc, ctx)
        opening(g, t["x"])
        stage_l0_attn(g, t["a_rms"], t["a_split"], t["a_wk"], t["a_wugg"], t["a_wout"])
        stage_l0_xattn(g, t["ctx"], t["b_mrow"], t["b_mcol"], t["b_g1"], t["b_b1"], t["b_g2"], t["b_b2"],
                       t["b_wq"], t["b_wk"], t["b_wv"], t["b_wo"])
        stage_l0_ffn(g, t["c_w1"], t["c_s1"], t["c_w2"], t["c_s2"], t["c_h1"], t["c_hs1"], t["c_h2"], t["c_hs2"],
                     t["c_w3"], t["c_s3"])
        stage_l1_attn(g, t["d_wqkv"], t["d_wout"], t["d_alpha"], t["d_beta"], t["same_head"])
        stage_ctx_attn(g, "exp", t["ctxT"], t["e_w"], t["e_w"], t["e_w"], t["e_bc"], t["e_bc"], t["e_br"], t["e_wo"], t["e_bo"],
                       sgn=t["sgn"], sgn_row=t["sgn_row"])
        stage_l1_ffn(g, t["f_gamma"], t["f_beta"], t["f_rw"], t["f_w1"], t["f_w2"])
        stage_l2_attn(g, t["g_wq"], t["g_wk"], t["g_wv"], t["g_bq"], t["g_bk"], t["g_bv"], t["g_wo"], t["g_bo"],
                      t["g_gamma"], t["g_beta"], t["causal"], t["own"])
        stage_ctx_attn(g, "mask", t["ctxT"], t["h_wq"], t["h_wk"], t["h_wv"], t["zero_col"], t["zero_col"], t["zero_row"],
                       t["h_wo"], t["h_bo"], mask=t["h_mask"])
        stage_l2_ffn(g, t["i_w"], t["i_gu"], t["i_v"])
        stage_l3_attn(g, t["j_dq"], t["j_uq"], t["j_dkv"], t["j_ukv"], t["j_qr"], t["j_kr"], t["same_head"], t["j_nw"],
                      t["j_wo"], t["neg"])
        stage_ctx_attn(g, "plain", t["ctxT"], t["k_wq"], t["k_wk"], t["k_wv"], t["k_bq"], t["k_bk"], t["k_bv"], t["k_wo"], t["k_bo"])
        stage_l3_ffn(g, t["l_w"], out)



def as_cols(v):
    return v.reshape(-1, 128).T


def as_rows(v):
    return np.broadcast_to(v[None, :], (128, v.shape[0]))


def pad_heads(w, width=16, room=32):
    w = w.reshape(*w.shape[:-1], -1, width)
    padded = np.zeros((*w.shape[:-1], room), w.dtype)
    padded[..., :width] = w
    return padded.reshape(*w.shape[:-2], -1)


def blocked(w, heads=16):
    i, o = w.shape
    full = np.zeros((heads, i, heads, o), w.dtype)
    for h in range(heads):
        full[h, :, h, :] = w
    return full.reshape(heads * i, heads * o)


def halves(w):
    return w.reshape(256, 2, 512).transpose(1, 0, 2)


def constants():
    k = np.arange(128)
    sign = np.where(np.arange(32) < 16, 1, -1).astype(np.float32)
    col = np.arange(272)
    return {
        "same_head": (k[:, None] // 16 == k[None, :] // 16).astype(np.float32),
        "sgn": np.tile(sign, 4)[:, None],
        "sgn_row": as_rows(np.tile(sign, 16)),
        "causal": (k[None, :] >= k[:, None]).astype(np.float32),
        "own": ((k[:, None] // 32 == (col % 68)[None] // 17) & (k[:, None] % 32 < 16)).astype(np.float32),
        "neg": np.stack([np.where(k[None] > k[:, None], -1e30, 0), np.where(k[:, None] > k[None], -1e30, 0)]).astype(np.float32),
        "zero_col": np.zeros((128, 4), np.float32),
        "zero_row": np.zeros((128, 512), np.float32),
    }


def layout(I):
    def rep(w, n=8):
        return np.tile(w, (1, n))

    wqkv, bqkv = I["L2_attn_Wqkv"], I["L2_attn_bqkv"]
    ukv = I["L3_attn_W_UKV"].T
    fm = I["L1_xattn_fm_w"].T
    wkv = I["L0_xattn_Wkv"]
    keep = I["mask_BxS2_bk0"].astype(np.int32)
    wo = np.zeros((4, 32, 68), np.float32)
    for h in range(4):
        wo[h, :16, h * 16:h * 16 + 16] = I["L3_attn_W_O"].T
        wo[h, 16, 64 + h] = 1
    t = {
        "x": I["x"], "ctx": I["ctx_1024"], "ctxT": I["ctx_1024"].reshape(-1, 256).T,
        "a_rms": as_cols(I["L0_attn_rms_scale"]), "a_split": as_cols(I["L0_attn_split_scale"]),
        "a_wk": I["L0_attn_W_K"], "a_wugg": I["L0_attn_W_ugg"], "a_wout": I["L0_attn_W_out"],
        "b_mrow": as_rows(keep.reshape(-1)), "b_mcol": keep.T,
        "b_g1": as_cols(I["L0_xattn_g1"]), "b_b1": as_cols(I["L0_xattn_b1"]),
        "b_g2": as_cols(I["L0_xattn_g2"]), "b_b2": as_cols(I["L0_xattn_b2"]),
        "b_wq": halves(I["L0_xattn_Wq"]), "b_wk": halves(wkv[:, :1024]), "b_wv": halves(wkv[:, 1024:]),
        "b_wo": I["L0_xattn_Wout"].reshape(2, 512, 256),
        "d_wqkv": I["L1_attn_w_qkv"], "d_wout": I["L1_attn_w_out"],
        "d_alpha": as_cols(np.repeat(I["L1_attn_alpha"], 16)), "d_beta": as_cols(np.repeat(I["L1_attn_beta"], 16)),
        "e_w": blocked(np.concatenate([fm, fm], 1)), "e_bc": as_cols(np.tile(I["L1_xattn_fm_b"], 32)),
        "e_br": as_rows(np.tile(I["L1_xattn_fm_b"], 32)), "e_wo": I["L1_xattn_fc_w"].T, "e_bo": as_rows(I["L1_xattn_fc_b"]),
        "f_gamma": as_cols(I["L1_ffn_gamma"]), "f_beta": as_cols(I["L1_ffn_beta"]), "f_rw": I["L1_ffn_router_w"].T,
        "f_w1": I["L1_ffn_W1"], "f_w2": I["L1_ffn_W2"],
        "g_wq": pad_heads(wqkv[:256].T), "g_wk": pad_heads(wqkv[256:512].T), "g_wv": wqkv[512:].T,
        "g_bq": as_cols(pad_heads(bqkv[:256])), "g_bk": as_cols(pad_heads(bqkv[256:512])), "g_bv": as_rows(bqkv[512:]),
        "g_wo": I["L2_attn_Wout"].T, "g_bo": as_rows(I["L2_attn_bout"]),
        "g_gamma": as_rows(I["L2_attn_gamma"]), "g_beta": as_rows(I["L2_attn_beta"]),
        "h_wo": pad_heads(I["L2_xattn_Wo"]).T, "h_bo": as_rows(I["L2_xattn_bo"]), "h_mask": I["mask_Bx1xSxS2_if1"],
        "i_w": I["L2_ffn_weight"].T,
        "i_gu": np.concatenate([I["L2_ffn_gate_w"], I["L2_ffn_lora_U"].reshape(128, 256)], 0).T,
        "i_v": I["L2_ffn_lora_V"].transpose(0, 2, 1).reshape(128, 256),
        "j_dq": rep(I["L3_attn_W_DQ"]), "j_uq": rep(I["L3_attn_W_UQ"].T), "j_dkv": rep(I["L3_attn_W_DKV"]),
        "j_ukv": np.concatenate([rep(ukv[:, :16]), rep(ukv[:, 16:])], 1),
        "j_qr": rep(I["L3_attn_W_QR"]), "j_kr": rep(I["L3_attn_W_KR"]),
        "j_nw": as_rows(np.concatenate([np.tile(I["L3_attn_q_norm_w"], 8), np.tile(I["L3_attn_k_norm_w"], 8)])),
        "j_wo": wo.reshape(128, 68),
        "k_bv": as_rows(pad_heads(I["L3_xattn_bv"])),
        "k_wo": pad_heads(I["L3_xattn_Wo"].T).T, "k_bo": as_rows(I["L3_xattn_bo"]),
        "l_w": I["L3_ffn_weight"].T,
    }
    for n in ("w1", "w2", "h1", "h2", "w3"):
        t[f"c_{n}"] = I[f"L0_ffn_{n}_w"].T
    for n, s in (("w1", "s1"), ("w2", "s2"), ("h1", "hs1"), ("h2", "hs2")):
        t[f"c_{s}"] = as_cols(I[f"L0_ffn_{n}_s"])
    t["c_s3"] = as_rows(I["L0_ffn_w3_s"])
    for n in "qkv":
        t[f"h_w{n}"] = pad_heads(blocked(I[f"L2_xattn_W{n}"].T))
        t[f"k_w{n}"] = pad_heads(I[f"L3_xattn_W{n}"])
    for n in "qk":
        t[f"k_b{n}"] = as_cols(pad_heads(I[f"L3_xattn_b{n}"]))
    t.update(constants())
    return t


def kernel(**inputs):
    import concourse.bacc as _bacc
    from concourse.bass_utils import run_bass_kernel_spmd as _run

    nc = _bacc.Bacc("TRN2", target_bir_lowering=False, num_devices=1)
    arrays, tensors = {}, {}
    for name, a in layout({k: np.asarray(v) for k, v in inputs.items()}).items():
        a = np.ascontiguousarray(a)
        arrays[f"in_{name}"] = a
        tensors[name] = nc.dram_tensor(f"in_{name}", a.shape, mybir.dt.from_np(a.dtype), kind="ExternalInput").ap()
    out = nc.dram_tensor("out", (B, S, D), F32, kind="ExternalOutput").ap()
    program(nc, tensors, out)
    r = _run(nc, [arrays], core_ids=[0])
    return r.results[0]["out"]
```

```python
import numpy as np
from contextlib import ExitStack
import concourse.bass as bass
from concourse import mybir

F32 = mybir.dt.float32
F32R = mybir.dt.float32r
ALU = mybir.AluOpType
ACT = mybir.ActivationFunctionType
AXX = mybir.AxisListType.X
ds = bass.ds

P = 128
B, S, D = 2, 1024, 256
NT = B * S // P
CH = 512
TC = CH // P
NC = B * S // CH
KD = D // P
L2 = 77
LN_EPS = 1e-5


CREDITED = ("z_added", "x_added", "zT_copied", "state_made", "hi_out", "odd_expert_used", "pv_done", "o_read")


class Event:

    def __init__(self, nc, name):
        self.sem = nc.alloc_semaphore(name)
        self.base = int(name in CREDITED)
        self.per = 0

    def begin(self, per):
        self.per = per

    def at(self, it, k):
        return self.sem, self.base + it * self.per + k

    def end(self, iters=1):
        self.base += self.per * iters


class Banks:

    def __init__(self, g, fills):
        self.g = g
        self.bank, self.nth, self.per = {}, {}, [0] * 8
        for name, b in fills:
            assert name not in self.bank
            self.bank[name], self.nth[name] = b, self.per[b]
            self.per[b] += 1

    def free(self, name, it):
        b = self.bank[name]
        return self.g.bank_free[b], self.g.fills[b] + it * self.per[b] + self.nth[name]

    def full(self, name, it):
        b = self.bank[name]
        return self.g.bank_full[b], self.g.fills[b] + it * self.per[b] + self.nth[name] + 1

    def read(self, name, it):
        sem, n = self.free(name, it)
        return sem, n + 1

    def fill(self, name):
        return self.g.bank_full[self.bank[name]]

    def release(self, name):
        return self.g.bank_free[self.bank[name]]

    def end(self, iters=1):
        for b in range(8):
            self.g.fills[b] += self.per[b] * iters


class Chain:

    def __init__(self, eng, event, it):
        self.eng, self.event, self.it, self.n = eng, event, it, 0

    def __call__(self, ins):
        self.later(ins)
        self.wait(self.n)

    def later(self, ins):
        self.n += 1
        ins.then_inc(self.event.sem, 1)

    def wait(self, n):
        self.eng.wait_ge(*self.event.at(self.it, n))

    def close(self):
        assert self.n == self.event.per, (self.n, self.event.per)


class Kernel:

    def __init__(self, nc, ctx):
        self.nc = nc
        self.ctx = ctx
        self.events = {}
        self.names = {}
        self.fills = [1] * 8
        self.bank_full = [nc.alloc_semaphore(f"bank_full{b}") for b in range(8)]
        self.bank_free = [nc.alloc_semaphore(f"bank_free{b}") for b in range(8)]
        self.x = self.sb(ctx, "x", [P, NT, D])
        self.ident = self.sb(ctx, "ident", [P, P])
        self.ps = ctx.enter_context(nc.psum_tensor("ps", [P, 8, 512], F32))
        self.eps = self.sb(ctx, "eps", [P, 4])
        self.bn = self.sb(ctx, "bn", [P, NT, 6])
        self.mean = self.sb(ctx, "mean", [P, NT])
        self.rstd = self.sb(ctx, "rstd", [P, NT])
        self.std = self.sb(ctx, "std", [P, NT])
        self.bt = self.sb(ctx, "bt", [P, 3, NT])
        self.stage = 0

    def sb(self, ctx, name, shape, dt=F32):
        self.names[name] = n = self.names.get(name, 0) + 1
        return ctx.enter_context(self.nc.sbuf_tensor(name if n == 1 else f"{name}_{n}", shape, dt))

    def ev(self, name, per=1):
        e = self.events.get(name)
        if e is None:
            e = self.events[name] = Event(self.nc, name)
        e.begin(per)
        return e

    def bk(self, b):
        return self.ps[:, b, :]


def rows(w):
    return w.rearrange("(k p) n -> p k n", p=P)


def col(v):
    return v.rearrange("(k p) -> p k", p=P)


def load(eng, dst, src, event):
    eng.dma_start(dst, src).then_inc(event.sem, 16)


def opening(g, x):
    nc = g.nc
    loaded = g.ev("x_loaded", 16)
    zeroed = g.ev("consts_zeroed", 1)
    made = g.ev("consts_made", 1)
    credited = [g.ev(name).sem for name in CREDITED]
    with nc.Block() as block:
        @block.sync
        def _(sp):
            sp.dma_start(g.x[:], x.rearrange("b (t p) d -> p (b t) d", p=P)).then_inc(loaded.sem, 16)
            sp.wait_ge(*loaded.at(0, 16))

        @block.scalar
        def _(act):
            for sem in g.bank_full + g.bank_free + credited:
                act.sem_inc(sem, 1)

        @block.vector
        def _(dve):
            dve.memset(g.eps[:, 0:1], LN_EPS)
            dve.memset(g.eps[:, 1:2], 0.0)
            dve.memset(g.eps[:, 2:3], 1.0)
            dve.memset(g.eps[:, 3:4], 1.1920929e-07)

        @block.gpsimd
        def _(pool):
            pool.memset(g.ident[:], 0.0).then_inc(zeroed.sem, 1)
            pool.wait_ge(*zeroed.at(0, 1))
            pool.affine_select(out=g.ident[:], in_=g.ident[:], compare_op=ALU.not_equal, fill=1.0,
                               base=0, pattern=[[-1, P]], channel_multiplier=1).then_inc(made.sem, 1)
            pool.wait_ge(*made.at(0, 1))
    for e in (loaded, zeroed, made):
        e.end()


def ln_stats_vector(g, dve, src, n, spread, rooted, link):
    for t in range(n):
        ins = dve.bn_stats(g.bn[:, t, :], src[:, t, :])
    ins.then_inc(g.ev_bn.sem, 1)
    dve.wait_ge(*g.ev_bn.at(0, 1))
    bt = g.bt[:, :, 0:n]
    dve.tensor_tensor(bt[:, 0, :], g.bn[:, 0:n, 1], g.bn[:, 0:n, 4], ALU.subtract)
    dve.tensor_tensor(bt[:, 1, :], g.bn[:, 0:n, 2], g.bn[:, 0:n, 5], ALU.add)
    link(dve.tensor_tensor(bt[:, 2, :], g.bn[:, 0:n, 1], g.bn[:, 0:n, 4], ALU.add))
    dve.tensor_scalar(g.mean[:, 0:n], bt[:, 2, :], 0.5, None, ALU.mult)
    link(dve.tensor_tensor(bt[:, 0, :], bt[:, 0, :], bt[:, 0, :], ALU.mult))
    dve.scalar_tensor_tensor(bt[:, 1, :], bt[:, 0, :], D / 4.0, bt[:, 1, :], ALU.mult, ALU.add)\
        .then_inc(spread.sem, 1)
    dve.wait_ge(*rooted.at(0, 1))
    link(dve.reciprocal(g.rstd[:, 0:n], g.std[:, 0:n]))


LN_LINKS = 3


def ln_stats_scalar(g, act, n, spread, rooted):
    act.wait_ge(*spread.at(0, 1))
    act.activation(g.std[:, 0:n], g.bt[:, 1, 0:n], ACT.Sqrt, scale=1.0 / D, bias=g.eps[:, 0:1])\
        .then_inc(rooted.sem, 1)


def ln_block(g, loads=None):
    nc = g.nc
    g.ev_bn = g.ev("bn_stats_done", 1)
    spread, rooted, step = g.ev("ln_variance", 1), g.ev("ln_root", 1), g.ev("ln_step", LN_LINKS)
    with nc.Block() as block:
        if loads is not None:
            @block.sync
            def _(sp):
                loads(sp)

        @block.vector
        def _(dve):
            link = Chain(dve, step, 0)
            ln_stats_vector(g, dve, g.x, NT, spread, rooted, link)
            link.close()

        @block.scalar
        def _(act):
            ln_stats_scalar(g, act, NT, spread, rooted)
    for e in (g.ev_bn, spread, rooted, step):
        e.end()


def normalise(g, dve, c, z4):
    for j in range(TC):
        t = ds(c * TC + j, 1)
        ins = dve.tensor_scalar(z4[:, j, :], g.x[:, t, :].rearrange("p a b -> p (a b)"), g.mean[:, t], g.rstd[:, t],
                                ALU.subtract, ALU.mult)
    return ins


def turn(g, pe, bk, it, names, src4):
    for k, name in enumerate(names):
        pe.wait_ge(*bk.free(name, it))
        for j in range(TC):
            ins = pe.transpose(g.ps[:, bk.bank[name], j * P:(j + 1) * P], src4[:, j, k * P:(k + 1) * P], g.ident[:])
        ins.then_inc(bk.fill(name), 1)


def twice_normalised(g, add, loads=None):
    nc = g.nc
    ln_block(g, loads)
    with nc.Block() as block:
        @block.vector
        def _(dve):
            for t in range(NT):
                dve.tensor_scalar(g.z[:, t, :], g.x[:, t, :], g.mean[:, t:t + 1], g.rstd[:, t:t + 1], ALU.subtract, ALU.mult)
    g.ev_bn = g.ev("bn_stats_done", 1)
    spread, rooted, step = g.ev("ln_variance", 1), g.ev("ln_root", 1), g.ev("ln_step", LN_LINKS)
    with nc.Block() as block:
        @block.vector
        def _(dve):
            link = Chain(dve, step, 0)
            ln_stats_vector(g, dve, g.z, NT, spread, rooted, link)
            link.close()

        @block.gpsimd
        def _(pool):
            if add:
                with pool.Fori(0, NC) as c:
                    t = ds(c * TC, TC)
                    pool.tensor_tensor(g.x[:, t, :], g.x[:, t, :], g.z[:, t, :], ALU.add)

        @block.scalar
        def _(act):
            ln_stats_scalar(g, act, NT, spread, rooted)
    for e in (g.ev_bn, spread, rooted, step):
        e.end()


def stage_l0_attn(g, rms, split, W_K, W_ugg, W_out):
    nc = g.nc
    H = 512
    HB = H // P
    with ExitStack() as ctx:
        sb = lambda n, s: g.sb(ctx, n, s)
        wk, wu, wo = sb("wk", [P, KD, H]), sb("wu", [P, KD, 3 * H]), sb("wo", [P, HB, D])
        rs, sps, gain = sb("rs", [P, KD]), sb("sps", [P, KD]), sb("gain", [P, KD])
        z4, xn4 = sb("z4", [P, TC, D]), sb("xn4", [P, TC, D])
        sq, ss, rn = sb("sq", [P, TC, D]), sb("ss", [P, TC]), sb("rn", [P, TC])
        zT = sb("zT", [P, KD, CH])
        keep = sb("keep", [P, HB, CH + 1])
        gi, go = sb("gi", [P, HB, CH]), sb("go", [P, HB, CH])
        u, sc, yT = sb("u", [P, HB, CH]), sb("sc", [P, HB, CH]), sb("yT", [P, HB, CH])
        carry = sb("carry", [P, HB])
        bk = Banks(g, [("t0", 0), ("t1", 1)] + [(f"{n}{f}", (f % 2) * 4 + i) for f in range(HB)
                                                for i, n in enumerate("kiuo")]
                   + [(f"y{j}", j) for j in range(TC)])
        w_in, gain_made = g.ev("w_loaded", 16 * 5), g.ev("gain_made", 1)
        z_made, norm_made, xn_made = g.ev("z_made", 1), g.ev("norm_made", 2), g.ev("xn_made", 1)
        z_added, step, gated = g.ev("z_added", 1), g.ev("dve_step", 3 + 2 * HB), g.ev("gated_made", HB)
        def load_weights(sp):
            load(sp, rs[:], rms, w_in)
            load(sp, sps[:], split, w_in)
            load(sp, wk[:], rows(W_K), w_in)
            load(sp, wu[:], rows(W_ugg), w_in)
            load(sp, wo[:], rows(W_out), w_in)

        ln_block(g, load_weights)
        with nc.Block() as block:
            @block.gpsimd
            def _(pool):
                with pool.Fori(0, NC) as c:
                    pool.wait_ge(*z_made.at(c, 1))
                    pool.tensor_tensor(g.x[:, ds(c * TC, TC), :], g.x[:, ds(c * TC, TC), :], z4[:], ALU.add)\
                        .then_inc(z_added.sem, 1)

            @block.tensor
            def _(pe):
                pe.wait_ge(*w_in.at(0, 80))
                with pe.Fori(0, NC) as c:
                    pe.wait_ge(*xn_made.at(c, 1))
                    turn(g, pe, bk, c, ("t0", "t1"), xn4)
                    pe.wait_ge(*bk.read("t0", c))
                    pe.wait_ge(*bk.read("t1", c))
                    for f in range(HB):
                        for n in "kiuo":
                            name = f"{n}{f}"
                            w = wk if n == "k" else wu[:, :, {"u": 0, "i": H, "o": 2 * H}[n]:{"u": 0, "i": H, "o": 2 * H}[n] + H]
                            pe.wait_ge(*bk.free(name, c))
                            for k in range(KD):
                                ins = pe.matmul(g.bk(bk.bank[name]), w[:, k, f * P:(f + 1) * P], zT[:, k, :],
                                                start=k == 0, stop=k == KD - 1)
                            ins.then_inc(bk.fill(name), 1)
                    pe.wait_ge(*gated.at(c, HB))
                    for j in range(TC):
                        pe.wait_ge(*bk.free(f"y{j}", c))
                        for f in range(HB):
                            ins = pe.matmul(g.bk(j)[:, 0:D], yT[:, f, j * P:(j + 1) * P], wo[:, f, :],
                                            start=f == 0, stop=f == HB - 1)
                        ins.then_inc(bk.fill(f"y{j}"), 1)

            @block.scalar
            def _(act):
                act.wait_ge(*gain_made.at(0, 1))
                with act.Fori(0, NC) as c:
                    act.wait_ge(*z_made.at(c, 1))
                    for j in range(TC):
                        ins = act.activation(sq[:, j, :], z4[:, j, :], ACT.Square, accum_out=ss[:, j:j + 1])
                    ins.then_inc(norm_made.sem, 1)
                    act.wait_ge(*norm_made.at(c, 1))
                    act.activation(rn[:], ss[:], ACT.Sqrt, scale=1.0 / D).then_inc(norm_made.sem, 1)
                    act.wait_ge(*bk.full("t0", c))
                    act.activation(zT[:, 0, :], g.bk(0), ACT.Copy, scale=gain[:, 0:1]).then_inc(bk.release("t0"), 1)
                    for f in range(HB):
                        for n, dst in (("k", keep[:, f, 1:CH + 1]), ("i", gi[:, f, :]), ("o", go[:, f, :])):
                            name = f"{n}{f}"
                            act.wait_ge(*bk.full(name, c))
                            act.activation(dst, g.bk(bk.bank[name]), ACT.Sigmoid).then_inc(bk.release(name), 1)

            @block.vector
            def _(dve):
                dve.wait_ge(*w_in.at(0, 80))
                dve.tensor_tensor(gain[:], rs[:], sps[:], ALU.mult).then_inc(gain_made.sem, 1)
                dve.wait_ge(*gain_made.at(0, 1))
                with dve.Fori(0, B) as b:
                    dve.memset(keep[:, :, 0:1], 0.0)
                    dve.memset(carry[:], 0.0)
                    with dve.Fori(0, NC // B) as h:
                        c = b * (NC // B) + h
                        link = Chain(dve, step, c)
                        dve.wait_ge(*z_added.at(c, 0))
                        normalise(g, dve, c, z4).then_inc(z_made.sem, 1)
                        dve.wait_ge(*norm_made.at(c, 2))
                        link(dve.tensor_scalar(rn[:], rn[:], 1e-8, None, ALU.add))
                        link(dve.reciprocal(rn[:], rn[:]))
                        for j in range(TC):
                            ins = dve.tensor_scalar(xn4[:, j, :], z4[:, j, :], rn[:, j:j + 1], None, ALU.mult)
                        ins.then_inc(xn_made.sem, 1)
                        dve.wait_ge(*bk.full("t1", c))
                        dve.tensor_scalar(zT[:, 1, :], g.bk(1), gain[:, 1:2], None, ALU.mult)\
                            .then_inc(bk.release("t1"), 1)
                        for f in range(HB):
                            dve.wait_ge(*bk.full(f"u{f}", c))
                            dve.wait_ge(*bk.read(f"i{f}", c))
                            dve.tensor_tensor(u[:, f, :], g.bk(bk.bank[f"u{f}"]), gi[:, f, :], ALU.mult)\
                                .then_inc(bk.release(f"u{f}"), 1)
                            dve.wait_ge(*bk.read(f"u{f}", c))
                            link(dve.scalar_tensor_tensor(u[:, f, :], keep[:, f, 1:CH + 1], 1.0, u[:, f, :],
                                                          ALU.subtract, ALU.mult))
                            link(dve.tensor_tensor_scan(sc[:, f, :], keep[:, f, 0:CH], u[:, f, :],
                                                        carry[:, f:f + 1], ALU.mult, ALU.subtract))
                            dve.wait_ge(*bk.read(f"o{f}", c))
                            dve.tensor_tensor(yT[:, f, :], sc[:, f, :], go[:, f, :], ALU.mult)\
                                .then_inc(gated.sem, 1)
                        dve.tensor_scalar(keep[:, :, 0:1], keep[:, :, CH:CH + 1], 1.0, None, ALU.mult)
                        link(dve.tensor_scalar(carry[:], sc[:, :, CH - 1], 1.0, None, ALU.mult))
                        dve.wait_ge(*z_added.at(c, 1))
                        for j in range(TC):
                            dve.wait_ge(*bk.full(f"y{j}", c))
                            xt = g.x[:, ds(c * TC + j, 1), :]
                            dve.tensor_tensor(xt, xt, g.bk(j)[:, 0:D].rearrange("p (a n) -> p a n", a=1), ALU.add)\
                                .then_inc(bk.release(f"y{j}"), 1)
                        link.close()
        bk.end(NC)
        for e in (w_in, gain_made):
            e.end()
        for e in (z_made, norm_made, xn_made, z_added, step, gated):
            e.end(NC)


def stage_l0_xattn(g, ctx_rows, mask_row, mask_col, g1, b1, g2, b2, Wq, Wk, Wv, Wo):
    nc = g.nc
    HN, HD = 4, 64
    PR = HN // 2
    HW = HN * HD
    NK = S // P
    NB = NC // B
    SC = float(np.float32(1.0) / np.sqrt(np.sqrt(HD)).astype(np.float32))
    with ExitStack() as ctx:
        sb = lambda n, s, dt=F32: g.sb(ctx, n, s, dt)
        zT_all, cxT = sb("zT_all", [P, KD, B * S]), sb("cxT", [P, KD, B * L2])
        mrow, mcol = sb("mrow", [P, B * L2]), sb("mcol", [L2, B])
        with ExitStack() as inner:
            sb = lambda n, s, dt=F32: g.sb(inner, n, s, dt)
            g.z = sb("z_all", [P, NT, D])
            twice_normalised(g, add=False)
            cx, cz, z4 = sb("cx", [P, B, D]), sb("cz", [P, B, D]), sb("z4", [P, TC, D])
            cols = sb("cols", [P, 4, KD])
            mrow_int, mcol_int = sb("mrow_int", [P, B * L2], mybir.dt.int32), sb("mcol_int", [L2, B], mybir.dt.int32)
            bk = Banks(g, [("t0", 0), ("t1", 1)])
            z_made = g.ev("z_made", 1)
            w_in = g.ev("w_loaded", 96)
            zeroed = g.ev("ctx_zeroed", 1)
            with nc.Block() as block:
                @block.sync
                def _(sp):
                    for i, v in enumerate((g1, b1, g2, b2)):
                        load(sp, cols[:, i, :], v, w_in)
                    load(sp, mrow_int[:], mask_row, w_in)
                    load(sp, mcol_int[:], mask_col, w_in)

                @block.vector
                def _(dve):
                    dve.memset(cx[:], 0.0).then_inc(zeroed.sem, 1)
                    with dve.Fori(0, NC) as c:
                        for k in range(KD):
                            dve.wait_ge(*bk.free(f"t{k}", c))
                        for j in range(TC):
                            t = ds(c * TC + j, 1)
                            ins = dve.tensor_scalar(z4[:, j, :], g.z[:, t, :].rearrange("p a b -> p (a b)"),
                                                    g.mean[:, t], g.rstd[:, t], ALU.subtract, ALU.mult)
                        ins.then_inc(z_made.sem, 1)

                @block.tensor
                def _(pe):
                    with pe.Fori(0, NC) as c:
                        pe.wait_ge(*z_made.at(c, 1))
                        turn(g, pe, bk, c, ("t0", "t1"), z4)

                @block.scalar
                def _(act):
                    act.wait_ge(*w_in.at(0, 96))
                    with act.Fori(0, NC) as c:
                        for k in range(KD):
                            act.wait_ge(*bk.full(f"t{k}", c))
                            act.activation(zT_all[:, k, ds(c * CH, CH)], g.bk(k), ACT.Identity, scale=cols[:, 2, k:k + 1],
                                           bias=cols[:, 3, k:k + 1]).then_inc(bk.release(f"t{k}"), 1)
            bk.end(NC)
            z_made.end(NC)
            w_in.end()
            zeroed.end()

            g.ev_bn = g.ev("bn_stats_done", 1)
            spread, rooted, step = g.ev("ln_variance", 1), g.ev("ln_root", 1), g.ev("dve_step", LN_LINKS)
            w_in, cz_made = g.ev("w_loaded", 16), g.ev("z_made", 1)
            bk = Banks(g, [("t0", 0), ("t1", 1)])
            with nc.Block() as block:
                @block.sync
                def _(sp):
                    load(sp, cx[0:L2, :, :], ctx_rows.rearrange("b l d -> l b d"), w_in)

                @block.vector
                def _(dve):
                    dve.wait_ge(*w_in.at(0, 16))
                    dve.tensor_scalar(mrow[:], mrow_int[:], 1.0, 1e30, ALU.subtract, ALU.mult)
                    dve.tensor_scalar(mcol[:], mcol_int[:], 1.0, 1e30, ALU.subtract, ALU.mult)
                    link = Chain(dve, step, 0)
                    ln_stats_vector(g, dve, cx, B, spread, rooted, link)
                    link.close()
                    for b in range(B):
                        ins = dve.tensor_scalar(cz[:, b, :], cx[:, b, :], g.mean[:, b:b + 1], g.rstd[:, b:b + 1], ALU.subtract, ALU.mult)
                    ins.then_inc(cz_made.sem, 1)

                @block.scalar
                def _(act):
                    ln_stats_scalar(g, act, B, spread, rooted)
                    for k in range(KD):
                        act.wait_ge(*bk.full(f"t{k}", 0))
                        act.activation(cxT[:, k, :], g.bk(k)[:, 0:B * L2], ACT.Identity, scale=cols[:, 0, k:k + 1],
                                       bias=cols[:, 1, k:k + 1]).then_inc(bk.release(f"t{k}"), 1)

                @block.tensor
                def _(pe):
                    pe.wait_ge(*cz_made.at(0, 1))
                    for k in range(KD):
                        pe.wait_ge(*bk.free(f"t{k}", 0))
                        for b in range(B):
                            ins = pe.transpose(g.bk(k)[:, b * L2:(b + 1) * L2], cz[0:L2, b, k * P:(k + 1) * P], g.ident[0:L2, 0:L2])
                        ins.then_inc(bk.fill(f"t{k}"), 1)
            bk.end()
            for e in (g.ev_bn, spread, rooted, step, w_in, cz_made):
                e.end()

        sb = lambda n, s, dt=F32: g.sb(ctx, n, s, dt)
        G = 4
        LP = L2 + 1
        wq, wk, wv, wo = sb("wq", [P, KD, HW]), sb("wk", [P, KD, HW]), sb("wv", [P, KD, HW]), sb("wo", [P, PR, D])
        zb, cb = sb("zb", [P, KD, S]), sb("cb", [P, KD, LP])
        kA, kB = sb("kA", [P, HN, S + LP], F32R), sb("kB", [P, HN, S + LP], F32R)
        qA, qB = sb("qA", [P, HN, S], F32R), sb("qB", [P, HN, S], F32R)
        vh, vl = sb("vh", [P, NK + 1, PR, 3, HD], F32R), sb("vl", [P, NK + 1, PR, 3, HD], F32R)
        mxa, mc, mx = sb("mxa", [P, 2, TC, 2, HN]), sb("mc", [P, 2, TC, HN]), sb("mx", [P, 2, TC, HN])
        nm = sb("nm", [P, TC, HN, 32])
        RING = 5
        pf, ph, pl = sb("pf", [P, RING, CH]), sb("ph", [P, RING, CH], F32R), sb("pl", [P, RING, CH], F32R)
        sums, rec, oraw, oT = sb("sums", [P, 2, CH]), sb("rec", [P, CH]), sb("oraw", [P, 2, CH]), sb("oT", [P, 2, PR, CH])
        mb = sb("mb", [L2, 1])

        kcols = [(0, CH), (CH, CH), (S, LP)]
        EVEN, ODD = slice(0, HD), slice(HD, P)
        SIDE = (EVEN, ODD)

        def lo(t):
            return t.bitcast(F32)

        NPC = HN * (NK + 1)
        pieces = [(cc, h, t) for cc in range(2) for h in range(HN) for t in range(NK + 1)]
        maxima = [(j, h) for j in range(TC) for h in range(HN)]
        others = [f"v{t}" for t in range(NK + 1)] + [f"q1_{p}" for p in range(PR)]
        EARLY = 4
        MAX_END, TURN_AT, Y_AT = 22, 25, (48, 52)
        AHEAD, OUT_AT = 3, 6

        def maxima_at(m):
            last = lambda n: EARLY + n * (len(maxima) - EARLY) // MAX_END
            return maxima[last(m):last(m + 1)] if m < MAX_END else []

        fills = [(f"k{p}_{i}", 3 * p + i) for p in range(PR) for i in range(3)] + [(f"q0_{p}", 6 + p) for p in range(PR)]
        for i, (j, h) in enumerate(maxima):
            fills += [(f"m0_{j}_{h}_{a}", 2 * (i % 2) + a) for a in range(2)]
            fills += [(others[i], 4 + i % 2)] if i < len(others) else []
            fills += [(f"c0_{j}", 6)] if h == HN - 1 else []
        for i, (j, h) in enumerate(maxima[:EARLY]):
            fills += [(f"m1_{j}_{h}_{a}", 2 * (i % 2) + a) for a in range(2)]
            fills += [(f"c1_{j}", 6)] if h == HN - 1 else []
        fills.append(("n0", 7))
        for m, (cc, h, t) in enumerate(pieces):
            fills.append((f"s{cc}_{h}_{t}", m % 4))
            fills += [(f"o{cc}_{h}", 4 + h % 2)] if t == NK else []
            for j, hh in maxima_at(m):
                fills += [(f"m1_{j}_{hh}_{a}", 6 + a) for a in range(2)]
                fills += [(f"c1_{j}", 6)] if hh == HN - 1 else []
            fills += [("n1", 7)] if m == TURN_AT else []
            if m in Y_AT:
                fills += [(f"y0_{2 * Y_AT.index(m) + a}", 6 + a) for a in range(2)]
        fills += [(f"y1_{j}", j) for j in range(TC)]
        bk = Banks(g, fills)
        w_in, wo_in = g.ev("w_loaded", 48), g.ev("wo_loaded", 16)
        filled, ones, halves_made = g.ev("pool_filled", 4), g.ev("ones_made", 2), g.ev("halves_made", 6)
        batch, mb_made = g.ev("batch_copied", 2), g.ev("key_bias_copied", 1)
        hi_out = g.ev("hi_out", 2 * 3 * PR + (NK + 1) + 2 * 2 * PR)
        nm_made, row_in = g.ev("negmax_made", 2), g.ev("negmax_row_made", 2 * HN)
        pv, ph_made, pl_made = g.ev("pv_done", 2 * HN * NK), g.ev("p_hi_made", 2 * NPC), g.ev("p_lo_made", 2 * NPC)
        mstep, step = g.ev("ctx_masked", 2 * TC), g.ev("dve_step", 4)
        o_out, inv, scaled = g.ev("head_sums_copied", 2 * HN), g.ev("inverted", 2 * PR), g.ev("heads_scaled", 2 * PR)
        with nc.Block() as block:
            @block.sync
            def _(sp):
                with sp.Fori(0, B) as b, sp.Fori(0, G) as grp:
                    it = b * G + grp
                    gs = ds(grp, 1)
                    sp.wait_ge(*hi_out.at(it, 0))
                    for dst, src in ((wq, Wq), (wk, Wk), (wv, Wv)):
                        sp.dma_start(dst[:], src[gs].rearrange("a (k p) n -> p (a k) n", p=P)).then_inc(w_in.sem, 16)
                    sp.wait_ge(*bk.read("q0_0", it))
                    sp.dma_start(wo[:], Wo[gs].rearrange("a (k p) n -> p (a k) n", p=P)).then_inc(wo_in.sem, 16)

            @block.gpsimd
            def _(pool):
                pool.memset(pf[:, 0, :], 0.0).then_inc(filled.sem, 1)
                pool.memset(pf[:, 1, :], 1.0).then_inc(filled.sem, 1)
                pool.memset(cb[:], 0.0).then_inc(filled.sem, 1)
                pool.memset(nm[:], 0.0).then_inc(filled.sem, 1)
                pool.wait_ge(*filled.at(0, 4))
                with pool.Fori(0, B) as b, pool.Fori(0, G) as grp:
                    it = b * G + grp
                    pool.wait_ge(*hi_out.at(it, 0))
                    pool.tensor_copy(zb[:], zT_all[:, :, ds(b * S, S)]).then_inc(batch.sem, 1)
                    pool.tensor_copy(cb[:, :, 0:L2], cxT[:, :, ds(b * L2, L2)]).then_inc(batch.sem, 1)
                    pool.wait_ge(*bk.free("k1_0", it))
                    pool.tensor_copy(mb[:], mcol[:, ds(b, 1)]).then_inc(mb_made.sem, 1)

            @block.tensor
            def _(pe):
                pe.wait_ge(*ones.at(0, 2))
                pe.wait_ge(*halves_made.at(0, 6))
                with pe.Fori(0, B) as b, pe.Fori(0, G) as grp:
                    it = b * G + grp
                    pe.wait_ge(*w_in.at(it, 48))
                    pe.wait_ge(*batch.at(it, 2))
                    for p in range(PR):
                        for i, (c0, w) in enumerate(kcols):
                            name = f"k{p}_{i}"
                            pe.wait_ge(*bk.free(name, it))
                            for k in range(KD):
                                src = cb[:, k, :] if i == 2 else zb[:, k, c0:c0 + w]
                                ins = pe.matmul(g.bk(bk.bank[name])[:, 0:w], wk[:, k, p * P:(p + 1) * P], src, start=k == 0, stop=k == KD - 1)
                            ins.then_inc(bk.fill(name), 1)
                    def values_of(t):
                        name, rows_ = f"v{t}", P if t < NK else L2
                        pe.wait_ge(*bk.free(name, it))
                        for k in range(KD):
                            src = zb[:, k, t * P:(t + 1) * P] if t < NK else cb[:, k, 0:L2]
                            ins = pe.matmul(g.bk(bk.bank[name])[0:rows_, 0:HW], src, wv[:, k, :], start=k == 0, stop=k == KD - 1)
                        ins.then_inc(bk.fill(name), 1)

                    def queries(cc, p):
                        name = f"q{cc}_{p}"
                        pe.wait_ge(*bk.free(name, it))
                        for k in range(KD):
                            ins = pe.matmul(g.bk(bk.bank[name]), wq[:, k, p * P:(p + 1) * P], zb[:, k, cc * CH:(cc + 1) * CH],
                                            start=k == 0, stop=k == KD - 1)
                        ins.then_inc(bk.fill(name), 1)

                    def score_rows(cc, j, h):
                        q0 = cc * CH + j * P
                        for a in range(2):
                            name = f"m{cc}_{j}_{h}_{a}"
                            pe.wait_ge(*bk.free(name, it))
                            pe.matmul(g.bk(bk.bank[name]), qA[:, h, q0:q0 + P], kA[:, h, a * CH:(a + 1) * CH],
                                      start=True, stop=True).then_inc(bk.fill(name), 1)
                        if h == HN - 1:
                            name = f"c{cc}_{j}"
                            pe.wait_ge(*bk.free(name, it))
                            for hh in range(HN):
                                ins = pe.matmul(g.bk(bk.bank[name])[:, hh * LP:(hh + 1) * LP], qA[:, hh, q0:q0 + P], kA[:, hh, S:],
                                                start=True, stop=True)
                            ins.then_inc(bk.fill(name), 1)

                    def turn_maxima(cc):
                        name = f"n{cc}"
                        pe.wait_ge(*nm_made.at(it, cc + 1))
                        pe.wait_ge(*bk.free(name, it))
                        for j in range(TC):
                            ins = pe.transpose(g.bk(bk.bank[name])[:, j * P:(j + 1) * P], nm[:, j].rearrange("p a b -> p (a b)"), g.ident[:])
                        ins.then_inc(bk.fill(name), 1)

                    for p in range(PR):
                        queries(0, p)
                    for p in range(PR):
                        for i in range(3):
                            pe.wait_ge(*bk.read(f"k{p}_{i}", it))
                    for p in range(PR):
                        pe.wait_ge(*bk.read(f"q0_{p}", it))
                    for i, (j, h) in enumerate(maxima):
                        score_rows(0, j, h)
                        if i <= NK:
                            values_of(i)
                        elif i < len(others):
                            queries(1, i - NK - 1)
                    for p in range(PR):
                        pe.wait_ge(*bk.read(f"q1_{p}", it))
                    for i, (j, h) in enumerate(maxima[:EARLY]):
                        if i == 2:
                            turn_maxima(0)
                        score_rows(1, j, h)

                    def scores(cc, h, t):
                        name, rows_ = f"s{cc}_{h}_{t}", P if t < NK else L2
                        if t == 0:
                            pe.wait_ge(*row_in.at(it, cc * HN + h + 1))
                        pe.wait_ge(*bk.free(name, it))
                        keys, q = slice(t * P, t * P + rows_), slice(cc * CH, (cc + 1) * CH)
                        out = g.bk(bk.bank[name])[0:rows_, :]
                        pe.matmul(out, kA[:, h, keys], qA[:, h, q], start=True, stop=False)
                        pe.matmul(out, kB[:, h, keys], qB[:, h, q], start=False, stop=True).then_inc(bk.fill(name), 1)

                    def values(m, cc, h, t):
                        rows_ = P if t < NK else L2
                        a, r = h % 2, m % RING
                        if t == 0:
                            pe.wait_ge(*bk.free(f"o{cc}_{h}", it))
                        both = lambda v: v[0:rows_, t, h // 2, a:a + 2, :].rearrange("p a d -> p (a d)")
                        out = g.bk(4 + a)
                        pe.wait_ge(*ph_made.at(it, m + 1))
                        pe.matmul(out, both(vh), ph[0:rows_, r, :], start=t == 0, stop=False)
                        pe.matmul(out, both(vl), ph[0:rows_, r, :], start=False, stop=False)
                        pe.wait_ge(*pl_made.at(it, m + 1))
                        last = pe.matmul(out, both(vh), pl[0:rows_, r, :], start=False, stop=t == NK)
                        last.then_inc(bk.fill(f"o{cc}_{h}") if t == NK else pv.sem, 1)

                    def project(cc, j):
                        if (cc, j) == (0, 0):
                            pe.wait_ge(*wo_in.at(it, 16))
                        pe.wait_ge(*scaled.at(it, PR * (cc + 1)))
                        name = f"y{cc}_{j}"
                        pe.wait_ge(*bk.free(name, it))
                        for p in range(PR):
                            ins = pe.matmul(g.bk(bk.bank[name])[:, 0:D], oT[:, cc, p, j * P:(j + 1) * P], wo[:, p, :],
                                            start=p == 0, stop=p == PR - 1)
                        ins.then_inc(bk.fill(name), 1)

                    for m in range(AHEAD):
                        scores(*pieces[m])
                    for m, piece in enumerate(pieces):
                        if m + AHEAD < len(pieces):
                            scores(*pieces[m + AHEAD])
                        values(m, *piece)
                        for j, h in maxima_at(m):
                            score_rows(1, j, h)
                        if m == TURN_AT:
                            turn_maxima(1)
                        if m in Y_AT:
                            for a in range(2):
                                project(0, 2 * Y_AT.index(m) + a)
                    for j in range(TC):
                        project(1, j)

            @block.scalar
            def _(act):
                zero, one = pf[:, 0, :], pf[:, 1, :]
                act.wait_ge(*filled.at(0, 2))
                for t, n in ((kB, S + LP), (qB, S)):
                    for a in range(2):
                        act.activation(t[SIDE[1 - a], a:HN:2, :], zero[SIDE[1 - a], 0:1].unsqueeze(2).broadcast_to([HD, PR, n]), ACT.Copy)\
                            .then_inc(halves_made.sem, 1)
                act.wait_ge(*halves_made.at(0, 4))
                for a in range(2):
                    r = HD * (1 - a)
                    act.activation(kB[r:r + 1, a:HN:2, :], one[r:r + 1, 0:1].unsqueeze(2).broadcast_to([1, PR, S + LP]), ACT.Copy)\
                        .then_inc(halves_made.sem, 1)
                act.wait_ge(*halves_made.at(0, 6))
                act.wait_ge(*ones.at(0, 2))
                with act.Fori(0, B) as b, act.Fori(0, G) as grp:
                    it = b * G + grp
                    for p in range(PR):
                        for i, (c0, w) in enumerate(kcols):
                            name = f"k{p}_{i}"
                            act.wait_ge(*bk.full(name, it))
                            for a, half in enumerate(SIDE):
                                src = g.bk(bk.bank[name])[half, 0:w]
                                act.activation(kB[half, 2 * p + a, c0:c0 + w], src, ACT.Copy, scale=SC)
                                act.activation(kA[half, 2 * p + a, c0:c0 + w], src, ACT.Copy, scale=SC).then_inc(hi_out.sem, 1)

                    def queries_hi(cc, p):
                        name = f"q{cc}_{p}"
                        act.wait_ge(*bk.full(name, it))
                        for a, half in enumerate(SIDE):
                            src = g.bk(bk.bank[name])[half, :]
                            act.activation(qA[SIDE[1 - a], 2 * p + a, cc * CH:(cc + 1) * CH], src, ACT.Copy, scale=SC)
                            act.activation(qA[half, 2 * p + a, cc * CH:(cc + 1) * CH], src, ACT.Copy, scale=SC).then_inc(hi_out.sem, 1)

                    def maxima_rows(cc):
                        name = f"n{cc}"
                        act.wait_ge(*bk.full(name, it))
                        for h in range(HN):
                            r = HD * (1 - h % 2)
                            act.activation(qB[r:r + 1, h, cc * CH:(cc + 1) * CH], g.bk(bk.bank[name])[32 * h:32 * h + 1, :], ACT.Copy)\
                                .then_inc(row_in.sem, 1)
                        act.wait_ge(*row_in.at(it, cc * HN + HN))
                        act.sem_inc(bk.release(name), 1)

                    def head_out(cc, h):
                        a, u = h % 2, cc * PR + h // 2
                        name = f"o{cc}_{h}"
                        act.wait_ge(*bk.full(name, it))
                        if u >= 2:
                            act.wait_ge(*scaled.at(it, u - 1))
                        act.activation(sums[SIDE[a], u % 2, :], g.bk(4 + a)[SIDE[1 - a], :], ACT.Copy).then_inc(o_out.sem, 1)
                        act.activation(oraw[SIDE[a], u % 2, :], g.bk(4 + a)[SIDE[a], :], ACT.Copy).then_inc(bk.release(name), 1)

                    for p in range(PR):
                        queries_hi(0, p)
                    for t in range(NK + 1):
                        name, rows_ = f"v{t}", P if t < NK else L2
                        act.wait_ge(*bk.full(name, it))
                        act.activation(vh[0:rows_, t, :, 0:3:2, :], g.bk(bk.bank[name])[0:rows_, 0:HW].rearrange("p (r a d) -> p r a d", a=2, d=HD),
                                       ACT.Copy).then_inc(hi_out.sem, 1)
                    for p in range(PR):
                        queries_hi(1, p)
                    maxima_rows(0)
                    def used(m):
                        if m < 0:
                            return pv.at(it, 0)
                        cc, h, t = pieces[m]
                        return bk.full(f"o{cc}_{h}", it) if t == NK else pv.at(it, (cc * HN + h) * NK + t + 1)

                    act.wait_ge(*mb_made.at(it, 1))
                    for m, (cc, h, t) in enumerate(pieces):
                        name, rows_ = f"s{cc}_{h}_{t}", P if t < NK else L2
                        bias = mb[:, 0:1] if t == NK else 0.0
                        act.wait_ge(*bk.full(name, it))
                        act.wait_ge(*used(m - RING))
                        act.activation(ph[0:rows_, m % RING, :], g.bk(bk.bank[name])[0:rows_, :], ACT.Exp, bias=bias).then_inc(ph_made.sem, 1)
                        act.activation(pf[0:rows_, m % RING, :], g.bk(bk.bank[name])[0:rows_, :], ACT.Exp, bias=bias).then_inc(bk.release(name), 1)
                        if t == OUT_AT and m > NK:
                            head_out(*pieces[m - t - 1][0:2])
                        if m == TURN_AT + AHEAD:
                            maxima_rows(1)
                    head_out(*pieces[-1][0:2])

            @block.vector
            def _(dve):
                dve.wait_ge(*filled.at(0, 4))
                for t, c in ((vh, 1), (vl, 0)):
                    dve.tensor_copy(t[:, :, :, 1, :], pf[:, c, 0:1].unsqueeze(2).unsqueeze(3).broadcast_to([P, NK + 1, PR, HD]))\
                        .then_inc(ones.sem, 1)
                dve.wait_ge(*ones.at(0, 2))
                with dve.Fori(0, B) as b, dve.Fori(0, G) as grp:
                    it = b * G + grp
                    link = Chain(dve, step, it)
                    nh = 0
                    for p in range(PR):
                        for i, (c0, w) in enumerate(kcols):
                            name = f"k{p}_{i}"
                            dve.wait_ge(*bk.full(name, it))
                            for a, half in enumerate(SIDE):
                                nh += 1
                                dve.wait_ge(*hi_out.at(it, nh))
                                ins = dve.scalar_tensor_tensor(kA[SIDE[1 - a], 2 * p + a, c0:c0 + w], g.bk(bk.bank[name])[half, 0:w], SC,
                                                               lo(kA[half, 2 * p + a, c0:c0 + w]), ALU.mult, ALU.subtract)
                            ins.then_inc(bk.release(name), 1)

                    def values_lo(t, nh):
                        name, rows_ = f"v{t}", P if t < NK else L2
                        dve.wait_ge(*bk.full(name, it))
                        dve.wait_ge(*hi_out.at(it, nh))
                        dve.tensor_tensor(vl[0:rows_, t, :, 0:3:2, :], g.bk(bk.bank[name])[0:rows_, 0:HW].rearrange("p (r a d) -> p r a d", a=2, d=HD),
                                          lo(vh[0:rows_, t, :, 0:3:2, :]), ALU.subtract).then_inc(bk.release(name), 1)

                    def queries_lo(cc, p, nh):
                        name = f"q{cc}_{p}"
                        dve.wait_ge(*bk.full(name, it))
                        for a, half in enumerate(SIDE):
                            dve.wait_ge(*hi_out.at(it, nh + a))
                            q = slice(cc * CH, (cc + 1) * CH)
                            ins = dve.scalar_tensor_tensor(qB[half, 2 * p + a, q], g.bk(bk.bank[name])[half, :], SC,
                                                           lo(qA[half, 2 * p + a, q]), ALU.mult, ALU.subtract)
                        ins.then_inc(bk.release(name), 1)

                    def maximum(cc, j, h):
                        first, second = (f"m{cc}_{j}_{h}_{a}" for a in range(2))
                        dve.wait_ge(*bk.full(first, it))
                        dve.wait_ge(*bk.full(second, it))
                        for a, name in enumerate((first, second)):
                            dve.tensor_reduce(mxa[:, cc, j, a, h:h + 1], g.bk(bk.bank[name]), AXX, ALU.max).then_inc(bk.release(name), 1)
                        if h == HN - 1:
                            name = f"c{cc}_{j}"
                            cv = g.bk(bk.bank[name])[:, 0:HN * LP].rearrange("p (h l) -> p h l", l=LP)[:, :, 0:L2]
                            dve.wait_ge(*bk.full(name, it))
                            dve.tensor_tensor(cv, cv, mrow[:, ds(b * L2, L2)].unsqueeze(1).broadcast_to([P, HN, L2]), ALU.add)\
                                .then_inc(mstep.sem, 1)
                            dve.wait_ge(*mstep.at(it, cc * TC + j + 1))
                            dve.tensor_reduce(mc[:, cc, j, :], cv, AXX, ALU.max).then_inc(bk.release(name), 1)
                            if j == TC - 1:
                                dve.wait_ge(*bk.read(name, it))
                                dve.wait_ge(*bk.read(first, it))
                                dve.wait_ge(*bk.read(second, it))
                                link(dve.tensor_tensor(mx[:, cc], mxa[:, cc, :, 0], mxa[:, cc, :, 1], ALU.max))
                                link(dve.tensor_tensor(mx[:, cc], mx[:, cc], mc[:, cc], ALU.max))
                                if cc == 1:
                                    dve.wait_ge(*bk.full("n0", it))
                                dve.tensor_scalar(nm[:, :, :, 0], mx[:, cc], -1.0, None, ALU.mult).then_inc(nm_made.sem, 1)

                    for p in range(PR):
                        queries_lo(0, p, nh + 1 + 2 * p)
                    nh += 2 * PR
                    for i, (j, h) in enumerate(maxima):
                        maximum(0, j, h)
                        if i <= NK:
                            values_lo(i, nh + 1 + i)
                        elif i < len(others):
                            queries_lo(1, i - NK - 1, nh + NK + 2 + 2 * (i - NK - 1))
                    for j, h in maxima[:EARLY]:
                        maximum(1, j, h)

                    def invert(u, q):
                        dve.wait_ge(*o_out.at(it, 2 * u + 2))
                        if q == 0 and u > 0:
                            dve.wait_ge(*scaled.at(it, u))
                        ins = dve.reciprocal(rec[:, q * P:(q + 1) * P], sums[:, u % 2, q * P:(q + 1) * P])
                        if q == TC - 1:
                            ins.then_inc(inv.sem, 1)

                    def scale(u):
                        dve.wait_ge(*inv.at(it, u + 1))
                        dve.wait_ge(*bk.read(f"o{u // PR}_{2 * (u % PR) + 1}", it))
                        dve.tensor_tensor(oT[:, u // PR, u % PR, :], oraw[:, u % 2, :], rec[:], ALU.mult).then_inc(scaled.sem, 1)

                    def add(cc, j):
                        name = f"y{cc}_{j}"
                        dve.wait_ge(*bk.full(name, it))
                        xt = g.x[:, ds(b * NK + cc * TC + j, 1), :].rearrange("p a b -> p (a b)")
                        dve.tensor_tensor(xt, xt, g.bk(bk.bank[name])[:, 0:D], ALU.add).then_inc(bk.release(name), 1)

                    LAG, UNIT = 2, 2 * (NK + 1)
                    for m, (cc, h, t) in enumerate(pieces):
                        name, rows_, r = f"s{cc}_{h}_{t}", P if t < NK else L2, m % RING
                        dve.wait_ge(*bk.read(name, it))
                        dve.tensor_tensor(pl[0:rows_, r, :], pf[0:rows_, r, :], lo(ph[0:rows_, r, :]), ALU.subtract)\
                            .then_inc(pl_made.sem, 1)
                        for j, hh in (maxima_at(m - LAG) if m >= LAG else []):
                            maximum(1, j, hh)
                        u, place = m // UNIT - 1, m % UNIT - OUT_AT - 1
                        if u >= 0 and 0 <= place < TC:
                            invert(u, place)
                        if u >= 0 and place == TC:
                            scale(u)
                        if m - LAG in Y_AT:
                            for a in range(2):
                                add(0, 2 * Y_AT.index(m - LAG) + a)
                    u = 2 * PR - 1
                    for q in range(TC):
                        invert(u, q)
                    scale(u)
                    for j in range(TC):
                        add(1, j)
                    link.close()
        bk.end(B * G)
        for e in (filled, ones, halves_made):
            e.end()
        for e in (w_in, wo_in, batch, mb_made, hi_out, nm_made, row_in, pv, ph_made, pl_made, mstep, step, o_out, inv, scaled):
            e.end(B * G)


def stage_l0_ffn(g, w1, s1, w2, s2, h1, hs1, h2, hs2, w3, s3):
    nc = g.nc
    H = 1024
    HB = H // P
    with ExitStack() as ctx:
        sb = lambda n, s: g.sb(ctx, n, s)
        w1s, w2s = sb("w1s", [P, KD, H]), sb("w2s", [P, KD, H])
        h1s, h2s, w3s = sb("h1s", [P, HB, H]), sb("h2s", [P, HB, H]), sb("w3s", [P, HB, D])
        c1, c2, c3, c4, r3 = sb("c1", [P, HB]), sb("c2", [P, HB]), sb("c3", [P, HB]), sb("c4", [P, HB]), sb("r3", [P, D])
        z4, zT = sb("z4", [P, TC, D]), sb("zT", [P, KD, CH])
        ga, gb = sb("ga", [P, HB, CH]), sb("gb", [P, HB, CH])
        ys = sb("ys", [P, TC, D])
        bk = Banks(g, [("t0", 0), ("t1", 1)]
                   + [(f"{n}{f}", 2 + (f % 3) * 2 + i) for f in range(HB) for i, n in enumerate("ab")]
                   + [(f"c{f}", f) for f in range(HB)] + [(f"d{f}", f) for f in range(HB)]
                   + [(f"y{j}", j) for j in range(TC)])
        loads = [(c1, s1), (c2, s2), (c3, hs1), (c4, hs2), (r3, s3), (w1s, rows(w1)), (w2s, rows(w2)),
                 (h1s, rows(h1)), (h2s, rows(h2)), (w3s, rows(w3))]
        w_in = g.ev("w_loaded", 16 * 7)
        h1_in, h2_in = g.ev("h1_loaded", 16), g.ev("h2_loaded", 32)
        z_made, x_added = g.ev("z_made", 1), g.ev("x_added", TC)
        def load_weights(sp):
            for dst, src in loads[:7]:
                load(sp, dst[:], src, w_in)
            load(sp, h1s[:], rows(h1), h1_in)
            load(sp, h2s[:], rows(h2), h2_in)
            load(sp, w3s[:], rows(w3), h2_in)

        ln_block(g, load_weights)
        with nc.Block() as block:
            @block.gpsimd
            def _(pool):
                with pool.Fori(0, NC) as c:
                    for j in range(TC):
                        xt = g.x[:, ds(c * TC + j, 1), :]
                        pool.wait_ge(*bk.read(f"y{j}", c))
                        pool.tensor_tensor(xt, xt, ys[:, j:j + 1, :], ALU.add).then_inc(x_added.sem, 1)

            @block.tensor
            def _(pe):
                pe.wait_ge(*w_in.at(0, 112))
                with pe.Fori(0, NC) as c:
                    pe.wait_ge(*z_made.at(c, 1))
                    turn(g, pe, bk, c, ("t0", "t1"), z4)
                    pe.wait_ge(*bk.read("t0", c))
                    pe.wait_ge(*bk.read("t1", c))
                    for f in range(HB):
                        for n, w in (("a", w1s), ("b", w2s)):
                            name = f"{n}{f}"
                            pe.wait_ge(*bk.free(name, c))
                            for k in range(KD):
                                ins = pe.matmul(g.bk(bk.bank[name]), w[:, k, f * P:(f + 1) * P], zT[:, k, :],
                                                start=k == 0, stop=k == KD - 1)
                            ins.then_inc(bk.fill(name), 1)
                    for n, w, src, made in (("c", h1s, ga, "b"), ("d", h2s, gb, "c")):
                        pe.wait_ge(*(h1_in.at(0, 16) if n == "c" else h2_in.at(0, 32)))
                        for f in range(HB):
                            name = f"{n}{f}"
                            pe.wait_ge(*bk.free(name, c))
                            for k in range(HB):
                                if f == 0:
                                    pe.wait_ge(*bk.read(f"{made}{k}", c))
                                ins = pe.matmul(g.bk(f), w[:, k, f * P:(f + 1) * P], src[:, k, :],
                                                start=k == 0, stop=k == HB - 1)
                            ins.then_inc(bk.fill(name), 1)
                    for j in range(TC):
                        pe.wait_ge(*bk.free(f"y{j}", c))
                        for k in range(HB):
                            if j == 0:
                                pe.wait_ge(*bk.read(f"d{k}", c))
                            ins = pe.matmul(g.bk(j)[:, 0:D], ga[:, k, j * P:(j + 1) * P], w3s[:, k, :],
                                            start=k == 0, stop=k == HB - 1)
                        ins.then_inc(bk.fill(f"y{j}"), 1)

            @block.scalar
            def _(act):
                act.wait_ge(*w_in.at(0, 112))
                with act.Fori(0, NC) as c:
                    act.wait_ge(*bk.full("t0", c))
                    act.activation(zT[:, 0, :], g.bk(0), ACT.Copy).then_inc(bk.release("t0"), 1)
                    for f in range(HB):
                        act.wait_ge(*bk.full(f"a{f}", c))
                        act.activation(ga[:, f, :], g.bk(bk.bank[f"a{f}"]), ACT.Silu, scale=c1[:, f:f + 1])\
                            .then_inc(bk.release(f"a{f}"), 1)
                    for n, dst, sc in (("c", gb, c3), ("d", ga, c4)):
                        for f in range(HB):
                            act.wait_ge(*bk.full(f"{n}{f}", c))
                            if n == "d" and f == 0:
                                act.wait_ge(*bk.full("c7", c))
                            act.activation(dst[:, f, :], g.bk(f), ACT.Gelu, scale=sc[:, f:f + 1])\
                                .then_inc(bk.release(f"{n}{f}"), 1)

            @block.vector
            def _(dve):
                dve.wait_ge(*w_in.at(0, 112))
                with dve.Fori(0, NC) as c:
                    normalise(g, dve, c, z4).then_inc(z_made.sem, 1)
                    dve.wait_ge(*bk.full("t1", c))
                    dve.tensor_scalar(zT[:, 1, :], g.bk(1), 1.0, None, ALU.mult).then_inc(bk.release("t1"), 1)
                    for f in range(HB):
                        dve.wait_ge(*bk.full(f"b{f}", c))
                        dve.wait_ge(*bk.read(f"a{f}", c))
                        dve.scalar_tensor_tensor(ga[:, f, :], g.bk(bk.bank[f"b{f}"]), c2[:, f:f + 1], ga[:, f, :],
                                                 ALU.mult, ALU.mult).then_inc(bk.release(f"b{f}"), 1)
                    dve.wait_ge(*x_added.at(c, 0))
                    for j in range(TC):
                        dve.wait_ge(*bk.full(f"y{j}", c))
                        dve.tensor_tensor(ys[:, j, :], g.bk(j)[:, 0:D], r3[:], ALU.mult)\
                            .then_inc(bk.release(f"y{j}"), 1)
        bk.end(NC)
        for e in (w_in, h1_in, h2_in):
            e.end()
        for e in (z_made, x_added):
            e.end(NC)


def stage_l1_attn(g, w_qkv, w_out, alpha, beta, headsum):
    nc = g.nc
    with ExitStack() as ctx:
        sb = lambda n, s: g.sb(ctx, n, s)
        wq, wo, hs = sb("wq", [P, KD, 3 * D]), sb("wo", [P, 2 * KD, D]), sb("hs", [P, P])
        decay = sb("decay", [P, 2, KD])
        z4, zT = sb("z4", [P, TC, D]), sb("zT", [P, KD, CH])
        q, k_, kv = sb("q", [P, KD, CH]), sb("k_", [P, KD, CH]), sb("kv", [P, KD, CH])
        run_k, run_kv = sb("run_k", [P, 2 * KD, CH]), sb("run_kv", [P, 2 * KD, CH])
        carry_k, carry_kv = sb("carry_k", [P, 2 * KD]), sb("carry_kv", [P, 2 * KD])
        qk, rec, yT = sb("qk", [P, 2 * KD, CH]), sb("rec", [P, 2 * KD, CH]), sb("yT", [P, 2 * KD, CH])
        bk = Banks(g, [("t0", 0), ("t1", 1), ("k0", 2), ("v0", 3), ("k1", 4), ("v1", 5), ("q0", 6), ("q1", 7)]
                   + [(f"d{i}", i) for i in range(4)] + [(f"y{j}", 4 + j) for j in range(TC)])
        w_in, decay_made = g.ev("w_loaded", 16 * 5), g.ev("decay_made", 1)
        ready = g.ev("decay_sigmoid", 1)
        z_made, exp_made = g.ev("z_made", 1), g.ev("exp_made", 4)
        qk_made, num_made, y_made, qready = g.ev("qk_made", 4), g.ev("num_made", 4), g.ev("y_made", 4), g.ev("scan_made", 4)
        step = g.ev("dve_step", 4 + 4 + 2 + 4)
        def load_weights(sp):
            load(sp, decay[:, 0, :], alpha, w_in)
            load(sp, decay[:, 1, :], beta, w_in)
            load(sp, hs[:], headsum, w_in)
            load(sp, wq[:], rows(w_qkv), w_in)
            load(sp, wo[:], rows(w_out), w_in)

        ln_block(g, load_weights)
        with nc.Block() as block:
            @block.tensor
            def _(pe):
                pe.wait_ge(*w_in.at(0, 80))
                with pe.Fori(0, NC) as c:
                    pe.wait_ge(*z_made.at(c, 1))
                    turn(g, pe, bk, c, ("t0", "t1"), z4)
                    pe.wait_ge(*bk.read("t0", c))
                    pe.wait_ge(*bk.read("t1", c))
                    for name in ("k0", "v0", "k1", "v1", "q0", "q1"):
                        o = {"q": 0, "k": D, "v": 2 * D}[name[0]] + int(name[1]) * P
                        pe.wait_ge(*bk.free(name, c))
                        for k in range(KD):
                            ins = pe.matmul(g.bk(bk.bank[name]), wq[:, k, o:o + P], zT[:, k, :], start=k == 0, stop=k == KD - 1)
                        ins.then_inc(bk.fill(name), 1)
                    for i in range(4):
                        pe.wait_ge(*qk_made.at(c, i + 1))
                        pe.wait_ge(*bk.free(f"d{i}", c))
                        pe.matmul(g.bk(i), hs[:], qk[:, i, :], start=True, stop=True).then_inc(bk.fill(f"d{i}"), 1)
                    pe.wait_ge(*y_made.at(c, 4))
                    for j in range(TC):
                        pe.wait_ge(*bk.free(f"y{j}", c))
                        for f in range(2 * KD):
                            ins = pe.matmul(g.bk(4 + j)[:, 0:D], yT[:, f, j * P:(j + 1) * P], wo[:, f, :],
                                            start=f == 0, stop=f == 2 * KD - 1)
                        ins.then_inc(bk.fill(f"y{j}"), 1)

            @block.scalar
            def _(act):
                act.wait_ge(*w_in.at(0, 80))
                act.activation(decay[:], decay[:], ACT.Sigmoid).then_inc(ready.sem, 1)
                with act.Fori(0, NC) as c:
                    act.wait_ge(*bk.full("t0", c))
                    act.activation(zT[:, 0, :], g.bk(0), ACT.Copy).then_inc(bk.release("t0"), 1)
                    for i, (name, dst) in enumerate((("k0", k_[:, 0, :]), ("k1", k_[:, 1, :]), ("q0", q[:, 0, :]), ("q1", q[:, 1, :]))):
                        act.wait_ge(*bk.full(name, c))
                        act.activation(dst, g.bk(bk.bank[name]), ACT.Exp).then_inc(exp_made.sem, 1)

            @block.gpsimd
            def _(pool):
                with pool.Fori(0, NC) as c:
                    for i in range(4):
                        pool.wait_ge(*qready.at(c, i + 1))
                        pool.tensor_tensor(yT[:, i, :], q[:, i % KD, :], run_kv[:, i, :], ALU.mult).then_inc(num_made.sem, 1)

            @block.vector
            def _(dve):
                dve.wait_ge(*ready.at(0, 1))
                dve.tensor_scalar(decay[:], decay[:], 1e-8, None, ALU.max).then_inc(decay_made.sem, 1)
                dve.wait_ge(*decay_made.at(0, 1))
                with dve.Fori(0, B) as b:
                    dve.memset(carry_k[:], 0.0)
                    dve.memset(carry_kv[:], 0.0)
                    with dve.Fori(0, NC // B) as hh:
                        c = b * (NC // B) + hh
                        link = Chain(dve, step, c)
                        normalise(g, dve, c, z4).then_inc(z_made.sem, 1)
                        dve.wait_ge(*bk.full("t1", c))
                        dve.tensor_scalar(zT[:, 1, :], g.bk(1), 1.0, None, ALU.mult).then_inc(bk.release("t1"), 1)
                        for i, (name, dst) in enumerate((("k0", k_[:, 0, :]), ("k1", k_[:, 1, :]), ("q0", q[:, 0, :]), ("q1", q[:, 1, :]))):
                            dve.wait_ge(*exp_made.at(c, i + 1))
                            link(dve.tensor_scalar(dst, dst, 1.0, None, ALU.min))
                            dve.scalar_tensor_tensor(dst, g.bk(bk.bank[name]), 0.0, dst, ALU.max, ALU.add)\
                                .then_inc(bk.release(name), 1)
                            dve.wait_ge(*bk.read(name, c))
                            if name[0] == "k":
                                f = int(name[1])
                                dve.wait_ge(*bk.full(f"v{f}", c))
                                dve.tensor_tensor(kv[:, f, :], dst, g.bk(bk.bank[f"v{f}"]), ALU.mult)\
                                    .then_inc(bk.release(f"v{f}"), 1)
                                dve.wait_ge(*bk.read(f"v{f}", c))
                        for i in range(4):
                            f, d = i % KD, decay[:, i // KD, i % KD:i % KD + 1].broadcast_to([P, CH])
                            dve.tensor_tensor_scan(run_kv[:, i, :], d, kv[:, f, :], carry_kv[:, i:i + 1], ALU.mult, ALU.add)\
                                .then_inc(qready.sem, 1)
                            link(dve.tensor_tensor_scan(run_k[:, i, :], d, k_[:, f, :], carry_k[:, i:i + 1], ALU.mult, ALU.add))
                            dve.tensor_tensor(qk[:, i, :], q[:, f, :], run_k[:, i, :], ALU.mult).then_inc(qk_made.sem, 1)
                        dve.wait_ge(*qready.at(c, 4))
                        link(dve.tensor_scalar(carry_k[:], run_k[:, :, CH - 1], 1.0, None, ALU.mult))
                        link(dve.tensor_scalar(carry_kv[:], run_kv[:, :, CH - 1], 1.0, None, ALU.mult))
                        for i in range(4):
                            dve.wait_ge(*bk.full(f"d{i}", c))
                            dve.tensor_scalar(rec[:, i, :], g.bk(i), 1e-6, None, ALU.max).then_inc(bk.release(f"d{i}"), 1)
                            dve.wait_ge(*bk.read(f"d{i}", c))
                            link(dve.reciprocal(rec[:, i, :], rec[:, i, :]))
                            dve.wait_ge(*num_made.at(c, i + 1))
                            dve.tensor_tensor(yT[:, i, :], yT[:, i, :], rec[:, i, :], ALU.mult).then_inc(y_made.sem, 1)
                        for j in range(TC):
                            dve.wait_ge(*bk.full(f"y{j}", c))
                            xt = g.x[:, ds(c * TC + j, 1), :].rearrange("p a b -> p (a b)")
                            dve.tensor_tensor(xt, xt, g.bk(4 + j)[:, 0:D], ALU.add).then_inc(bk.release(f"y{j}"), 1)
                        link.close()
        bk.end(NC)
        for e in (w_in, decay_made, ready):
            e.end()
        for e in (z_made, exp_made, qk_made, num_made, y_made, qready, step):
            e.end(NC)


def stage_ctx_attn(g, kind, ctxT, Wq, Wk, Wv, bq, bk_, bv, Wo, bo, sgn=None, sgn_row=None, mask=None):
    nc = g.nc
    G, W, NL = 4, 512, B * L2
    blocks = lambda f: range(KD) if kind == "plain" else (f // 2,)
    scale = {"exp": 1.0 / 16, "mask": 1.0 / 16, "plain": 1.0 / 4}[kind]
    with ExitStack() as ctx:
        sb = lambda n, s, dt=F32: g.sb(ctx, n, s, dt)
        wq, wk, wv, wo = sb("wq", [P, KD, W]), sb("wk", [P, KD, W]), sb("wv", [P, KD, W]), sb("wo", [P, G, D])
        cq, ck, rv, ro = sb("cq", [P, G]), sb("ck", [P, G]), sb("rv", [P, W]), sb("ro", [P, D])
        cT = sb("cT", [P, KD, NL])
        kT, v = sb("kT", [P, G, NL]), sb("v", [L2, B, W])
        kb, vb = sb("kb", [P, G, L2]), sb("vb", [L2, W])
        z4, zT, qT = sb("z4", [P, TC, D]), sb("zT", [P, KD, CH]), sb("qT", [P, G, CH])
        e = sb("e", [P, 2, G, G, L2])
        mx2, sm2 = sb("mx2", [P, 2, G, G]), sb("sm2", [P, 2, G, G])
        pT, oT = sb("pT", [L2, G, G, CH]), sb("oT", [P, G, CH])
        loads = [(cq, bq), (ck, bk_), (rv, bv), (ro, bo), (cT, rows(ctxT)), (wk, rows(Wk)), (wv, rows(Wv)), (wq, rows(Wq)), (wo, rows(Wo))]
        if kind == "exp":
            sg, sr = sb("sg", [P, 1]), sb("sr", [P, W])
            loads += [(sg, sgn), (sr, sgn_row)]
        if kind == "mask":
            mi, mf, ma = sb("mi", [P, NT, L2], mybir.dt.int32), sb("mf", [P, NT, L2]), sb("ma", [P, NT, L2])
            loads += [(mi, mask.rearrange("b o (t p) l -> p (b o t) l", p=P))]
        nload = 16 * len(loads)
        NB = NC // B

        bk = Banks(g, [(f"k{f}", f) for f in range(G)] + [(f"v{b}", 4 + b) for b in range(B)])
        w_in, v_step, prepared = g.ev("w_loaded", nload), g.ev("dve_step", 2 * B if kind == "exp" else 0), g.ev("mask_made", 1)
        def load_weights(sp):
            for dst, src in loads:
                load(sp, dst[:], src, w_in)

        ln_block(g, load_weights)
        with nc.Block() as block:
            @block.tensor
            def _(pe):
                pe.wait_ge(*w_in.at(0, nload))
                for f in range(G):
                    pe.wait_ge(*bk.free(f"k{f}", 0))
                    for k in blocks(f):
                        ins = pe.matmul(g.bk(f)[:, 0:NL], wk[:, k, f * P:(f + 1) * P], cT[:, k, :], start=k == blocks(f)[0], stop=k == blocks(f)[-1])
                    ins.then_inc(bk.fill(f"k{f}"), 1)
                for b in range(B):
                    pe.wait_ge(*bk.free(f"v{b}", 0))
                    for k in range(KD):
                        ins = pe.matmul(g.bk(4 + b)[0:L2, :], cT[:, k, b * L2:(b + 1) * L2], wv[:, k, :], start=k == 0, stop=k == KD - 1)
                    ins.then_inc(bk.fill(f"v{b}"), 1)

            @block.scalar
            def _(act):
                act.wait_ge(*w_in.at(0, nload))
                if kind == "exp":
                    act.wait_ge(*prepared.at(0, 1))
                for f in range(G):
                    act.wait_ge(*bk.full(f"k{f}", 0))
                    act.activation(kT[:, f, :], g.bk(f)[:, 0:NL], ACT.Exp if kind == "exp" else ACT.Identity,
                                   scale=sg[:, 0:1] if kind == "exp" else 1.0, bias=ck[:, f:f + 1]).then_inc(bk.release(f"k{f}"), 1)
                if kind == "exp":
                    for b in range(B):
                        act.wait_ge(*v_step.at(0, b + 1))
                        act.activation(v[:, b, :], v[:, b, :], ACT.Exp)

            @block.vector
            def _(dve):
                dve.wait_ge(*w_in.at(0, nload))
                if kind == "exp":
                    dve.tensor_scalar(cq[:], cq[:], sg[:, 0:1], None, ALU.mult)
                    dve.tensor_scalar(ck[:], ck[:], sg[:, 0:1], None, ALU.mult).then_inc(prepared.sem, 1)
                for b in range(B):
                    dve.wait_ge(*bk.full(f"v{b}", 0))
                    dve.tensor_tensor(v[:, b, :], g.bk(4 + b)[0:L2, :], rv[0:L2, :], ALU.add).then_inc(bk.release(f"v{b}"), 1)
                    dve.wait_ge(*bk.read(f"v{b}", 0))
                    if kind == "exp":
                        dve.tensor_tensor(v[:, b, :], v[:, b, :], sr[0:L2, :], ALU.mult).then_inc(v_step.sem, 1)
                if kind == "mask":
                    dve.tensor_scalar(mf[:], mi[:], 0.0, None, ALU.not_equal).then_inc(prepared.sem, 1)
                    dve.wait_ge(*prepared.at(0, 1))
                    dve.tensor_scalar(ma[:], mf[:], 1.0, 1e20, ALU.subtract, ALU.mult)
        if kind == "plain":
            prepared.begin(0)
        v_step.begin(B if kind == "exp" else 0)
        bk.end()
        for ev in (w_in, v_step, prepared):
            ev.end()

        fills = [("t0", 4), ("t1", 5)] + [(f"q{f}", [6, 7, 4, 5][f]) for f in range(G)]
        order = [("s", 0)]
        for j in range(TC):
            if j + 1 < TC:
                order.append(("s", j + 1))
            order.append(("p", j))
        for n, j in order:
            fills += [(f"{n}{j}_{h}", h + (4 if n == "p" else 0)) for h in range(G)]
        fills += [(f"o{f}", f) for f in range(G)] + [(f"y{j}", 4 + j) for j in range(TC)]
        bk = Banks(g, fills)
        z_made, kv_ready, y_added = g.ev("z_made", 1), g.ev("kv_ready", 2), g.ev("x_added", 1)
        e_made, exp_made, p_made = g.ev("e_made", TC), g.ev("exp_made", TC), g.ev("p_made", TC)
        step = g.ev("dve_step", TC * (5 if kind == "mask" else 3))
        with nc.Block() as block:
            @block.gpsimd
            def _(pool):
                with pool.Fori(0, B) as b:
                    bl = ds(b * L2, L2)
                    pool.wait_ge(g.bank_full[7], g.fills[7] + b * (NB * bk.per[7]))
                    pool.tensor_copy(kb[:], kT[:, :, bl]).then_inc(kv_ready.sem, 1)
                    pool.tensor_copy(vb[:], v[:, ds(b, 1), :].rearrange("p a b -> p (a b)")).then_inc(kv_ready.sem, 1)
                    with pool.Fori(0, NB) as hh:
                        c = b * NB + hh
                        pool.wait_ge(*z_made.at(c, 1))
                        x4 = g.x[:, ds(c * TC, TC), :]
                        pool.tensor_tensor(x4, x4, ro[:].unsqueeze(1).broadcast_to([P, TC, D]), ALU.add).then_inc(y_added.sem, 1)

            @block.tensor
            def _(pe):
                def scores(c, j):
                    for h in range(G):
                        pe.wait_ge(*bk.free(f"s{j}_{h}", c))
                    for f in range(G):
                        for h in range(G):
                            r = slice(32 * h, 32 * h + 32)
                            ins = pe.matmul(g.bk(h)[:, f * L2:(f + 1) * L2], qT[r, f, j * P:(j + 1) * P], kb[r, f, :],
                                            start=True, stop=True)
                            if f == G - 1:
                                ins.then_inc(bk.fill(f"s{j}_{h}"), 1)

                with pe.Fori(0, B) as b, pe.Fori(0, NB) as hh:
                    c = b * NB + hh
                    pe.wait_ge(*z_made.at(c, 1))
                    turn(g, pe, bk, c, ("t0", "t1"), z4)
                    pe.wait_ge(*bk.read("t0", c))
                    pe.wait_ge(*bk.read("t1", c))
                    for f in range(G):
                        b_ = bk.bank[f"q{f}"]
                        pe.wait_ge(*bk.free(f"q{f}", c))
                        for k in blocks(f):
                            ins = pe.matmul(g.bk(b_), wq[:, k, f * P:(f + 1) * P], zT[:, k, :], start=k == blocks(f)[0], stop=k == blocks(f)[-1])
                        ins.then_inc(bk.fill(f"q{f}"), 1)
                    for f in range(G):
                        pe.wait_ge(*bk.read(f"q{f}", c))
                    pe.wait_ge(*kv_ready.at(b, 2))
                    scores(c, 0)
                    for j in range(TC):
                        if j + 1 < TC:
                            scores(c, j + 1)
                        pe.wait_ge(*p_made.at(c, j + 1))
                        for h in range(G):
                            pe.wait_ge(*bk.free(f"p{j}_{h}", c))
                            for f in range(G):
                                ins = pe.transpose(g.bk(4 + h)[0:L2, f * P:(f + 1) * P], e[:, j % 2, h, f, :], g.ident[:])
                            ins.then_inc(bk.fill(f"p{j}_{h}"), 1)
                    for f in range(G):
                        if f == 0:
                            for h in range(G):
                                pe.wait_ge(*bk.read(f"p{TC - 1}_{h}", c))
                        pe.wait_ge(*bk.free(f"o{f}", c))
                        for h in range(G):
                            ins = pe.matmul(g.bk(f)[32 * h:32 * h + 32, :], vb[:, (f * G + h) * 32:(f * G + h + 1) * 32], pT[:, h, f, :],
                                            start=True, stop=True)
                        ins.then_inc(bk.fill(f"o{f}"), 1)
                    for j in range(TC):
                        pe.wait_ge(*bk.free(f"y{j}", c))
                        for f in range(G):
                            if j == 0:
                                pe.wait_ge(*bk.read(f"o{f}", c))
                            ins = pe.matmul(g.bk(4 + j)[:, 0:D], oT[:, f, j * P:(j + 1) * P], wo[:, f, :], start=f == 0, stop=f == G - 1)
                        ins.then_inc(bk.fill(f"y{j}"), 1)

            @block.scalar
            def _(act):
                def probs_out(act, c, j):
                    for h in range(G):
                        act.wait_ge(*bk.full(f"p{j}_{h}", c))
                        act.activation(pT[:, h, :, j * P:(j + 1) * P], g.bk(4 + h)[0:L2, :].rearrange("p (f q) -> p f q", q=P),
                                       ACT.Copy).then_inc(bk.release(f"p{j}_{h}"), 1)

                with act.Fori(0, NC) as c:
                    act.wait_ge(*bk.full("t0", c))
                    act.activation(zT[:, 0, :], g.bk(4), ACT.Copy).then_inc(bk.release("t0"), 1)
                    for f in range(G):
                        act.wait_ge(*bk.full(f"q{f}", c))
                        act.activation(qT[:, f, :], g.bk(bk.bank[f"q{f}"]), ACT.Exp if kind == "exp" else ACT.Identity,
                                       scale=sg[:, 0:1] if kind == "exp" else 1.0, bias=cq[:, f:f + 1]).then_inc(bk.release(f"q{f}"), 1)
                    for j in range(TC):
                        for h in range(G):
                            act.wait_ge(*bk.full(f"s{j}_{h}", c))
                            if j >= 2:
                                act.wait_ge(*bk.full(f"p{j - 2}_{h}", c))
                            act.activation(e[:, j % 2, h], g.bk(h)[:, 0:G * L2].rearrange("p (f l) -> p f l", l=L2), ACT.Copy)\
                                .then_inc(bk.release(f"s{j}_{h}"), 1)
                        if j:
                            probs_out(act, c, j - 1)
                        act.wait_ge(*e_made.at(c, j + 1))
                        act.activation(e[:, j % 2], e[:, j % 2], ACT.Exp, scale=scale).then_inc(exp_made.sem, 1)
                    probs_out(act, c, TC - 1)
                    for f in (0, 2):
                        act.wait_ge(*bk.full(f"o{f}", c))
                        act.activation(oT[:, f, :], g.bk(f), ACT.Copy).then_inc(bk.release(f"o{f}"), 1)

            @block.vector
            def _(dve):
                rows16 = lambda a: a.rearrange("p h f l -> p (h f) l")
                wide = lambda a: a.rearrange("p h f -> p (h f)").unsqueeze(2).broadcast_to([P, G * G, L2])

                def shifted(c, j, link):
                    for h in range(G):
                        dve.wait_ge(*bk.read(f"s{j}_{h}", c))
                    ej, mx = e[:, j % 2], mx2[:, j % 2]
                    if kind == "mask":
                        m = lambda a: a[:, ds(c * TC + j, 1), :].broadcast_to([P, G * G, L2])
                        link(dve.tensor_tensor(rows16(ej), rows16(ej), m(mf), ALU.mult))
                        link(dve.tensor_tensor(rows16(ej), rows16(ej), m(ma), ALU.add))
                    link(dve.tensor_reduce(mx, ej, AXX, ALU.max))
                    dve.tensor_tensor(rows16(ej), rows16(ej), wide(mx), ALU.subtract).then_inc(e_made.sem, 1)

                def softened(c, j, link):
                    dve.wait_ge(*exp_made.at(c, j + 1))
                    ej, sm = e[:, j % 2], sm2[:, j % 2]
                    link(dve.tensor_reduce(sm, ej, AXX, ALU.add))
                    link(dve.reciprocal(sm, sm))
                    dve.tensor_tensor(rows16(ej), rows16(ej), wide(sm), ALU.mult).then_inc(p_made.sem, 1)

                with dve.Fori(0, NC) as c:
                    link = Chain(dve, step, c)
                    normalise(g, dve, c, z4).then_inc(z_made.sem, 1)
                    dve.wait_ge(*bk.full("t1", c))
                    dve.tensor_scalar(zT[:, 1, :], g.bk(5), 1.0, None, ALU.mult).then_inc(bk.release("t1"), 1)
                    for j in range(TC):
                        shifted(c, j, link)
                        softened(c, j, link)
                    for f in (1, 3):
                        dve.wait_ge(*bk.full(f"o{f}", c))
                        dve.tensor_scalar(oT[:, f, :], g.bk(f), 1.0, None, ALU.mult).then_inc(bk.release(f"o{f}"), 1)
                    dve.wait_ge(*y_added.at(c, 1))
                    for j in range(TC):
                        dve.wait_ge(*bk.full(f"y{j}", c))
                        xt = g.x[:, ds(c * TC + j, 1), :].rearrange("p a b -> p (a b)")
                        dve.tensor_tensor(xt, xt, g.bk(4 + j)[:, 0:D], ALU.add).then_inc(bk.release(f"y{j}"), 1)
                    link.close()
        bk.end(NC)
        kv_ready.end(B)
        for ev in (z_made, y_added, e_made, exp_made, p_made, step):
            ev.end(NC)


E8 = 8


def moe_prologue(g, zTh, zTl, wd, gamma, beta, rw, load_first, split_first):
    nc = g.nc
    twice_normalised(g, True, load_first)
    with ExitStack() as ctx:
        sb = lambda n, s: g.sb(ctx, n, s)
        gm, bt, rws = sb("gm", [P, KD]), sb("bt_", [P, KD]), sb("rws", [P, KD, E8])
        z4, zT = sb("z4", [P, TC, D]), sb("zT", [P, KD, CH])
        lg, pr, mx, sm = sb("lg", [P, NT, E8]), sb("pr", [P, NT, E8]), sb("mx", [P, NT]), sb("sm", [P, NT])
        rank, cmp_ = sb("rank", [P, NT, E8]), sb("cmp_", [P, NT, E8])
        bk = Banks(g, [("t0", 0), ("t1", 1), ("lg", 2)])
        w_in, z_made, copied, hi = g.ev("w_loaded", 16 * 3), g.ev("z_made", 1), g.ev("zT_copied", 1), g.ev("zT_hi_made", 1)
        with nc.Block() as block:
            @block.sync
            def _(sp):
                load(sp, gm[:], gamma, w_in)
                load(sp, bt[:], beta, w_in)
                load(sp, rws[:], rows(rw), w_in)

            @block.vector
            def _(dve):
                with dve.Fori(0, NC) as c:
                    for j in range(TC):
                        t = ds(c * TC + j, 1)
                        ins = dve.tensor_scalar(z4[:, j, :], g.z[:, t, :].rearrange("p a b -> p (a b)"),
                                                g.mean[:, t], g.rstd[:, t], ALU.subtract, ALU.mult)
                    ins.then_inc(z_made.sem, 1)
                    dve.wait_ge(*bk.full("lg", c))
                    dve.tensor_scalar(lg[:, ds(c * TC, TC), :], g.bk(2)[:, 0:TC * E8].rearrange("p (t e) -> p t e", e=E8),
                                      1.0 / 1.5, None, ALU.mult).then_inc(bk.release("lg"), 1)

            @block.scalar
            def _(act):
                act.wait_ge(*w_in.at(0, 48))
                with act.Fori(0, NC) as c:
                    act.wait_ge(*copied.at(c, 0))
                    for k in range(KD):
                        act.wait_ge(*bk.full(f"t{k}", c))
                        act.activation(zT[:, k, :], g.bk(k), ACT.Identity, scale=gm[:, k:k + 1], bias=bt[:, k:k + 1])\
                            .then_inc(bk.release(f"t{k}"), 1)

            @block.gpsimd
            def _(pool):
                with pool.Fori(0, NC) as c:
                    pool.wait_ge(*bk.read("t0", c))
                    pool.wait_ge(*bk.read("t1", c))
                    t = ds(c * CH, CH)
                    pool.tensor_copy(zTh[:, :, t], zT[:]).then_inc(hi.sem, 1)
                    pool.wait_ge(*hi.at(c, 1))
                    pool.tensor_tensor(zTl[:, :, t], zT[:], zTh[:, :, t].bitcast(F32), ALU.subtract).then_inc(copied.sem, 1)

            @block.tensor
            def _(pe):
                pe.wait_ge(*w_in.at(0, 48))
                with pe.Fori(0, NC) as c:
                    pe.wait_ge(*z_made.at(c, 1))
                    turn(g, pe, bk, c, ("t0", "t1"), z4)
                    pe.wait_ge(*bk.read("t0", c))
                    pe.wait_ge(*bk.read("t1", c))
                    pe.wait_ge(*bk.free("lg", c))
                    for j in range(TC):
                        for k in range(KD):
                            ins = pe.matmul(g.bk(2)[:, j * E8:(j + 1) * E8], zT[:, k, j * P:(j + 1) * P], rws[:, k, :],
                                            start=k == 0, stop=k == KD - 1)
                    ins.then_inc(bk.fill("lg"), 1)
        bk.end(NC)
        w_in.end()
        for e in (z_made, copied, hi):
            e.end(NC)

        expd = g.ev("router_exp", 1)
        step = g.ev("dve_step", 7 + 2 * E8)
        wide = lambda a: a.unsqueeze(2).broadcast_to([P, NT, E8])
        with nc.Block() as block:
            @block.gpsimd
            def _(pool):
                split_first(pool)

            @block.scalar
            def _(act):
                split_first(act)
                act.wait_ge(*step.at(0, 2))
                act.activation(pr[:], lg[:], ACT.Exp).then_inc(expd.sem, 1)

            @block.vector
            def _(dve):
                link = Chain(dve, step, 0)
                link(dve.tensor_reduce(mx[:], lg[:], AXX, ALU.max))
                link(dve.tensor_tensor(lg[:], lg[:], wide(mx[:]), ALU.subtract))
                dve.wait_ge(*expd.at(0, 1))
                link(dve.tensor_reduce(sm[:], pr[:], AXX, ALU.add))
                link(dve.reciprocal(sm[:], sm[:]))
                link(dve.tensor_tensor(pr[:], pr[:], wide(sm[:]), ALU.mult))
                link(dve.memset(rank[:], 0.0))
                for j in range(E8):
                    pj = pr[:, :, j:j + 1]
                    if j < E8 - 1:
                        dve.tensor_tensor(cmp_[:, :, j + 1:], pj.broadcast_to([P, NT, E8 - 1 - j]), pr[:, :, j + 1:], ALU.is_ge)
                    link(dve.tensor_tensor(cmp_[:, :, 0:j + 1], pj.broadcast_to([P, NT, j + 1]), pr[:, :, 0:j + 1], ALU.is_gt))
                    link(dve.tensor_tensor(rank[:], rank[:], cmp_[:], ALU.add))
                link(dve.tensor_scalar(cmp_[:], rank[:], 1.5, None, ALU.is_lt))
                dve.tensor_tensor(wd[:], pr[:], cmp_[:], ALU.mult)
                link.close()
        for e in (expd, step):
            e.end()


def stage_l1_ffn(g, gamma, beta, rw, W1, W2):
    nc = g.nc
    H = 1024
    HB = H // P
    PASSES = ((0, 0), (1, 0), (0, 1))
    with ExitStack() as ctx:
        sb = lambda n, s, dt=F32: g.sb(ctx, n, s, dt)
        w1f, w2f = sb("w1f", [P, KD, H]), sb("w2f", [P, HB, D])
        w1s = [[sb(f"w1{n}{i}", [P, KD, H], F32R) for n in ("hi", "lo")] for i in range(2)]
        w2s = [[sb(f"w2{n}{i}", [P, HB, D], F32R) for n in ("hi", "lo")] for i in range(2)]
        zTs = [sb("zT_hi", [P, KD, B * S], F32R), sb("zT_lo", [P, KD, B * S], F32R)]
        wd = sb("wd", [P, NT, E8])
        RING = 4
        hf = sb("hf", [P, RING, CH])
        hs = [sb("h_hi", [P, RING, CH], F32R), sb("h_lo", [P, RING, CH], F32R)]
        w_in, split, wstep = g.ev("expert_loaded", 32), g.ev("expert_split", 1), g.ev("expert_hi_made", 2)
        used = [g.ev("even_expert_used", 1), g.ev("odd_expert_used", 1)]

        def load_first(sp):
            load(sp, w1f[:], rows(W1[0]), w_in)
            load(sp, w2f[:], rows(W2[0]), w_in)

        def split_hi(eng, s, e):
            eng.wait_ge(*w_in.at(e, 32))
            for dst, src in ((w1s[s][0], w1f), (w2s[s][0], w2f)):
                if eng is nc.scalar:
                    eng.activation(dst[:], src[:], ACT.Copy).then_inc(wstep.sem, 1)
                else:
                    zero = g.eps[:, 1:2].unsqueeze(2).broadcast_to([P, *src.shape[1:]])
                    eng.tensor_tensor(dst[:], src[:], zero, ALU.add).then_inc(wstep.sem, 1)

        def split_lo(pool, s, e):
            pool.wait_ge(*wstep.at(e, 2))
            pool.tensor_tensor(w1s[s][1][:], w1f[:], w1s[s][0][:].bitcast(F32), ALU.subtract)
            pool.tensor_tensor(w2s[s][1][:], w2f[:], w2s[s][0][:].bitcast(F32), ALU.subtract).then_inc(split.sem, 1)

        def split_first(eng):
            if eng is nc.scalar:
                split_hi(eng, 0, 0)
            else:
                split_lo(eng, 0, 0)

        with ExitStack() as inner:
            g.z = g.sb(inner, "z_all", [P, NT, D])
            moe_prologue(g, *zTs, wd, gamma, beta, rw, load_first, split_first)
        bk = Banks(g, [(f"a{f}", f % RING) for f in range(HB)] + [(f"y{j}", 4 + j) for j in range(TC)])
        lo_made, y_part = g.ev("h_lo_made", HB), g.ev("h_used", HB - 1)
        with nc.Block() as block:
            @block.sync
            def _(sp):
                with sp.Fori(1, E8) as e:
                    sp.wait_ge(*split.at(e, 0))
                    es = ds(e, 1)
                    sp.dma_start(w1f[:], W1[es].rearrange("a (k p) n -> p (a k) n", p=P)).then_inc(w_in.sem, 16)
                    sp.dma_start(w2f[:], W2[es].rearrange("a (k p) n -> p (a k) n", p=P)).then_inc(w_in.sem, 16)

            @block.gpsimd
            def _(pool):
                with pool.Fori(0, E8 // 2 - 1) as i:
                    pool.wait_ge(*used[1].at(i, 0))
                    split_hi(pool, 1, i * 2 + 1)
                    split_lo(pool, 1, i * 2 + 1)
                    pool.wait_ge(*used[0].at(i, 1))
                    split_hi(pool, 0, i * 2 + 2)
                    split_lo(pool, 0, i * 2 + 2)
                pool.wait_ge(*used[1].at(E8 // 2 - 1, 0))
                split_hi(pool, 1, E8 - 1)
                split_lo(pool, 1, E8 - 1)

            @block.tensor
            def _(pe):
                with pe.Fori(0, E8 // 2) as i:
                    for s in range(2):
                        with pe.Fori(0, NC) as c:
                            pe.wait_ge(*split.at(i * 2 + s, 1))
                            it = (i * 2 + s) * NC + c

                            def hidden(f):
                                pe.wait_ge(*bk.free(f"a{f}", it))
                                n = 0
                                for k in range(KD):
                                    for a, b in PASSES:
                                        ins = pe.matmul(g.bk(f % RING), w1s[s][a][:, k, f * P:(f + 1) * P], zTs[b][:, k, ds(c * CH, CH)],
                                                        start=n == 0, stop=n == 3 * KD - 1)
                                        n += 1
                                ins.then_inc(bk.fill(f"a{f}"), 1)

                            def output(f):
                                pe.wait_ge(*lo_made.at(it, f + 1))
                                for j in range(TC):
                                    if f == 0:
                                        pe.wait_ge(*bk.free(f"y{j}", it))
                                    for n, (a, b) in enumerate(PASSES):
                                        ins = pe.matmul(g.bk(4 + j)[:, 0:D], hs[a][:, f % RING, j * P:(j + 1) * P], w2s[s][b][:, f, :],
                                                        start=f == 0 and n == 0, stop=f == HB - 1 and n == 2)
                                    if f == HB - 1:
                                        ins.then_inc(bk.fill(f"y{j}"), 1)
                                if f < HB - 1:
                                    ins.then_inc(y_part.sem, 1)

                            for f in range(HB):
                                hidden(f)
                                if f >= 2:
                                    output(f - 2)
                            output(HB - 2)
                            output(HB - 1)

            @block.scalar
            def _(act):
                with act.Fori(0, E8) as e:
                    with act.Fori(0, NC) as c:
                        it = e * NC + c
                        for f in range(HB):
                            act.wait_ge(*bk.full(f"a{f}", it))
                            if f >= RING:
                                act.wait_ge(*y_part.at(it, f - RING + 1))
                            else:
                                act.wait_ge(*bk.free(f"y{TC - 1}", it))
                            act.activation(hs[0][:, f % RING, :], g.bk(f % RING), ACT.Silu)
                            act.activation(hf[:, f % RING, :], g.bk(f % RING), ACT.Silu).then_inc(bk.release(f"a{f}"), 1)

            @block.vector
            def _(dve):
                with dve.Fori(0, E8 // 2) as i:
                    for s in range(2):
                        with dve.Fori(0, NC) as c:
                            e = i * 2 + s
                            it = e * NC + c
                            for f in range(HB):
                                dve.wait_ge(*bk.read(f"a{f}", it))
                                dve.tensor_tensor(hs[1][:, f % RING, :], hf[:, f % RING, :], hs[0][:, f % RING, :].bitcast(F32), ALU.subtract)\
                                    .then_inc(lo_made.sem, 1)
                            for j in range(TC):
                                t = ds(c * TC + j, 1)
                                xt = g.x[:, t, :].rearrange("p a b -> p (a b)")
                                dve.wait_ge(*bk.full(f"y{j}", it))
                                dve.scalar_tensor_tensor(xt, g.bk(4 + j)[:, 0:D], wd[:, t, ds(e, 1)].rearrange("p a b -> p (a b)"),
                                                         xt, ALU.mult, ALU.add).then_inc(bk.release(f"y{j}"), 1)
                        dve.wait_ge(*bk.read(f"y{TC - 1}", (i * 2 + s) * NC + NC - 1))
                        dve.sem_inc(used[s].sem, 1)
        bk.end(E8 * NC)
        for e in (w_in, split, wstep):
            e.end(E8)
        for e in used:
            e.end(E8 // 2)
        for e in (lo_made, y_part):
            e.end(E8 * NC)


def stage_l2_attn(g, Wq, Wk, Wv, bq, bk_, bv, Wo, bo, gamma, beta, causal, own):
    nc = g.nc
    NH, HD, VW, G = 16, 16, 17, 4
    GW = G * VW
    FE = 1e-4
    with ExitStack() as ctx:
        sb = lambda n, s: g.sb(ctx, n, s)
        out = sb("attn_out", [P, NT, D])
        with ExitStack() as inner:
            sb = lambda n, s: g.sb(inner, n, s)
            wq, wk, wv, wo = sb("wq", [P, KD, 512]), sb("wk", [P, KD, 512]), sb("wv", [P, KD, D]), sb("wo", [P, KD, D])
            cq, ck, rv, ro = sb("cq", [P, G]), sb("ck", [P, G]), sb("rv", [P, D]), sb("ro", [P, D])
            ceq = sb("ceq", [P, 2, G])
            cau, ownm = sb("cau", [P, P]), sb("ownm", [P, G * GW])
            z4, zT = sb("z4", [P, TC, D]), sb("zT", [P, KD, CH])
            q, k_, pos = sb("q", [P, G, CH]), sb("k_", [P, G, CH]), sb("pos", [P, 2, CH])
            v1 = [sb(f"v1_{i}", [P, NH, VW]) for i in range(2)]
            ktok = sb("ktok", [P, 512])
            am = sb("am", [P, NH, P])
            st, dst_ = sb("state", [P, G * GW]), sb("state_new", [P, G * GW])
            den, o, oT = sb("den", [P, NH]), sb("o", [P, NH, HD]), sb("oT", [P, D])
            fills = [("t0", 4), ("t1", 5)] + [(f"{n}{f}", f) for n in "kq" for f in range(G)]
            for j in range(TC):
                fills += [(f"v_{j}", 4), (f"kt_{j}", 5)] + [(f"a{f}_{j}", f) for f in range(G)]
                fills += [(f"s_{j}", 7), (f"o_{j}", 6), (f"ot_{j}", 5), (f"w_{j}", 7)]
            bk = Banks(g, fills)
            w_in, ones_made = g.ev("w_loaded", 16 * 10), g.ev("ones_made", 1)
            z_made, exp_made = g.ev("z_made", 1), g.ev("exp_made", 2 * G)
            state_zero, state_made, o_made = g.ev("state_zero", 1), g.ev("state_made", TC), g.ev("o_made", TC)
            step = g.ev("dve_step", 2 * TC)
            qk_step = g.ev("qk_pos_made", 2 * G)
            NB = NC // B
            def load_weights(sp):
                for dst, src in ((cq, bq), (ck, bk_), (rv, bv), (ro, bo), (cau, causal), (ownm, own)):
                    load(sp, dst[:], src, w_in)
                for dst, src in ((wq, Wq), (wk, Wk), (wv, Wv), (wo, Wo)):
                    load(sp, dst[:], rows(src), w_in)

            ln_block(g, load_weights)
            with nc.Block() as block:
                @block.tensor
                def _(pe):
                    pe.wait_ge(*w_in.at(0, 160))
                    pe.wait_ge(*ones_made.at(0, 1))
                    with pe.Fori(0, B) as b, pe.Fori(0, NB) as hh:
                        c = b * NB + hh
                        pe.wait_ge(*z_made.at(c, 1))
                        turn(g, pe, bk, c, ("t0", "t1"), z4)
                        pe.wait_ge(*bk.read("t0", c))
                        pe.wait_ge(*bk.read("t1", c))
                        for n, w in (("k", wk), ("q", wq)):
                            for f in range(G):
                                pe.wait_ge(*bk.free(f"{n}{f}", c))
                                for k in range(KD):
                                    ins = pe.matmul(g.bk(f), w[:, k, f * P:(f + 1) * P], zT[:, k, :], start=k == 0, stop=k == KD - 1)
                                ins.then_inc(bk.fill(f"{n}{f}"), 1)
                        for j in range(TC):
                            tile = slice(j * P, (j + 1) * P)
                            pe.wait_ge(*bk.free(f"v_{j}", c))
                            for k in range(KD):
                                ins = pe.matmul(g.bk(4)[:, 0:D], zT[:, k, tile], wv[:, k, :], start=k == 0, stop=k == KD - 1)
                            ins.then_inc(bk.fill(f"v_{j}"), 1)
                            pe.wait_ge(*bk.read("k3", c))
                            pe.wait_ge(*bk.free(f"kt_{j}", c))
                            for f in range(G):
                                ins = pe.transpose(g.bk(5)[:, f * P:(f + 1) * P], k_[:, f, tile], g.ident[:])
                            ins.then_inc(bk.fill(f"kt_{j}"), 1)
                            pe.wait_ge(*bk.read("q3", c))
                            for h in range(G):
                                pe.wait_ge(*bk.free(f"a{h}_{j}", c))
                            for f in range(G):
                                for h in range(G):
                                    r = slice(32 * h, 32 * h + HD)
                                    ins = pe.matmul(g.bk(h)[:, f * P:(f + 1) * P], k_[r, f, tile], q[r, f, tile], start=True, stop=True)
                                    if f == G - 1:
                                        ins.then_inc(bk.fill(f"a{h}_{j}"), 1)
                            pe.wait_ge(*bk.read(f"v_{j}", c))
                            pe.wait_ge(*bk.read(f"kt_{j}", c))
                            pe.wait_ge(*bk.free(f"s_{j}", c))
                            for f in range(G):
                                ins = pe.matmul(g.bk(7)[:, f * GW:(f + 1) * GW], ktok[:, f * P:(f + 1) * P],
                                                v1[j % 2][:, f * G:(f + 1) * G, :].rearrange("p a b -> p (a b)"), start=True, stop=True)
                            ins.then_inc(bk.fill(f"s_{j}"), 1)
                            pe.wait_ge(*state_made.at(c, j))
                            pe.wait_ge(*state_zero.at(b, 1))
                            pe.wait_ge(*bk.free(f"o_{j}", c))
                            for f in range(G):
                                pe.matmul(g.bk(6)[:, f * GW:(f + 1) * GW], q[:, f, tile], st[:, f * GW:(f + 1) * GW],
                                          start=True, stop=False, skip_group_check=True)
                                if f == 0:
                                    for h in range(G):
                                        pe.wait_ge(*bk.read(f"a{h}_{j}", c))
                                for h in range(G):
                                    o0 = (f * G + h) * VW
                                    ins = pe.matmul(g.bk(6)[:, o0:o0 + VW], am[:, f * G + h, :], v1[j % 2][:, f * G + h, :],
                                                    start=False, stop=True, skip_group_check=True)
                            ins.then_inc(bk.fill(f"o_{j}"), 1)
                            pe.wait_ge(*o_made.at(c, j + 1))
                            pe.wait_ge(*bk.free(f"ot_{j}", c))
                            for k in range(KD):
                                ins = pe.transpose(g.bk(5)[:, k * P:(k + 1) * P],
                                                   o[:, k * 8:(k + 1) * 8, :].rearrange("p a b -> p (a b)"), g.ident[:])
                            ins.then_inc(bk.fill(f"ot_{j}"), 1)
                            pe.wait_ge(*bk.read(f"ot_{j}", c))
                            pe.wait_ge(*bk.free(f"w_{j}", c))
                            for k in range(KD):
                                ins = pe.matmul(g.bk(7)[:, 0:D], oT[:, k * P:(k + 1) * P], wo[:, k, :], start=k == 0, stop=k == KD - 1)
                            ins.then_inc(bk.fill(f"w_{j}"), 1)

                @block.scalar
                def _(act):
                    act.wait_ge(*w_in.at(0, 160))
                    with act.Fori(0, NC) as c:
                        act.wait_ge(*bk.full("t0", c))
                        act.activation(zT[:, 0, :], g.bk(4), ACT.Copy).then_inc(bk.release("t0"), 1)
                        for n, dst, bias in (("k", k_, ck), ("q", q, cq)):
                            for f in range(G):
                                act.wait_ge(*bk.full(f"{n}{f}", c))
                                act.activation(dst[:, f, :], g.bk(f), ACT.Exp, bias=bias[:, f:f + 1]).then_inc(exp_made.sem, 1)
                        for j in range(TC):
                            act.wait_ge(*bk.full(f"kt_{j}", c))
                            act.activation(ktok[:], g.bk(5), ACT.Copy).then_inc(bk.release(f"kt_{j}"), 1)
                            act.wait_ge(*bk.full(f"ot_{j}", c))
                            act.activation(oT[:], g.bk(5)[:, 0:D], ACT.Copy).then_inc(bk.release(f"ot_{j}"), 1)

                @block.gpsimd
                def _(pool):
                    with pool.Fori(0, B) as b:
                        pool.memset(st[:], 0.0).then_inc(state_zero.sem, 1)
                        with pool.Fori(0, NB) as hh:
                            c = b * NB + hh
                            for j in range(TC):
                                pool.wait_ge(*state_zero.at(b, 1))
                                pool.wait_ge(*bk.read(f"s_{j}", c))
                                pool.wait_ge(*bk.full(f"o_{j}", c))
                                pool.tensor_tensor(st[:], st[:], dst_[:], ALU.add).then_inc(state_made.sem, 1)
                                pool.wait_ge(*state_made.at(c, j + 1))

                @block.vector
                def _(dve):
                    dve.memset(v1[0][:, :, HD:VW], 1.0)
                    dve.memset(v1[1][:, :, HD:VW], 1.0)
                    dve.wait_ge(*w_in.at(0, 160))
                    dve.tensor_scalar(ceq[:, 0, :], ck[:], FE, None, ALU.add)
                    dve.tensor_scalar(ceq[:, 1, :], cq[:], FE, None, ALU.add).then_inc(ones_made.sem, 1)
                    dve.wait_ge(*ones_made.at(0, 1))
                    with dve.Fori(0, NC) as c:
                        link = Chain(dve, step, c)
                        normalise(g, dve, c, z4).then_inc(z_made.sem, 1)
                        dve.wait_ge(*bk.full("t1", c))
                        dve.tensor_scalar(zT[:, 1, :], g.bk(5), 1.0, None, ALU.mult).then_inc(bk.release("t1"), 1)
                        for i, (n, dst) in enumerate((("k", k_), ("q", q))):
                            for f in range(G):
                                dve.wait_ge(*exp_made.at(c, i * G + f + 1))
                                dve.tensor_scalar(pos[:, f % 2, :], g.bk(f), ceq[:, i, f:f + 1], FE, ALU.add, ALU.max)\
                                    .then_inc(qk_step.sem, 1)
                                dve.wait_ge(*qk_step.at(c, i * G + f + 1))
                                dve.scalar_tensor_tensor(dst[:, f, :], dst[:, f, :], 1.0, pos[:, f % 2, :], ALU.min, ALU.add)\
                                    .then_inc(bk.release(f"{n}{f}"), 1)
                                dve.wait_ge(*bk.read(f"{n}{f}", c))
                        for j in range(TC):
                            dve.wait_ge(*bk.full(f"v_{j}", c))
                            dve.tensor_tensor(v1[j % 2][:, :, 0:HD], g.bk(4)[:, 0:D].rearrange("p (h d) -> p h d", d=HD),
                                              rv[:].rearrange("p (h d) -> p h d", d=HD), ALU.add).then_inc(bk.release(f"v_{j}"), 1)
                            for f in range(G):
                                dve.wait_ge(*bk.full(f"a{f}_{j}", c))
                                dve.tensor_tensor(am[:, f::G, :], g.bk(f).rearrange("p (h q) -> p h q", q=P),
                                                  cau[:].unsqueeze(1).broadcast_to([P, G, P]), ALU.mult)\
                                    .then_inc(bk.release(f"a{f}_{j}"), 1)
                            dve.wait_ge(*bk.full(f"s_{j}", c))
                            dve.wait_ge(*state_made.at(c, j))
                            dve.tensor_tensor(dst_[:], g.bk(7)[:, 0:G * GW], ownm[:], ALU.mult).then_inc(bk.release(f"s_{j}"), 1)
                            dve.wait_ge(*bk.full(f"o_{j}", c))
                            ov = g.bk(6)[:, 0:NH * VW].rearrange("p (h e) -> p h e", e=VW)
                            link(dve.tensor_scalar(den[:], ov[:, :, HD], 4.0 * FE, None, ALU.add))
                            link(dve.reciprocal(den[:], den[:]))
                            dve.tensor_tensor(o[:], ov[:, :, 0:HD], den[:].unsqueeze(2).broadcast_to([P, NH, HD]), ALU.mult)\
                                .then_inc(bk.release(f"o_{j}"), 1)
                            dve.wait_ge(*bk.read(f"o_{j}", c))
                            dve.sem_inc(o_made.sem, 1)
                            dve.wait_ge(*bk.full(f"w_{j}", c))
                            dve.tensor_tensor(out[:, ds(c * TC + j, 1), :].rearrange("p a b -> p (a b)"), g.bk(7)[:, 0:D], ro[:], ALU.add)\
                                .then_inc(bk.release(f"w_{j}"), 1)
                        link.close()
            bk.end(NC)
            for e in (w_in, ones_made):
                e.end()
            state_zero.end(B)
            for e in (z_made, exp_made, state_made, o_made, step, qk_step):
                e.end(NC)

        sb = lambda n, s: g.sb(ctx, n, s)
        rg, rb = sb("rg", [P, D]), sb("rb", [P, D])
        g.ev_bn = g.ev("bn_stats_done", 1)
        spread, rooted, step = g.ev("ln_variance", 1), g.ev("ln_root", 1), g.ev("dve_step", LN_LINKS)
        w_in = g.ev("w_loaded", 32)
        with nc.Block() as block:
            @block.sync
            def _(sp):
                load(sp, rg[:], gamma, w_in)
                load(sp, rb[:], beta, w_in)

            @block.gpsimd
            def _(pool):
                pool.wait_ge(*w_in.at(0, 32))
                for c in range(NC):
                    xt = g.x[:, c * TC:(c + 1) * TC, :]
                    pool.tensor_tensor(xt, xt, rb[:].unsqueeze(1).broadcast_to([P, TC, D]), ALU.add)

            @block.vector
            def _(dve):
                link = Chain(dve, step, 0)
                ln_stats_vector(g, dve, out, NT, spread, rooted, link)
                link.close()

            @block.scalar
            def _(act):
                ln_stats_scalar(g, act, NT, spread, rooted)
        for e in (g.ev_bn, spread, rooted, step, w_in):
            e.end()
        normed, scaled = g.ev("out_normed", NC), g.ev("out_scaled", NC)
        with nc.Block() as block:
            @block.vector
            def _(dve):
                chunk = lambda a, c: a[:, c * TC:(c + 1) * TC, :]
                for t in range(NT):
                    ins = dve.tensor_scalar(out[:, t, :], out[:, t, :], g.mean[:, t:t + 1], g.rstd[:, t:t + 1], ALU.subtract, ALU.mult)
                    if t % TC == TC - 1:
                        ins.then_inc(normed.sem, 1)
                for c in range(NC):
                    dve.wait_ge(*normed.at(0, c + 1))
                    dve.tensor_tensor(chunk(out, c), chunk(out, c), rg[:].unsqueeze(1).broadcast_to([P, TC, D]), ALU.mult)\
                        .then_inc(scaled.sem, 1)
                for c in range(NC):
                    dve.wait_ge(*scaled.at(0, c + 1))
                    dve.tensor_tensor(chunk(g.x, c), chunk(g.x, c), chunk(out, c), ALU.add)
        for e in (normed, scaled):
            e.end()


def stage_l2_ffn(g, W, gu, V):
    nc = g.nc
    E, R = 8, 16
    with ExitStack() as ctx:
        sb = lambda n, s: g.sb(ctx, n, s)
        w, gus, v = sb("w", [P, KD, D]), sb("gus", [P, KD, E + E * R]), sb("v", [P, D])
        z4, zT = sb("z4", [P, TC, D]), sb("zT", [P, KD, CH])
        t, gate, mx = sb("t", [P, TC, E * R]), sb("gate", [P, TC, E]), sb("mx", [P, TC])
        tT = sb("tT", [P, CH])
        bk = Banks(g, [("t0", 0), ("t1", 1), ("p0", 2), ("p1", 3), ("p2", 4), ("p3", 5), ("tT", 6)]
                   + [(f"y{j}", [7, 0, 1, 2][j]) for j in range(TC)])
        w_in, z_made, step = g.ev("w_loaded", 48), g.ev("z_made", 1), g.ev("dve_step", 5)
        logit, expd, t_made = g.ev("logit_made", 1), g.ev("exp_made", 1), g.ev("t_made", 1)
        def load_weights(sp):
            load(sp, gus[:], rows(gu), w_in)
            load(sp, w[:], rows(W), w_in)
            load(sp, v[:], V, w_in)

        ln_block(g, load_weights)
        with nc.Block() as block:
            @block.tensor
            def _(pe):
                pe.wait_ge(*w_in.at(0, 48))
                with pe.Fori(0, NC) as c:
                    pe.wait_ge(*z_made.at(c, 1))
                    turn(g, pe, bk, c, ("t0", "t1"), z4)
                    pe.wait_ge(*bk.read("t0", c))
                    pe.wait_ge(*bk.read("t1", c))
                    for j in range(TC):
                        pe.wait_ge(*bk.free(f"p{j}", c))
                        for k in range(KD):
                            ins = pe.matmul(g.bk(2 + j)[:, 0:E + E * R], zT[:, k, j * P:(j + 1) * P], gus[:, k, :],
                                            start=k == 0, stop=k == KD - 1)
                        ins.then_inc(bk.fill(f"p{j}"), 1)
                    pe.wait_ge(*t_made.at(c, 1))
                    pe.wait_ge(*bk.free("tT", c))
                    for j in range(TC):
                        ins = pe.transpose(g.bk(6)[:, j * P:(j + 1) * P], t[:, j, :], g.ident[:])
                    ins.then_inc(bk.fill("tT"), 1)
                    for j in range(TC):
                        b = bk.bank[f"y{j}"]
                        pe.wait_ge(*bk.free(f"y{j}", c))
                        for k in range(KD):
                            pe.matmul(g.bk(b)[:, 0:D], zT[:, k, j * P:(j + 1) * P], w[:, k, :], start=k == 0, stop=False)
                        pe.wait_ge(*bk.read("tT", c))
                        pe.matmul(g.bk(b)[:, 0:D], tT[:, j * P:(j + 1) * P], v[:], start=False, stop=True)\
                            .then_inc(bk.fill(f"y{j}"), 1)

            @block.scalar
            def _(act):
                with act.Fori(0, NC) as c:
                    act.wait_ge(*bk.full("t0", c))
                    act.activation(zT[:, 0, :], g.bk(0), ACT.Copy).then_inc(bk.release("t0"), 1)
                    act.wait_ge(*logit.at(c, 1))
                    act.activation(gate[:], gate[:], ACT.Exp).then_inc(expd.sem, 1)
                    act.wait_ge(*bk.full("tT", c))
                    act.activation(tT[:], g.bk(6), ACT.Copy).then_inc(bk.release("tT"), 1)

            @block.vector
            def _(dve):
                with dve.Fori(0, NC) as c:
                    link = Chain(dve, step, c)
                    normalise(g, dve, c, z4).then_inc(z_made.sem, 1)
                    dve.wait_ge(*bk.full("t1", c))
                    dve.tensor_scalar(zT[:, 1, :], g.bk(1), 1.0, None, ALU.mult).then_inc(bk.release("t1"), 1)
                    for j in range(TC):
                        dve.wait_ge(*bk.full(f"p{j}", c))
                    lg = g.ps[:, 2:6, 0:E]
                    link(dve.tensor_reduce(mx[:], lg, AXX, ALU.max))
                    dve.tensor_tensor(gate[:], lg, mx[:].unsqueeze(2).broadcast_to([P, TC, E]), ALU.subtract)\
                        .then_inc(logit.sem, 1)
                    dve.wait_ge(*expd.at(c, 1))
                    link(dve.tensor_reduce(mx[:], gate[:], AXX, ALU.add))
                    link(dve.reciprocal(mx[:], mx[:]))
                    link(dve.tensor_scalar(mx[:], mx[:], 1.0 / R, None, ALU.mult))
                    link(dve.tensor_tensor(gate[:], gate[:], mx[:].unsqueeze(2).broadcast_to([P, TC, E]), ALU.mult))
                    for j in range(TC):
                        dve.tensor_tensor(t[:, j, :].rearrange("p (e r) -> p e r", r=R),
                                          g.bk(2 + j)[:, E:E + E * R].rearrange("p (e r) -> p e r", r=R),
                                          gate[:, j, :].unsqueeze(2).broadcast_to([P, E, R]), ALU.mult)\
                            .then_inc(bk.release(f"p{j}"), 1)
                    for j in range(TC):
                        dve.wait_ge(*bk.read(f"p{j}", c))
                    dve.sem_inc(t_made.sem, 1)
                    for j in range(TC):
                        dve.wait_ge(*bk.full(f"y{j}", c))
                        xt = g.x[:, ds(c * TC + j, 1), :].rearrange("p a b -> p (a b)")
                        dve.tensor_tensor(xt, xt, g.bk(bk.bank[f"y{j}"])[:, 0:D], ALU.add).then_inc(bk.release(f"y{j}"), 1)
                    link.close()
        bk.end(NC)
        w_in.end()
        for e in (z_made, step, logit, expd, t_made):
            e.end(NC)


def stage_l3_ffn(g, W, out):
    nc = g.nc
    with ExitStack() as ctx:
        sb = lambda n, s: g.sb(ctx, n, s)
        w, z4, zT = sb("w", [P, KD, D]), sb("z4", [P, TC, D]), sb("zT", [P, KD, CH])
        bk = Banks(g, [("t0", 0), ("t1", 1)] + [(f"y{j}", 2 + j) for j in range(TC)])
        w_in, signed, z_made, stored = g.ev("w_loaded", 16), g.ev("sign_made", 1), g.ev("z_made", 1), g.ev("out_stored", 16)
        out_t = out.rearrange("b (t p) d -> p (b t) d", p=P)
        def load_weights(sp):
            load(sp, w[:], rows(W), w_in)

        ln_block(g, load_weights)
        with nc.Block() as block:
            @block.sync
            def _(sp):
                with sp.Fori(0, NC) as c:
                    sp.wait_ge(*bk.read(f"y{TC - 1}", c))
                    t = ds(c * TC, TC)
                    sp.dma_start(out_t[:, t, :], g.x[:, t, :]).then_inc(stored.sem, 16)
                sp.wait_ge(*stored.at(NC - 1, 16))

            @block.tensor
            def _(pe):
                pe.wait_ge(*signed.at(0, 1))
                with pe.Fori(0, NC) as c:
                    pe.wait_ge(*z_made.at(c, 1))
                    turn(g, pe, bk, c, ("t0", "t1"), z4)
                    pe.wait_ge(*bk.read("t0", c))
                    pe.wait_ge(*bk.read("t1", c))
                    for j in range(TC):
                        pe.wait_ge(*bk.free(f"y{j}", c))
                        for k in range(KD):
                            ins = pe.matmul(g.bk(2 + j)[:, 0:D], zT[:, k, j * P:(j + 1) * P], w[:, k, :], start=k == 0, stop=k == KD - 1)
                        ins.then_inc(bk.fill(f"y{j}"), 1)

            @block.scalar
            def _(act):
                act.wait_ge(*w_in.at(0, 16))
                act.activation(w[:], w[:], ACT.Sign).then_inc(signed.sem, 1)
                with act.Fori(0, NC) as c:
                    act.wait_ge(*bk.full("t0", c))
                    act.activation(zT[:, 0, :], g.bk(0), ACT.Copy).then_inc(bk.release("t0"), 1)

            @block.vector
            def _(dve):
                with dve.Fori(0, NC) as c:
                    normalise(g, dve, c, z4).then_inc(z_made.sem, 1)
                    dve.wait_ge(*bk.full("t1", c))
                    dve.tensor_scalar(zT[:, 1, :], g.bk(1), 1.0, None, ALU.mult).then_inc(bk.release("t1"), 1)
                    for j in range(TC):
                        dve.wait_ge(*bk.full(f"y{j}", c))
                        xt = g.x[:, ds(c * TC + j, 1), :].rearrange("p a b -> p (a b)")
                        dve.tensor_tensor(xt, xt, g.bk(2 + j)[:, 0:D], ALU.add).then_inc(bk.release(f"y{j}"), 1)
        bk.end(NC)
        for e in (w_in, signed):
            e.end()
        for e in (z_made, stored):
            e.end(NC)


def stage_l3_attn(g, DQ, UQ, DKV, UKV, QR, KR, same_head, norm_w, WO, neg):
    nc = g.nc
    NH, HD, G = 16, 16, 4
    ST = S // P
    NB = NC // B
    EPS = 1.1920929e-07
    with ExitStack() as ctx:
        sb = lambda n, s, dt=F32: g.sb(ctx, n, s, dt)
        NB2 = NH // 2
        qT_all, kT_all = sb("qT_all", [P, B * NB2, S], F32R), sb("kT_all", [P, B * NB2, S], F32R)
        v_all = sb("v_all", [P, NT, NH, HD + 1])

        with ExitStack() as inner:
            sb = lambda n, s, dt=F32: g.sb(inner, n, s, dt)
            dq, uq = sb("dq", [P, P]), sb("uq", [P, P])
            dkv, ukv = sb("dkv", [P, 2, P]), sb("ukv", [P, 2, 2 * P])
            kr, qr = sb("kr", [64, P]), sb("qr", [64, P])
            same, nw = sb("same", [P, P]), sb("nw", [P, 2 * P])
            w = sb("w", [P, 4 * P])
            z4, zT = sb("z4", [P, TC, D]), sb("zT", [P, KD, CH])
            sq, ss = sb("sq", [P, 2, 2 * P]), sb("ss", [P, 2, 16])
            qk = sb("qk", [P, 2, 2 * P])
            qf, kf = sb("qf", [P, NH, HD]), sb("kf", [P, NH, HD])
            qp, kp = sb("qp", [P, NH, 4, HD]), sb("kp", [P, NH, 4, HD])
            qh, kh = sb("qh", [P, NH, HD], F32R), sb("kh", [P, NH, HD], F32R)
            bk = Banks(g, [("wq", 0), ("wkv", 1), ("wr", 2)])
            w_in, w_made = g.ev("w_loaded", 16 * 8), g.ev("maps_made", 1)
            def load_weights(sp):
                for dst, src in ((dq, DQ), (uq, UQ), (kr, KR), (qr, QR), (same, same_head), (nw, norm_w)):
                    load(sp, dst[:], src, w_in)
                for dst, src in ((dkv, DKV), (ukv, UKV)):
                    load(sp, dst[:], rows(src), w_in)

            ln_block(g, load_weights)
            with nc.Block() as block:
                @block.tensor
                def _(pe):
                    pe.wait_ge(*w_in.at(0, 128))
                    pe.wait_ge(*bk.free("wq", 0))
                    pe.matmul(g.bk(0)[:, 0:P], dq[:], uq[:], start=True, stop=True).then_inc(bk.fill("wq"), 1)
                    pe.wait_ge(*bk.free("wkv", 0))
                    for k in range(2):
                        ins = pe.matmul(g.bk(1)[:, 0:2 * P], dkv[:, k, :], ukv[:, k, :], start=k == 0, stop=k == 1)
                    ins.then_inc(bk.fill("wkv"), 1)
                    pe.wait_ge(*bk.free("wr", 0))
                    pe.matmul(g.bk(2)[:, 0:P], kr[:], qr[:], start=True, stop=True).then_inc(bk.fill("wr"), 1)

                @block.gpsimd
                def _(pool):
                    pool.memset(qp[:], 0.0)
                    pool.memset(kp[:], 0.0)
                    pool.memset(v_all[:], 0.0).then_inc(w_made.sem, 1)
                    pool.wait_ge(*w_made.at(0, 1))
                    pool.memset(kp[:, :, 3, 0:1], 1.0)
                    pool.memset(v_all[:, :, :, HD:HD + 1], 1.0)

                @block.vector
                def _(dve):
                    dve.wait_ge(*w_in.at(0, 128))
                    same2 = same[:].unsqueeze(1).broadcast_to([P, 2, P])
                    dve.wait_ge(*bk.full("wq", 0))
                    dve.tensor_tensor(w[:, 0:P], g.bk(0)[:, 0:P], same[:], ALU.mult).then_inc(bk.release("wq"), 1)
                    dve.wait_ge(*bk.full("wkv", 0))
                    dve.tensor_tensor(w[:, P:3 * P].rearrange("p (a n) -> p a n", a=2), g.bk(1)[:, 0:2 * P].rearrange("p (a n) -> p a n", a=2),
                                      same2, ALU.mult).then_inc(bk.release("wkv"), 1)
                    dve.wait_ge(*bk.full("wr", 0))
                    dve.tensor_tensor(w[:, 3 * P:], g.bk(2)[:, 0:P], same[:], ALU.mult).then_inc(bk.release("wr"), 1)
            bk.end()
            w_in.end()
            w_made.end()

            fills = [("t0", 0), ("t1", 1)]
            for j in range(TC):
                fills += [(f"p{j}_0", 2 + 2 * (j % 2)), (f"p{j}_1", 3 + 2 * (j % 2))] + [(f"{s}{j}_{a}", 6 + a) for s in "qk" for a in range(2)]
            bk = Banks(g, fills)
            z_made, sq_made, root_made = g.ev("z_made", 1), g.ev("sq_made", TC), g.ev("root_made", TC)
            padded, step, ss_made = g.ev("padded_made", TC), g.ev("dve_step", 3 * TC), g.ev("ss_made", TC)
            qk_made = g.ev("qk_made", TC)
            with nc.Block() as block:
                @block.tensor
                def _(pe):
                    def turn_qk(c, j):
                        pe.wait_ge(*padded.at(c, j + 1))
                        for s, src in (("q", qp), ("k", kp)):
                            for a in range(2):
                                name = f"{s}{j}_{a}"
                                pe.wait_ge(*bk.free(name, c))
                                for f in range(4):
                                    h = 8 * a + 2 * f
                                    ins = pe.transpose(g.bk(bk.bank[name])[:, f * P:(f + 1) * P],
                                                       src[:, h:h + 2].rearrange("p a b d -> p (a b d)"), g.ident[:])
                                ins.then_inc(bk.fill(name), 1)

                    with pe.Fori(0, NC) as c:
                        pe.wait_ge(*z_made.at(c, 1))
                        turn(g, pe, bk, c, ("t0", "t1"), z4)
                        pe.wait_ge(*bk.read("t0", c))
                        pe.wait_ge(*bk.read("t1", c))
                        for j in range(TC):
                            for k in range(KD):
                                pe.wait_ge(*bk.free(f"p{j}_{k}", c))
                                pe.matmul(g.bk(bk.bank[f"p{j}_{k}"]), zT[:, k, j * P:(j + 1) * P], w[:], start=True, stop=True)\
                                    .then_inc(bk.fill(f"p{j}_{k}"), 1)
                            if j:
                                turn_qk(c, j - 1)
                        turn_qk(c, TC - 1)

                @block.scalar
                def _(act):
                    def keep_qk(b, hh, c, j):
                        t = ds(hh * CH + j * P, P)
                        for s, dst in (("q", qT_all), ("k", kT_all)):
                            for a in range(2):
                                name = f"{s}{j}_{a}"
                                act.wait_ge(*bk.full(name, c))
                                act.activation(dst[:, ds(b * NB2 + 4 * a, 4), t], g.bk(bk.bank[name]).rearrange("p (f n) -> p f n", n=P),
                                               ACT.Copy).then_inc(bk.release(name), 1)

                    with act.Fori(0, B) as b, act.Fori(0, NB) as hh:
                        c = b * NB + hh
                        act.wait_ge(*bk.full("t0", c))
                        act.activation(zT[:, 0, :], g.bk(0), ACT.Copy).then_inc(bk.release("t0"), 1)
                        for j in range(TC):
                            for k in range(KD):
                                act.wait_ge(*bk.full(f"p{j}_{k}", c))
                            if j:
                                act.wait_ge(*ss_made.at(c, j))
                            p0 = bk.bank[f"p{j}_0"]
                            act.activation(sq[:], g.ps[:, p0:p0 + 2, 0:2 * P], ACT.Square).then_inc(sq_made.sem, 1)
                            act.wait_ge(*ss_made.at(c, j + 1))
                            act.activation(ss[:], ss[:], ACT.Sqrt, scale=1.0 / HD, bias=g.eps[:, 3:4]).then_inc(root_made.sem, 1)
                            if j:
                                keep_qk(b, hh, c, j - 1)
                        keep_qk(b, hh, c, TC - 1)

                @block.vector
                def _(dve):
                    with dve.Fori(0, NC) as c:
                        link = Chain(dve, step, c)
                        normalise(g, dve, c, z4).then_inc(z_made.sem, 1)
                        dve.wait_ge(*bk.full("t1", c))
                        dve.tensor_scalar(zT[:, 1, :], g.bk(1), 1.0, None, ALU.mult).then_inc(bk.release("t1"), 1)
                        for j in range(TC):
                            p0 = bk.bank[f"p{j}_0"]
                            pj = g.ps[:, p0:p0 + 2, :]
                            heads = lambda a, n: a.rearrange("p k (h d) -> p k h d", d=HD)
                            dve.wait_ge(*sq_made.at(c, j + 1))
                            dve.tensor_reduce(ss[:], heads(sq[:], 16), AXX, ALU.add).then_inc(ss_made.sem, 1)
                            t = ds(c * TC + j, 1)
                            dve.tensor_scalar(v_all[:, t, :, 0:HD].rearrange("p a (k h) d -> p (a k) h d", k=KD),
                                              heads(pj[:, :, 2 * P:3 * P], 8), 1.0, None, ALU.mult)
                            dve.wait_ge(*root_made.at(c, j + 1))
                            link(dve.reciprocal(ss[:], ss[:]))
                            for k in range(KD):
                                ins = dve.tensor_tensor(heads(qk[:], 16)[:, k], heads(pj[:, :, 0:2 * P], 16)[:, k],
                                                        ss[:, k].unsqueeze(2).broadcast_to([P, 2 * 8, HD]), ALU.mult)
                            ins.then_inc(qk_made.sem, 1)
                            dve.wait_ge(*qk_made.at(c, j + 1))
                            nwh = nw[:].rearrange("p (s h d) -> p s h d", s=2, d=HD)
                            qkh = qk[:].rearrange("p k (s h d) -> p k s h d", s=2, d=HD)
                            for k in range(KD):
                                hk = slice(k * 8, k * 8 + 8)
                                dve.tensor_tensor(qf[:, hk, :], qkh[:, k, 0], nwh[:, 0], ALU.mult)
                                ins = dve.tensor_tensor(kf[:, hk, :], qkh[:, k, 1], nwh[:, 1], ALU.mult)
                            link(ins)
                            dve.tensor_copy(qh[:], qf[:])
                            for k in range(KD):
                                hk = slice(k * 8, k * 8 + 8)
                                dve.tensor_tensor(kf[:, hk, :], kf[:, hk, :],
                                                  pj[:, k, 3 * P:].rearrange("p (h d) -> p h d", d=HD), ALU.add)\
                                    .then_inc(bk.release(f"p{j}_{k}"), 1)
                            for k in range(KD):
                                dve.wait_ge(*bk.read(f"p{j}_{k}", c))
                            link(dve.tensor_copy(kh[:], kf[:]))
                            if j:
                                dve.wait_ge(*bk.full(f"k{j - 1}_0", c))
                                dve.wait_ge(*bk.full(f"k{j - 1}_1", c))
                            split = lambda t: t[:].bitcast(F32)
                            dve.tensor_copy(qp[:, :, 0:2, :], split(qh).unsqueeze(2).broadcast_to([P, NH, 2, HD]))
                            dve.tensor_tensor(qp[:, :, 2, :], qf[:], split(qh), ALU.subtract)
                            dve.tensor_copy(kp[:, :, 0:3:2, :], split(kh).unsqueeze(2).broadcast_to([P, NH, 2, HD]))
                            dve.tensor_tensor(kp[:, :, 1, :], kf[:], split(kh), ALU.subtract).then_inc(padded.sem, 1)
                            dve.wait_ge(*padded.at(c, j + 1))
                        link.close()
            bk.end(NC)
            for ev in (z_made, sq_made, root_made, padded, step, ss_made, qk_made):
                ev.end(NC)

        sb = lambda n, s, dt=F32: g.sb(ctx, n, s, dt)
        qs, ks = sb("qs", [P, 2, S], F32R), sb("ks", [P, 2, S], F32R)
        vs = sb("vs", [P, ST, G, 32])
        ngq, ngk = sb("ngq", [P, P]), sb("ngk", [P, P])
        wo = sb("wo", [P, HD * G + G])
        mx, m4, nm = sb("mx", [P, ST, 2, G]), sb("m4", [P, TC, G]), sb("nm", [P, TC, G, 64])
        pT = sb("pT", [P, 4, 2, CH])
        oT, rec, y = sb("oT", [P, CH]), sb("rec", [P, 2, TC, G]), sb("y", [P, TC, HD * G])
        ps1 = [(i, half, pr) for i in range(ST) for half in range(i // TC + 1) for pr in range(2)]
        ps2 = [[(kt, pr) for kt in range((cc + 1) * TC) for pr in range(2)] for cc in range(2)]
        mp = [[p for p in ps1 if p[0] // TC == cc] for cc in range(2)]
        EARLY, AHEAD = 8, 3
        order = [("m", p) for p in mp[0]] + [("m", p) for p in mp[1][:EARLY]] + [("n", 0)]
        beside = [mp[1][EARLY + n:EARLY + n + 1] for n in range(len(ps2[0]))]
        assert sum(map(len, beside)) == len(mp[1]) - EARLY
        for cc in range(2):
            N = len(ps2[cc])
            order += [("s", (cc, n)) for n in range(AHEAD)] + ([("y", 0)] if cc else [])
            for n in range(N):
                order += [("s", (cc, n + AHEAD))] if n + AHEAD < N else []
                order.append(("v", (cc, n)))
                order += [("m", p) for p in beside[n]] if cc == 0 else []
            order.append(("y", 1) if cc else ("n", 1))
        fills, n, sets = [], 0, {}
        for kind, what in order:
            if kind in "ms":
                key = ("m",) + what if kind == "m" else (what[0],) + ps2[what[0]][what[1]]
                sets[key] = 2 * (n % 3)
                fills += [(f"{key}{a}", sets[key] + a) for a in range(2)]
                n += 1
            elif kind == "n":
                fills += [(f"n{what}_{pr}", 6) for pr in range(2)]
            elif kind == "y":
                fills.append((f"y{what}", 6))
        bk = Banks(g, fills)
        NP2 = [len(p) for p in ps2]
        first = [0, NP2[0]]
        w_in, nm_zero = g.ev("w_loaded", 48), g.ev("zeroed", 2)
        copied, v_copied = g.ev("head_copied", 2), g.ev("values_copied", 1)
        step = g.ev("dve_step", 2 * ST + 3)
        nm_made, masked = g.ev("negmax_made", 2), g.ev("diag_masked", 2 * ST)
        pv, o_read, added = g.ev("pv_done", sum(NP2)), g.ev("o_read", 2), g.ev("x_added", 2)
        with nc.Block() as block:
            @block.sync
            def _(sp):
                load(sp, ngq[:], neg[0], w_in)
                load(sp, ngk[:], neg[1], w_in)
                load(sp, wo[:], WO, w_in)

            @block.gpsimd
            def _(pool):
                pool.memset(nm[:], 0.0).then_inc(nm_zero.sem, 1)
                pool.memset(vs[:], 0.0).then_inc(nm_zero.sem, 1)
                pool.wait_ge(*nm_zero.at(0, 2))
                with pool.Fori(0, B) as b, pool.Fori(0, G) as f:
                    it = b * G + f
                    pool.wait_ge(*pv.at(it, 0))
                    pool.tensor_copy(vs[:, :, :, 0:HD + 1], v_all[:, ds(b * ST, ST), ds(f * G, G), :]).then_inc(v_copied.sem, 1)
                    for cc in range(2):
                        pool.wait_ge(*bk.read(f"y{cc}", it))
                        xt = g.x[:, ds(b * ST + cc * TC, TC), ds(f * (G * HD), G * HD)]
                        pool.tensor_tensor(xt, xt, y[:], ALU.add).then_inc(added.sem, 1)

            @block.tensor
            def _(pe):
                def max_piece(it, i, half, pr):
                    key = ("m", i, half, pr)
                    wd = min(CH, (i + 1) * P - half * CH)
                    for a in range(2):
                        pe.wait_ge(*bk.free(f"{key}{a}", it))
                        r = slice(64 * a, 64 * a + 64)
                        pe.matmul(g.bk(sets[key] + a)[:, 0:wd], qs[r, pr, i * P:(i + 1) * P], ks[r, pr, half * CH:half * CH + wd],
                                  start=True, stop=True).then_inc(bk.fill(f"{key}{a}"), 1)

                def score_piece(it, cc, kt, pr):
                    key = (cc, kt, pr)
                    lo = max(0, kt * P - cc * CH)
                    for a in range(2):
                        pe.wait_ge(*bk.free(f"{key}{a}", it))
                        r = slice(64 * a, 64 * a + 64)
                        pe.matmul(g.bk(sets[key] + a)[:, lo:CH], ks[r, pr, kt * P:(kt + 1) * P], qs[r, pr, cc * CH + lo:(cc + 1) * CH],
                                  start=True, stop=True).then_inc(bk.fill(f"{key}{a}"), 1)

                def value_piece(it, cc, n):
                    kt, pr = ps2[cc][n]
                    lo = max(0, kt * P - cc * CH)
                    pe.wait_ge(*bk.read(f"{(cc, kt, pr)}0", it))
                    pe.wait_ge(*bk.read(f"{(cc, kt, pr)}1", it))
                    if n == 0:
                        pe.wait_ge(*v_copied.at(it, 1))
                        pe.wait_ge(*o_read.at(it, cc))
                    for a in range(2):
                        h = 2 * pr + a
                        ins = pe.matmul(g.bk(7)[32 * h:32 * h + 32, lo:CH], vs[:, kt, h, :], pT[:, (first[cc] + n) % 4, a, lo:CH],
                                        start=kt == 0, stop=kt == (cc + 1) * TC - 1, skip_group_check=True)
                    ins.then_inc(pv.sem, 1)

                def turn_maxima(it, cc):
                    pe.wait_ge(*nm_made.at(it, cc + 1))
                    for pr in range(2):
                        name = f"n{cc}_{pr}"
                        pe.wait_ge(*bk.free(name, it))
                        for j in range(TC):
                            ins = pe.transpose(g.bk(6)[:, j * P:(j + 1) * P], nm[:, j, 2 * pr:2 * pr + 2].rearrange("p h d -> p (h d)"), g.ident[:])
                        ins.then_inc(bk.fill(name), 1)
                    pe.wait_ge(*bk.read(f"n{cc}_1", it))

                def project(it, cc):
                    pe.wait_ge(*o_read.at(it, cc + 1))
                    pe.wait_ge(*bk.free(f"y{cc}", it))
                    for j in range(TC):
                        ins = pe.matmul(g.bk(6)[:, j * 68:(j + 1) * 68], oT[:, j * P:(j + 1) * P], wo[:], start=True, stop=True)
                    ins.then_inc(bk.fill(f"y{cc}"), 1)

                pe.wait_ge(*w_in.at(0, 48))
                with pe.Fori(0, B) as b, pe.Fori(0, G) as f:
                    it = b * G + f
                    pe.wait_ge(*copied.at(it, 2))
                    for kind, what in order:
                        if kind == "m":
                            max_piece(it, *what)
                        elif kind == "s":
                            score_piece(it, what[0], *ps2[what[0]][what[1]])
                        elif kind == "v":
                            value_piece(it, *what)
                        elif kind == "n":
                            turn_maxima(it, what)
                        else:
                            project(it, what)

            @block.scalar
            def _(act):
                with act.Fori(0, B) as b, act.Fori(0, G) as f:
                    it = b * G + f
                    act.wait_ge(*pv.at(it, 0))
                    act.activation(ks[:], kT_all[:, ds(it * 2, 2), :], ACT.Copy).then_inc(copied.sem, 1)
                    nd = 0
                    for cc in range(2):
                        for n, (kt, pr) in enumerate(ps2[cc]):
                            key = (cc, kt, pr)
                            lo = max(0, kt * P - cc * CH)
                            m = first[cc] + n
                            if kt >= cc * TC:
                                nd += 1
                                act.wait_ge(*masked.at(it, nd))
                            for a in range(2):
                                act.wait_ge(*bk.full(f"{key}{a}", it))
                            act.wait_ge(*pv.at(it, max(0, m - 3)))
                            for a in range(2):
                                act.activation(pT[:, m % 4, a, lo:CH], g.bk(sets[key] + a)[:, lo:CH], ACT.Exp, scale=HD ** -0.5)\
                                    .then_inc(bk.release(f"{key}{a}"), 1)
                        act.wait_ge(*pv.at(it, first[cc] + NP2[cc]))
                        if cc:
                            act.wait_ge(*bk.full("y0", it))
                        act.activation(oT[:], g.bk(7), ACT.Copy).then_inc(o_read.sem, 1)

            @block.vector
            def _(dve):
                dve.wait_ge(*w_in.at(0, 48))
                dve.wait_ge(*nm_zero.at(0, 2))
                with dve.Fori(0, B) as b, dve.Fori(0, G) as f:
                    it = b * G + f
                    link = Chain(dve, step, it)
                    dve.wait_ge(*pv.at(it, 0))
                    dve.tensor_scalar(qs[:], qT_all[:, ds(it * 2, 2), :], 1.0, None, ALU.mult)\
                        .then_inc(copied.sem, 1)
                    nd = 0

                    def two(base):
                        return g.ps[:, base:base + 2, :]

                    def maxima(ps):
                        for i, half, pr in ps:
                            key = ("m", i, half, pr)
                            wd = min(CH, (i + 1) * P - half * CH)
                            for a in range(2):
                                dve.wait_ge(*bk.full(f"{key}{a}", it))
                            if half == i // TC:
                                link(dve.tensor_tensor(two(sets[key])[:, :, wd - P:wd], two(sets[key])[:, :, wd - P:wd],
                                                       ngq[:].unsqueeze(1).broadcast_to([P, 2, P]), ALU.add))
                            for a in range(2):
                                dve.tensor_reduce(mx[:, i, half, 2 * pr + a:2 * pr + a + 1], g.bk(sets[key] + a)[:, 0:wd], AXX, ALU.max)\
                                    .then_inc(bk.release(f"{key}{a}"), 1)

                    def negate(cc):
                        last = {bk.bank[f"{('m',) + p}{a}"]: f"{('m',) + p}{a}" for p in ps1 if p[0] // TC == cc for a in range(2)}
                        for name in last.values():
                            dve.wait_ge(*bk.read(name, it))
                        if cc:
                            link(dve.tensor_tensor(m4[:], mx[:, TC:, 0, :], mx[:, TC:, 1, :], ALU.max))
                            src = m4[:]
                            dve.wait_ge(*bk.full("n0_1", it))
                        else:
                            src = mx[:, 0:TC, 0, :]
                        dve.tensor_scalar(nm[:, :, :, 3 * HD], src, -1.0, None, ALU.mult).then_inc(nm_made.sem, 1)

                    def queries(cc):
                        h = slice(cc * CH, (cc + 1) * CH)
                        for pr in range(2):
                            dve.wait_ge(*bk.full(f"n{cc}_{pr}", it))
                            dve.tensor_tensor(qs[:, pr, h], qs[:, pr, h].bitcast(F32), g.bk(6), ALU.add).then_inc(bk.release(f"n{cc}_{pr}"), 1)

                    def mask_diagonal(cc, ps):
                        for kt, pr in ps:
                            if kt >= cc * TC:
                                key = (cc, kt, pr)
                                lo = kt * P - cc * CH
                                for a in range(2):
                                    dve.wait_ge(*bk.full(f"{key}{a}", it))
                                v = two(sets[key])[:, :, lo:lo + P]
                                dve.tensor_tensor(v, v, ngk[:].unsqueeze(1).broadcast_to([P, 2, P]), ALU.add).then_inc(masked.sem, 1)

                    def rows_out(cc):
                        dve.wait_ge(*bk.full(f"y{cc}", it))
                        yv = g.bk(6)[:, 0:TC * 68].rearrange("p (t e) -> p t e", e=68)
                        link(dve.reciprocal(rec[:, cc], yv[:, :, 64:68]))
                        dve.wait_ge(*added.at(it, cc))
                        for j in range(TC):
                            ins = dve.tensor_tensor(y[:, j].rearrange("p (h d) -> p h d", d=HD),
                                                    yv[:, j, 0:64].rearrange("p (h d) -> p h d", d=HD),
                                                    rec[:, cc, j].unsqueeze(2).broadcast_to([P, G, HD]), ALU.mult)
                        ins.then_inc(bk.release(f"y{cc}"), 1)

                    maxima(mp[0])
                    negate(0)
                    maxima(mp[1][:EARLY])
                    queries(0)
                    mask_diagonal(0, ps2[0][:AHEAD])
                    for n in range(NP2[0]):
                        mask_diagonal(0, ps2[0][n + AHEAD:n + AHEAD + 1])
                        maxima(beside[n])
                    negate(1)
                    queries(1)
                    rows_out(0)
                    mask_diagonal(1, ps2[1])
                    rows_out(1)
                    link.close()
        bk.end(B * G)
        w_in.end()
        nm_zero.end()
        for ev in (copied, v_copied, step, nm_made, masked, pv, o_read, added):
            ev.end(B * G)



def program(nc, t, out):
    with ExitStack() as ctx:
        g = Kernel(nc, ctx)
        opening(g, t["x"])
        stage_l0_attn(g, t["a_rms"], t["a_split"], t["a_wk"], t["a_wugg"], t["a_wout"])
        stage_l0_xattn(g, t["ctx"], t["b_mrow"], t["b_mcol"], t["b_g1"], t["b_b1"], t["b_g2"], t["b_b2"],
                       t["b_wq"], t["b_wk"], t["b_wv"], t["b_wo"])
        stage_l0_ffn(g, t["c_w1"], t["c_s1"], t["c_w2"], t["c_s2"], t["c_h1"], t["c_hs1"], t["c_h2"], t["c_hs2"],
                     t["c_w3"], t["c_s3"])
        stage_l1_attn(g, t["d_wqkv"], t["d_wout"], t["d_alpha"], t["d_beta"], t["same_head"])
        stage_ctx_attn(g, "exp", t["ctxT"], t["e_w"], t["e_w"], t["e_w"], t["e_bc"], t["e_bc"], t["e_br"], t["e_wo"], t["e_bo"],
                       sgn=t["sgn"], sgn_row=t["sgn_row"])
        stage_l1_ffn(g, t["f_gamma"], t["f_beta"], t["f_rw"], t["f_w1"], t["f_w2"])
        stage_l2_attn(g, t["g_wq"], t["g_wk"], t["g_wv"], t["g_bq"], t["g_bk"], t["g_bv"], t["g_wo"], t["g_bo"],
                      t["g_gamma"], t["g_beta"], t["causal"], t["own"])
        stage_ctx_attn(g, "mask", t["ctxT"], t["h_wq"], t["h_wk"], t["h_wv"], t["zero_col"], t["zero_col"], t["zero_row"],
                       t["h_wo"], t["h_bo"], mask=t["h_mask"])
        stage_l2_ffn(g, t["i_w"], t["i_gu"], t["i_v"])
        stage_l3_attn(g, t["j_dq"], t["j_uq"], t["j_dkv"], t["j_ukv"], t["j_qr"], t["j_kr"], t["same_head"], t["j_nw"],
                      t["j_wo"], t["neg"])
        stage_ctx_attn(g, "plain", t["ctxT"], t["k_wq"], t["k_wk"], t["k_wv"], t["k_bq"], t["k_bk"], t["k_bv"], t["k_wo"], t["k_bo"])
        stage_l3_ffn(g, t["l_w"], out)



def as_cols(v):
    return v.reshape(-1, 128).T


def as_rows(v):
    return np.broadcast_to(v[None, :], (128, v.shape[0]))


def pad_heads(w, width=16, room=32):
    w = w.reshape(*w.shape[:-1], -1, width)
    padded = np.zeros((*w.shape[:-1], room), w.dtype)
    padded[..., :width] = w
    return padded.reshape(*w.shape[:-2], -1)


def blocked(w, heads=16):
    i, o = w.shape
    full = np.zeros((heads, i, heads, o), w.dtype)
    for h in range(heads):
        full[h, :, h, :] = w
    return full.reshape(heads * i, heads * o)


def quarters(w):
    return w.reshape(256, 4, 256).transpose(1, 0, 2)


def constants():
    k = np.arange(128)
    sign = np.where(np.arange(32) < 16, 1, -1).astype(np.float32)
    col = np.arange(272)
    return {
        "same_head": (k[:, None] // 16 == k[None, :] // 16).astype(np.float32),
        "sgn": np.tile(sign, 4)[:, None],
        "sgn_row": as_rows(np.tile(sign, 16)),
        "causal": (k[None, :] >= k[:, None]).astype(np.float32),
        "own": ((k[:, None] // 32 == (col % 68)[None] // 17) & (k[:, None] % 32 < 16)).astype(np.float32),
        "neg": np.stack([np.where(k[None] > k[:, None], -1e30, 0), np.where(k[:, None] > k[None], -1e30, 0)]).astype(np.float32),
        "zero_col": np.zeros((128, 4), np.float32),
        "zero_row": np.zeros((128, 512), np.float32),
    }


def layout(I):
    def rep(w, n=8):
        return np.tile(w, (1, n))

    wqkv, bqkv = I["L2_attn_Wqkv"], I["L2_attn_bqkv"]
    ukv = I["L3_attn_W_UKV"].T
    fm = I["L1_xattn_fm_w"].T
    wkv = I["L0_xattn_Wkv"]
    keep = I["mask_BxS2_bk0"].astype(np.int32)
    wo = np.zeros((4, 32, 68), np.float32)
    for h in range(4):
        wo[h, :16, h * 16:h * 16 + 16] = I["L3_attn_W_O"].T
        wo[h, 16, 64 + h] = 1
    t = {
        "x": I["x"], "ctx": I["ctx_1024"], "ctxT": I["ctx_1024"].reshape(-1, 256).T,
        "a_rms": as_cols(I["L0_attn_rms_scale"]), "a_split": as_cols(I["L0_attn_split_scale"]),
        "a_wk": I["L0_attn_W_K"], "a_wugg": I["L0_attn_W_ugg"], "a_wout": I["L0_attn_W_out"],
        "b_mrow": as_rows(keep.reshape(-1)), "b_mcol": keep.T,
        "b_g1": as_cols(I["L0_xattn_g1"]), "b_b1": as_cols(I["L0_xattn_b1"]),
        "b_g2": as_cols(I["L0_xattn_g2"]), "b_b2": as_cols(I["L0_xattn_b2"]),
        "b_wq": quarters(I["L0_xattn_Wq"]), "b_wk": quarters(wkv[:, :1024]), "b_wv": quarters(wkv[:, 1024:]),
        "b_wo": I["L0_xattn_Wout"].reshape(4, 256, 256),
        "d_wqkv": I["L1_attn_w_qkv"], "d_wout": I["L1_attn_w_out"],
        "d_alpha": as_cols(np.repeat(I["L1_attn_alpha"], 16)), "d_beta": as_cols(np.repeat(I["L1_attn_beta"], 16)),
        "e_w": blocked(np.concatenate([fm, fm], 1)), "e_bc": as_cols(np.tile(I["L1_xattn_fm_b"], 32)),
        "e_br": as_rows(np.tile(I["L1_xattn_fm_b"], 32)), "e_wo": I["L1_xattn_fc_w"].T, "e_bo": as_rows(I["L1_xattn_fc_b"]),
        "f_gamma": as_cols(I["L1_ffn_gamma"]), "f_beta": as_cols(I["L1_ffn_beta"]), "f_rw": I["L1_ffn_router_w"].T,
        "f_w1": I["L1_ffn_W1"], "f_w2": I["L1_ffn_W2"],
        "g_wq": pad_heads(wqkv[:256].T), "g_wk": pad_heads(wqkv[256:512].T), "g_wv": wqkv[512:].T,
        "g_bq": as_cols(pad_heads(bqkv[:256])), "g_bk": as_cols(pad_heads(bqkv[256:512])), "g_bv": as_rows(bqkv[512:]),
        "g_wo": I["L2_attn_Wout"].T, "g_bo": as_rows(I["L2_attn_bout"]),
        "g_gamma": as_rows(I["L2_attn_gamma"]), "g_beta": as_rows(I["L2_attn_beta"]),
        "h_wo": pad_heads(I["L2_xattn_Wo"]).T, "h_bo": as_rows(I["L2_xattn_bo"]), "h_mask": I["mask_Bx1xSxS2_if1"],
        "i_w": I["L2_ffn_weight"].T,
        "i_gu": np.concatenate([I["L2_ffn_gate_w"], I["L2_ffn_lora_U"].reshape(128, 256)], 0).T,
        "i_v": I["L2_ffn_lora_V"].transpose(0, 2, 1).reshape(128, 256),
        "j_dq": rep(I["L3_attn_W_DQ"]), "j_uq": rep(I["L3_attn_W_UQ"].T), "j_dkv": rep(I["L3_attn_W_DKV"]),
        "j_ukv": np.concatenate([rep(ukv[:, :16]), rep(ukv[:, 16:])], 1),
        "j_qr": rep(I["L3_attn_W_QR"]), "j_kr": rep(I["L3_attn_W_KR"]),
        "j_nw": as_rows(np.concatenate([np.tile(I["L3_attn_q_norm_w"], 8), np.tile(I["L3_attn_k_norm_w"], 8)])),
        "j_wo": wo.reshape(128, 68),
        "k_bv": as_rows(pad_heads(I["L3_xattn_bv"])),
        "k_wo": pad_heads(I["L3_xattn_Wo"].T).T, "k_bo": as_rows(I["L3_xattn_bo"]),
        "l_w": I["L3_ffn_weight"].T,
    }
    for n in ("w1", "w2", "h1", "h2", "w3"):
        t[f"c_{n}"] = I[f"L0_ffn_{n}_w"].T
    for n, s in (("w1", "s1"), ("w2", "s2"), ("h1", "hs1"), ("h2", "hs2")):
        t[f"c_{s}"] = as_cols(I[f"L0_ffn_{n}_s"])
    t["c_s3"] = as_rows(I["L0_ffn_w3_s"])
    for n in "qkv":
        t[f"h_w{n}"] = pad_heads(blocked(I[f"L2_xattn_W{n}"].T))
        t[f"k_w{n}"] = pad_heads(I[f"L3_xattn_W{n}"])
    for n in "qk":
        t[f"k_b{n}"] = as_cols(pad_heads(I[f"L3_xattn_b{n}"]))
    t.update(constants())
    return t


def kernel(**inputs):
    import concourse.bacc as _bacc
    from concourse.bass_utils import run_bass_kernel_spmd as _run

    nc = _bacc.Bacc("TRN2", target_bir_lowering=False, num_devices=1)
    arrays, tensors = {}, {}
    for name, a in layout({k: np.asarray(v) for k, v in inputs.items()}).items():
        a = np.ascontiguousarray(a)
        arrays[f"in_{name}"] = a
        tensors[name] = nc.dram_tensor(f"in_{name}", a.shape, mybir.dt.from_np(a.dtype), kind="ExternalInput").ap()
    out = nc.dram_tensor("out", (B, S, D), F32, kind="ExternalOutput").ap()
    program(nc, tensors, out)
    r = _run(nc, [arrays], core_ids=[0])
    return r.results[0]["out"]
```
